# Optimizing a Trainium2 kernel written in Bass

```python
import numpy as np
import jax
import jax.numpy as jnp

def _softmax(x, axis=-1):
    return jax.nn.softmax(x, axis=axis)

def _gelu(x):
    return jax.nn.gelu(x, approximate=True)

def _silu(x):
    return jax.nn.silu(x)

def _sigmoid(x):
    return jax.nn.sigmoid(x)

def _layernorm(x, axis=-1, eps=1e-05):
    m = jnp.mean(x, axis=axis, keepdims=True)
    v = jnp.var(x, axis=axis, keepdims=True)
    return (x - m) / jnp.sqrt(v + eps)

def _scatter_add(tgt, idx, src, axis=0):
    return tgt.at[idx].add(src)

def _segment_sum(src, seg, n):
    return jax.ops.segment_sum(src, seg, n)
kernel_name = 'mk_decoder_postln_d2_seqx_r8_2e1848'

def setup_inputs(seed: int=0):
    np.random.seed(seed)
    _w = jnp.asarray

    def _rec_inputs():
        import jax
        import jax.numpy as jnp
        _rk = jax.random.key(seed)
        x = -0.0001033 + 0.9999 * jax.random.normal(jax.random.fold_in(_rk, 1), (4, 512, 128), jnp.float32)
        _lenS = 512 - jax.random.randint(jax.random.fold_in(_rk, 7), (4,), 0, max(1, 512 // 4) + 1, jnp.int32)
        _lenS2 = 32 - jax.random.randint(jax.random.fold_in(_rk, 8), (4,), 0, max(1, 32 // 4) + 1, jnp.int32)
        _ctx_1024P = jax.random.normal(jax.random.fold_in(_rk, 11), (4, 16, 128), jnp.float32)
        _ctx_1024c = jax.random.dirichlet(jax.random.fold_in(_rk, 511), 0.3 * jnp.ones((16,), jnp.float32), (4, 32))
        _ctx_1024t = jnp.einsum('bsk,bkd->bsd', _ctx_1024c, _ctx_1024P)
        _ctx_1024t = _ctx_1024t * jax.lax.rsqrt(jnp.mean(jnp.square(_ctx_1024t)) + 1e-12) * 0.953939
        ctx_1024 = -0.000292821 + 1.00034 * (_ctx_1024t + 0.3 * jax.random.normal(jax.random.fold_in(_rk, 611), (4, 32, 128), jnp.float32))
        _validS = jnp.arange(512)[None, :] < _lenS[:, None]
        _validS2 = jnp.arange(32)[None, :] < _lenS2[:, None]
        _causal = jnp.tril(jnp.ones((512, 512), dtype=bool))
        mask_1x1xSxS2_if1 = jnp.where(jnp.ones((1, 1, 512, 32), dtype=bool), 1, 0).astype(jnp.int32)
        return (x, ctx_1024, mask_1x1xSxS2_if1)
    x, ctx_1024, mask_1x1xSxS2_if1 = _rec_inputs()

    def _L0_attn_setup():
        import jax, jax.numpy as jnp
        import numpy as np
        B_, L, DM = (2, 256, 128)
        DS = 64
        EXP = 2
        DC = 4
        DI = DM * EXP

        def _forward(x, W_in, conv_w, conv_b, W_x, A_log, D, W_out):
            xz = jnp.einsum('bld,ed->ble', x, W_in)
            x_in, z = jnp.split(xz, 2, axis=-1)
            xc = jnp.transpose(x_in, (0, 2, 1))
            xc = jax.lax.conv_general_dilated(xc, conv_w, window_strides=(1,), padding=[(DC - 1, 0)], dimension_numbers=('NCH', 'OIH', 'NCH'), feature_group_count=DI)
            xc = xc + conv_b[None, :, None]
            xc = jax.nn.silu(jnp.transpose(xc, (0, 2, 1)))
            ssm = jnp.einsum('bld,ed->ble', xc, W_x)
            Bm = ssm[..., :DS]
            Cm = ssm[..., DS:2 * DS]
            dt = jax.nn.softplus(ssm[..., -1])
            A = -jnp.exp(A_log)

            def step(h, inp):
                x_t, B_t, C_t, dt_t = inp
                dtb = dt_t[:, None, None]
                A_bar = jnp.exp(A[None, None, :] * dtb)
                h = A_bar * h + x_t[:, :, None] * (B_t[:, None, :] * dtb)
                y_t = jnp.einsum('bds,bs->bd', h, C_t)
                return (h, y_t)
            h0 = jnp.zeros((x.shape[0], DI, DS), xc.dtype)
            xs = (jnp.swapaxes(xc, 0, 1), jnp.swapaxes(Bm, 0, 1), jnp.swapaxes(Cm, 0, 1), jnp.swapaxes(dt, 0, 1))
            _, ys = jax.lax.scan(step, h0, xs)
            y = jnp.swapaxes(ys, 0, 1)
            y = y + xc * D
            y = y * jax.nn.silu(z)
            return jnp.einsum('bld,od->blo', y, W_out)
        key = jax.random.key(seed)
        ks = jax.random.split(key, 6)
        sc = lambda k, shape, fan: jax.random.normal(k, shape, jnp.float32) * fan ** (-0.5)
        x = jax.random.normal(ks[0], (B_, L, DM), jnp.float32)
        W_in = sc(ks[1], (2 * DI, DM), DM)
        conv_w = sc(ks[2], (DI, 1, DC), DC)
        conv_b = sc(ks[3], (DI,), DC)
        W_x = sc(ks[4], (2 * DS + 1, DI), DI)
        A_log = jnp.log(jnp.arange(1, DS + 1, dtype=jnp.float32))
        D = jnp.ones((DI,), jnp.float32)
        W_out = sc(ks[5], (DM, DI), DI)
        return {'x': x, 'W_in': W_in, 'conv_w': conv_w, 'conv_b': conv_b, 'W_x': W_x, 'A_log': A_log, 'D': D, 'W_out': W_out}
    _L0_attn_all = _L0_attn_setup()
    _L0_attn_in = {k: v for k, v in _L0_attn_all.items() if k in ('W_in', 'conv_w', 'conv_b', 'W_x', 'A_log', 'D', 'W_out')}
    del _L0_attn_all

    def _L0_xattn_setup():
        import jax, jax.numpy as jnp
        import numpy as np
        from jax import lax
        B, T, F = (32, 128, 128)
        CONV_UNITS = 256
        SHORT_UNITS = 256
        RATE = 4
        key = jax.random.key(seed)
        k1, k2, k3 = jax.random.split(key, 3)
        inputs = jax.random.normal(k1, (B, T, F), dtype=jnp.float32)
        memory = jax.random.normal(k2, (B, CONV_UNITS + SHORT_UNITS, F), dtype=jnp.float32)
        conv_w = jax.random.normal(k3, (RATE, F, F), dtype=jnp.float32) * 0.02
        conv_b = jnp.zeros((F,), dtype=jnp.float32)
        return {'inputs': inputs, 'memory': memory, 'conv_w': conv_w, 'conv_b': conv_b, 'conv_units': CONV_UNITS, 'short_units': SHORT_UNITS, 'rate': RATE}
    _L0_xattn_all = _L0_xattn_setup()
    _L0_xattn_in = {k: v for k, v in _L0_xattn_all.items() if k in ('conv_w', 'conv_b')}
    del _L0_xattn_all

    def _L0_ffn_setup():
        import jax, jax.numpy as jnp
        import numpy as np
        HIDDEN = 128
        INNER = 512

        def _weight_quant(w):
            scale = 1.0 / jnp.clip(jnp.mean(jnp.abs(w)), 1e-05)
            wq = jnp.clip(jnp.round(w * scale), -1.0, 1.0) / scale
            return w + jax.lax.stop_gradient(wq - w)

        def _act_quant(x):
            scale = 127.0 / jnp.clip(jnp.max(jnp.abs(x), axis=-1, keepdims=True), 1e-05)
            xq = jnp.clip(jnp.round(x * scale), -128.0, 127.0) / scale
            return x + jax.lax.stop_gradient(xq - x)

        def _bitlinear(x, w):
            return jnp.einsum('bsi,oi->bso', _act_quant(x), _weight_quant(w))
        key = jax.random.key(seed)
        k0, k1, k2, k3 = jax.random.split(key, 4)
        x = jax.random.normal(k0, (4, 256, HIDDEN), dtype=jnp.float32)
        w_gate = jax.random.normal(k1, (INNER, HIDDEN), dtype=jnp.float32) / np.sqrt(HIDDEN)
        w_up = jax.random.normal(k2, (INNER, HIDDEN), dtype=jnp.float32) / np.sqrt(HIDDEN)
        w_down = jax.random.normal(k3, (HIDDEN, INNER), dtype=jnp.float32) / np.sqrt(INNER)
        return {'x': x, 'w_gate': w_gate, 'w_up': w_up, 'w_down': w_down}
    _L0_ffn_all = _L0_ffn_setup()
    _L0_ffn_in = {k: v for k, v in _L0_ffn_all.items() if k in ('w_gate', 'w_up', 'w_down')}
    del _L0_ffn_all

    def _L1_attn_setup():
        import jax, jax.numpy as jnp
        import numpy as np
        B, T, C = (4, 256, 128)
        NUM_HEADS = 16
        OUT_DIM = 128
        HEAD_DIM = OUT_DIM // NUM_HEADS
        key = jax.random.key(seed)
        kx, kk, kq, kv, kp = jax.random.split(key, 5)
        return {'x': jax.random.normal(kx, (B, T, C), dtype=jnp.float32), 'W_key': jax.random.normal(kk, (OUT_DIM, C), dtype=jnp.float32), 'W_query': jax.random.normal(kq, (OUT_DIM, C), dtype=jnp.float32), 'W_value': jax.random.normal(kv, (OUT_DIM, C), dtype=jnp.float32), 'W_proj': jax.random.normal(kp, (OUT_DIM, OUT_DIM), dtype=jnp.float32)}
    _L1_attn_all = _L1_attn_setup()
    _L1_attn_in = {k: v for k, v in _L1_attn_all.items() if k in ('W_key', 'W_query', 'W_value', 'W_proj')}
    del _L1_attn_all

    def _L1_xattn_setup():
        import jax, jax.numpy as jnp
        import numpy as np
        B, S, D, H = (2, 256, 128, 16)
        DK = D // H
        key = jax.random.key(seed)
        ks = jax.random.split(key, 8)

        def lin(k):
            kw, kb = jax.random.split(k)
            w = jax.random.normal(kw, (D, D), dtype=jnp.float32) / np.sqrt(D)
            b = jax.random.normal(kb, (D,), dtype=jnp.float32) * 0.01
            return (w, b)
        wq, bq = lin(ks[0])
        wk, bk = lin(ks[1])
        wv, bv = lin(ks[2])
        wo, bo = lin(ks[3])
        return {'q': jax.random.normal(ks[4], (B, S, D), dtype=jnp.float32), 'k': jax.random.normal(ks[5], (B, S, D), dtype=jnp.float32), 'v': jax.random.normal(ks[6], (B, S, D), dtype=jnp.float32), 'mask': jnp.ones((1, 1, S, S), dtype=jnp.int32), 'wq': wq, 'bq': bq, 'wk': wk, 'bk': bk, 'wv': wv, 'bv': bv, 'wo': wo, 'bo': bo}
    _L1_xattn_all = _L1_xattn_setup()
    _L1_xattn_in = {k: v for k, v in _L1_xattn_all.items() if k in ('wq', 'bq', 'wk', 'bk', 'wv', 'bv', 'wo', 'bo')}
    del _L1_xattn_all

    def _L1_ffn_setup():
        import jax, jax.numpy as jnp
        import numpy as np
        D_MODEL = 128
        N_EXPERTS = 8
        TOP_K = 2
        HIDDEN = 4 * D_MODEL
        key = jax.random.key(seed)
        ks = jax.random.split(key, 6)
        B, S = (2, 256)
        x = jax.random.normal(ks[0], (B, S, D_MODEL), dtype=jnp.float32)
        shared_w1 = jax.random.normal(ks[1], (HIDDEN, D_MODEL), dtype=jnp.float32) * 0.02
        shared_w2 = jax.random.normal(ks[2], (D_MODEL, HIDDEN), dtype=jnp.float32) * 0.02
        experts_w1 = jax.random.normal(ks[3], (N_EXPERTS, HIDDEN, D_MODEL), dtype=jnp.float32) * 0.02
        experts_w2 = jax.random.normal(ks[4], (N_EXPERTS, D_MODEL, HIDDEN), dtype=jnp.float32) * 0.02
        gate_w = jax.random.normal(ks[5], (N_EXPERTS, D_MODEL), dtype=jnp.float32) * 0.02
        return {'x': x, 'shared_w1': shared_w1, 'shared_w2': shared_w2, 'experts_w1': experts_w1, 'experts_w2': experts_w2, 'gate_w': gate_w}
    _L1_ffn_all = _L1_ffn_setup()
    _L1_ffn_in = {k: v for k, v in _L1_ffn_all.items() if k in ('shared_w1', 'shared_w2', 'experts_w1', 'experts_w2', 'gate_w')}
    del _L1_ffn_all
    return {'x': x, 'ctx_1024': ctx_1024, 'mask_1x1xSxS2_if1': mask_1x1xSxS2_if1, 'L0_attn_W_in': _L0_attn_in['W_in'], 'L0_attn_conv_w': _L0_attn_in['conv_w'], 'L0_attn_conv_b': _L0_attn_in['conv_b'], 'L0_attn_W_x': _L0_attn_in['W_x'], 'L0_attn_A_log': _L0_attn_in['A_log'], 'L0_attn_D': _L0_attn_in['D'], 'L0_attn_W_out': _L0_attn_in['W_out'], 'L0_xattn_conv_w': _L0_xattn_in['conv_w'], 'L0_xattn_conv_b': _L0_xattn_in['conv_b'], 'L0_ffn_w_gate': _L0_ffn_in['w_gate'], 'L0_ffn_w_up': _L0_ffn_in['w_up'], 'L0_ffn_w_down': _L0_ffn_in['w_down'], 'L1_attn_W_key': _L1_attn_in['W_key'], 'L1_attn_W_query': _L1_attn_in['W_query'], 'L1_attn_W_value': _L1_attn_in['W_value'], 'L1_attn_W_proj': _L1_attn_in['W_proj'], 'L1_xattn_wq': _L1_xattn_in['wq'], 'L1_xattn_bq': _L1_xattn_in['bq'], 'L1_xattn_wk': _L1_xattn_in['wk'], 'L1_xattn_bk': _L1_xattn_in['bk'], 'L1_xattn_wv': _L1_xattn_in['wv'], 'L1_xattn_bv': _L1_xattn_in['bv'], 'L1_xattn_wo': _L1_xattn_in['wo'], 'L1_xattn_bo': _L1_xattn_in['bo'], 'L1_ffn_shared_w1': _L1_ffn_in['shared_w1'], 'L1_ffn_shared_w2': _L1_ffn_in['shared_w2'], 'L1_ffn_experts_w1': _L1_ffn_in['experts_w1'], 'L1_ffn_experts_w2': _L1_ffn_in['experts_w2'], 'L1_ffn_gate_w': _L1_ffn_in['gate_w']}

def reference(x, ctx_1024, mask_1x1xSxS2_if1, L0_attn_W_in, L0_attn_conv_w, L0_attn_conv_b, L0_attn_W_x, L0_attn_A_log, L0_attn_D, L0_attn_W_out, L0_xattn_conv_w, L0_xattn_conv_b, L0_ffn_w_gate, L0_ffn_w_up, L0_ffn_w_down, L1_attn_W_key, L1_attn_W_query, L1_attn_W_value, L1_attn_W_proj, L1_xattn_wq, L1_xattn_bq, L1_xattn_wk, L1_xattn_bk, L1_xattn_wv, L1_xattn_bv, L1_xattn_wo, L1_xattn_bo, L1_ffn_shared_w1, L1_ffn_shared_w2, L1_ffn_experts_w1, L1_ffn_experts_w2, L1_ffn_gate_w):
    import jax
    import jax.numpy as jnp

    def _L0_attn_ref(x, W_in, conv_w, conv_b, W_x, A_log, D, W_out):
        import jax, jax.numpy as jnp
        import numpy as np
        B_, L, DM = (2, 256, 128)
        DS = 64
        EXP = 2
        DC = 4
        DI = DM * EXP

        def _forward(x, W_in, conv_w, conv_b, W_x, A_log, D, W_out):
            xz = jnp.einsum('bld,ed->ble', x, W_in)
            x_in, z = jnp.split(xz, 2, axis=-1)
            xc = jnp.transpose(x_in, (0, 2, 1))
            xc = jax.lax.conv_general_dilated(xc, conv_w, window_strides=(1,), padding=[(DC - 1, 0)], dimension_numbers=('NCH', 'OIH', 'NCH'), feature_group_count=DI)
            xc = xc + conv_b[None, :, None]
            xc = jax.nn.silu(jnp.transpose(xc, (0, 2, 1)))
            ssm = jnp.einsum('bld,ed->ble', xc, W_x)
            Bm = ssm[..., :DS]
            Cm = ssm[..., DS:2 * DS]
            dt = jax.nn.softplus(ssm[..., -1])
            A = -jnp.exp(A_log)

            def step(h, inp):
                x_t, B_t, C_t, dt_t = inp
                dtb = dt_t[:, None, None]
                A_bar = jnp.exp(A[None, None, :] * dtb)
                h = A_bar * h + x_t[:, :, None] * (B_t[:, None, :] * dtb)
                y_t = jnp.einsum('bds,bs->bd', h, C_t)
                return (h, y_t)
            h0 = jnp.zeros((x.shape[0], DI, DS), xc.dtype)
            xs = (jnp.swapaxes(xc, 0, 1), jnp.swapaxes(Bm, 0, 1), jnp.swapaxes(Cm, 0, 1), jnp.swapaxes(dt, 0, 1))
            _, ys = jax.lax.scan(step, h0, xs)
            y = jnp.swapaxes(ys, 0, 1)
            y = y + xc * D
            y = y * jax.nn.silu(z)
            return jnp.einsum('bld,od->blo', y, W_out)
        return _forward(x, W_in, conv_w, conv_b, W_x, A_log, D, W_out)

    def _L0_xattn_ref(inputs, memory, conv_w, conv_b, conv_units, short_units, rate):
        import jax, jax.numpy as jnp
        import numpy as np
        from jax import lax
        B, T, F = (32, 128, 128)
        CONV_UNITS = 256
        SHORT_UNITS = 256
        RATE = 4
        b, t, f = inputs.shape
        conv_mem = memory[:, :conv_units]
        short_mem = memory[:, -short_units:]
        old_memory = short_mem[:, :t]
        compression = lax.conv_general_dilated(old_memory, conv_w, window_strides=(rate,), padding='VALID', dimension_numbers=('NWC', 'WIO', 'NWC')) + conv_b
        tc = compression.shape[1]
        new_short = jnp.concatenate([short_mem[:, t:], inputs], axis=1)
        new_conv = jnp.concatenate([conv_mem[:, tc:], compression], axis=1)
        return jnp.concatenate([new_conv, new_short], axis=1)

    def _L0_ffn_ref(x, w_gate, w_up, w_down):
        import jax, jax.numpy as jnp
        import numpy as np
        HIDDEN = 128
        INNER = 512

        def _weight_quant(w):
            scale = 1.0 / jnp.clip(jnp.mean(jnp.abs(w)), 1e-05)
            wq = jnp.clip(jnp.round(w * scale), -1.0, 1.0) / scale
            return w + jax.lax.stop_gradient(wq - w)

        def _act_quant(x):
            scale = 127.0 / jnp.clip(jnp.max(jnp.abs(x), axis=-1, keepdims=True), 1e-05)
            xq = jnp.clip(jnp.round(x * scale), -128.0, 127.0) / scale
            return x + jax.lax.stop_gradient(xq - x)

        def _bitlinear(x, w):
            return jnp.einsum('bsi,oi->bso', _act_quant(x), _weight_quant(w))
        gate = jax.nn.silu(_bitlinear(x, w_gate))
        up = _bitlinear(x, w_up)
        return _bitlinear(gate * up, w_down)

    def _L1_attn_ref(x, W_key, W_query, W_value, W_proj):
        import jax, jax.numpy as jnp
        import numpy as np
        B, T, C = (4, 256, 128)
        NUM_HEADS = 16
        OUT_DIM = 128
        HEAD_DIM = OUT_DIM // NUM_HEADS
        b, t, c = x.shape
        h, hd = (NUM_HEADS, HEAD_DIM)
        inv_sqrt_c = c ** (-0.5)

        def proj(W):
            return jnp.einsum('btc,oc->bto', x, W).reshape(b, t, h, hd).transpose(0, 2, 1, 3) * inv_sqrt_c
        k = proj(W_key)
        q = proj(W_query)
        v = proj(W_value)
        scores = jnp.einsum('bhqd,bhkd->bhqk', q, k) * hd ** (-0.5)
        causal = jnp.tril(jnp.ones((t, t), dtype=bool))
        scores = jnp.where(causal, scores, -jnp.inf)
        weight = jax.nn.softmax(scores, axis=-1)
        out = jnp.einsum('bhqk,bhkd->bhqd', weight, v)
        out = out.transpose(0, 2, 1, 3).reshape(b, t, h * hd)
        out = jnp.einsum('bto,po->btp', out, W_proj) * W_proj.shape[-1] ** (-0.5)
        return out

    def _L1_xattn_ref(q, k, v, mask, wq, bq, wk, bk, wv, bv, wo, bo):
        import jax, jax.numpy as jnp
        import numpy as np
        B, S, D, H = (2, 256, 128, 16)
        DK = D // H
        b, s, _ = q.shape
        Q = (q @ wq.T + bq).reshape(b, s, H, DK).transpose(0, 2, 1, 3)
        K = (k @ wk.T + bk).reshape(b, -1, H, DK).transpose(0, 2, 1, 3)
        V = (v @ wv.T + bv).reshape(b, -1, H, DK).transpose(0, 2, 1, 3)
        scores = jnp.einsum('bhqd,bhkd->bhqk', Q, K) / np.sqrt(DK)
        scores = jnp.where(mask == 0, jnp.float32(-1e-09), scores)
        att = jax.nn.softmax(scores, axis=-1)
        x = jnp.einsum('bhqk,bhkd->bhqd', att, V)
        x = x.transpose(0, 2, 1, 3).reshape(b, s, H * DK)
        return x @ wo.T + bo

    def _L1_ffn_ref(x, shared_w1, shared_w2, experts_w1, experts_w2, gate_w):
        import jax, jax.numpy as jnp
        import numpy as np
        D_MODEL = 128
        N_EXPERTS = 8
        TOP_K = 2
        HIDDEN = 4 * D_MODEL
        B, S, D = x.shape
        T = B * S
        x_flat = x.reshape(T, D)
        shared = jnp.einsum('td,dh->th', x_flat, shared_w1.T)
        shared = jnp.einsum('th,hd->td', jax.nn.silu(shared), shared_w2.T)
        gate_logits = x_flat @ gate_w.T
        top_k_gates, top_k_idx = jax.lax.top_k(gate_logits, TOP_K)
        top_k_gates = jax.nn.softmax(top_k_gates, axis=1)
        gates = jnp.zeros((T, N_EXPERTS), dtype=x.dtype)
        gates = gates.at[jnp.arange(T)[:, None], top_k_idx].set(top_k_gates)
        h = jnp.einsum('td,ehd->teh', x_flat, experts_w1)
        expert_out = jnp.einsum('teh,edh->ted', jax.nn.silu(h), experts_w2)
        selected = jnp.einsum('ted,te->td', expert_out, gates)
        return (shared + selected).reshape(B, S, D)
    x = _layernorm(x + _L0_attn_ref(x, L0_attn_W_in, L0_attn_conv_w, L0_attn_conv_b, L0_attn_W_x, L0_attn_A_log, L0_attn_D, L0_attn_W_out), axis=-1)
    x = _layernorm(x + _L0_xattn_ref(ctx_1024, x, L0_xattn_conv_w, L0_xattn_conv_b, 256, 256, 4), axis=-1)
    x = _layernorm(x + _L0_ffn_ref(x, L0_ffn_w_gate, L0_ffn_w_up, L0_ffn_w_down), axis=-1)
    x = _layernorm(x + _L1_attn_ref(x, L1_attn_W_key, L1_attn_W_query, L1_attn_W_value, L1_attn_W_proj), axis=-1)
    x = _layernorm(x + _L1_xattn_ref(x, ctx_1024, ctx_1024, mask_1x1xSxS2_if1, L1_xattn_wq, L1_xattn_bq, L1_xattn_wk, L1_xattn_bk, L1_xattn_wv, L1_xattn_bv, L1_xattn_wo, L1_xattn_bo), axis=-1)
    x = _layernorm(x + _L1_ffn_ref(x, L1_ffn_shared_w1, L1_ffn_shared_w2, L1_ffn_experts_w1, L1_ffn_experts_w2, L1_ffn_gate_w), axis=-1)
    return x

_drawn_inputs = setup_inputs


def setup_inputs(seed=0):
    import zlib

    import numpy as np

    out = dict(_drawn_inputs(seed))
    spreads = {'L0_attn_D': (1.0, 0.2), 'L0_xattn_conv_b': (0.0, 0.732)}
    factors = {'L1_xattn_bq': 23.416, 'L1_xattn_bk': 64.0, 'L1_xattn_bv': 6.694, 'L1_xattn_bo': 5.973}
    for name, (base, spread) in spreads.items():
        noise = np.random.default_rng([zlib.crc32(name.encode()), seed]).standard_normal(out[name].shape)
        drawn = base * np.exp(spread * noise) if base else spread * noise
        out[name] = jnp.asarray(drawn.astype(out[name].dtype))
    for name, factor in factors.items():
        out[name] = (out[name] * factor).astype(out[name].dtype)
    return out
```

```python
from contextlib import ExitStack

import numpy as np
import concourse.bass as bass
from concourse import mybir

ALU = mybir.AluOpType
ACT = mybir.ActivationFunctionType
AX = mybir.AxisListType
F32 = mybir.dt.float32
BF16 = mybir.dt.bfloat16
I32 = mybir.dt.int32

B, T, D = 4, 512, 128
P = 128
NT = T // P
DI = 2 * D
NC = DI // P
DS = 64
TAPS = 4
NLEV = 8
CTX = 32
COMP = 8
KEEP = 256
FF = 512
FC = FF // P
H, HD = 16, 8
NPAIR = H // 2
HG = 8
PARTS = 6
NE = 8
SLICES = NE + 1
EPS = 1e-5
MAGIC = 1.5 * 2.0 ** 23
NEG = -1e30
PRODUCTS = [(0, 0), (0, 1), (1, 0), (0, 2), (2, 0), (1, 1)]
LEVELS_A = [64, 16, 4]
LEVELS_B = [32, 8, 2, 1]
SCORE_SCALE = (1.0 / D) * HD ** -0.5
CROSS_SCALE = HD ** -0.5
PROJ_SCALE = 1.0 / D


def decoder(nc, a, out):
    with ExitStack() as ctx:
        def sb(name, shape, dt=F32):
            return ctx.enter_context(nc.sbuf_tensor(name, shape, dt))

        def sem(name):
            return ctx.enter_context(nc.semaphore(name))

        names = {}

        def resident(name, dt=F32):
            names[name] = sb("s_" + name, list(a[name].shape), dt)
            return names[name]

        def share(name, size):
            region = sb(name, [P, size])

            def view(at, shape, dt=F32):
                n = int(np.prod(shape)) // (1 if dt == F32 else 2)
                flat = region[:, at:at + n]
                if dt != F32:
                    flat = flat.bitcast(dt)
                dims = [f"d{i}" for i in range(len(shape))]
                if len(shape) == 1:
                    return flat
                return flat.rearrange(f"p ({' '.join(dims)}) -> p {' '.join(dims)}",
                                      **{d: v for d, v in zip(dims[1:], shape[1:])})

            return view

        one = share("region1", 8192)
        two = share("region2", 4096)

        xT = resident("xT")
        xtok = sb("xtok", [P, NT, D])
        ctxT = resident("ctxT")
        w_in = resident("w_in")
        conv_w = resident("conv_w")
        chan = resident("chan")
        w_bb = resident("w_bb")
        w_cc = resident("w_cc")
        w_bdt = resident("w_bdt")
        alog = resident("alog")
        w_out = resident("w_out")
        lev_a = resident("lev_a")
        lev_b = resident("lev_b")
        suf = resident("suf")
        lmask = resident("lmask", BF16)
        ident = resident("ident")
        identb = resident("identb", BF16)
        ones = resident("ones")
        cconv = resident("cconv")
        cols = resident("cols")
        wg = names["wg"] = one(0, [FF])
        wu = names["wu"] = one(512, [FF])
        wd = names["wd"] = one(1024, [FC, D])
        w_q = resident("w_q")
        w_k = resident("w_k")
        w_v = resident("w_v")
        w_p = resident("w_p")
        tri_q = resident("tri_q", BF16)
        tri_k = resident("tri_k", BF16)
        pick = resident("pick", BF16)
        c_q = resident("c_q")
        c_k = resident("c_k")
        c_v = resident("c_v")
        c_o = resident("c_o")
        rows = resident("rows")
        hmask = resident("hmask")
        vmask = resident("vmask")
        mask = resident("mask", I32)
        w1 = resident("w1")
        w2 = resident("w2")
        wgate = resident("wgate")
        before = resident("before")

        neg_a = sb("neg_a", [P, 2 * DS])
        minus_half = sb("minus_half", [P, NT])
        wgq, wuq = sb("wgq", [P, FF], BF16), sb("wuq", [P, FF], BF16)
        wdq = sb("wdq", [P, FC, D], BF16)
        wabs = sb("wabs", [P, 3])
        wscale = sb("wscale", [P, 3])
        winv = sb("winv", [P, 3])
        wtmp = one(1536, [FF])
        mkeep = sb("mkeep", [P, NT, CTX])
        mfill = sb("mfill", [P, NT, CTX])
        vpad = sb("vpad", [P, NT, H, P])

        xin = sb("xin", [P, NC, TAPS - 1 + T])
        cacc = two(0, [NC, T])
        xc = sb("xc", [P, NC, T])
        zs = sb("zs", [P, NC, T])
        bs = sb("bs", [P, T])
        cs = sb("cs", [P, T])
        dts = sb("dts", [P, 4, NT])
        dta = sb("dta", [P, NT, P])
        xdt = two(0, [NT, DI])
        esuf = sb("esuf", [P, NT, DS])
        bsuf = sb("bsuf", [P, NT, DS])
        dec = one(0, [NT, 4, P])
        ct = one(2048, [NT, 4, P])
        bt = one(4096, [NT, 4, P])
        mm = one(6144, [2, NLEV, P])
        mix = two(1024, [NT, P])
        hst = sb("hst", [DS, NT - 1, DI])
        ya = two(1536, [NC, T])
        yg = two(2560, [NC, T])

        res = sb("res", [P, NT, D])
        rows_even, rows_odd = sb("rows_even", [P, NT, D]), sb("rows_odd", [P, NT, D])
        xs = [rows_odd, rows_even, rows_odd, rows_even, rows_odd, sb("result", [P, NT, D])]
        stats = sb("stats", [P, NT, 6])
        mv = sb("mv", [P, NT, 2])
        var = sb("var", [P, NT])
        rstd = sb("rstd", [P, NT])
        turned = sb("turned", [P, T + CTX])

        amax = sb("amax", [P, NT])
        ainv = sb("ainv", [P, NT])
        xqf = two(0, [NT, D])
        xq = sb("xq", [P, NT, D], BF16)
        xqT = sb("xqT", [P, T], BF16)
        gsc = sb("gsc", [P, NT, 2])
        gact = one(6144, [2, FF])
        hid = one(0, [NT, FF])
        hmax = sb("hmax", [P, NT])
        hinv = sb("hinv", [P, NT])
        hqf = one(2048, [NT, FF])
        hq = one(4096, [NT, FF], BF16)
        hqT = one(5120, [NT, FC, P], BF16)
        dsc = sb("dsc", [P, NT])

        part = [[two(256 * (3 * s + i), [T], BF16) for i in range(3)] for s in range(2)]
        rest = [two(1536 + 512 * s, [T]) for s in range(2)]
        stack = [one(2048 * i, [NPAIR, T], BF16) for i in range(2)]
        smax = sb("smax", [P, 2, NT, HG])
        srest = sb("srest", [P, 2, NT, HG])
        sparts = sb("sparts", [P, 2, NT, 3, HG], BF16)
        mT = sb("mT", [3 * HG, 2, T], BF16)
        prob = one(4096, [2, 3, T])
        rden = two(2560, [T])
        att = sb("att", [P, T])

        ctx4 = sb("ctx4", [P, 4, CTX])
        kcol = sb("kcol", [P, CTX])
        kblk = sb("kblk", [P, H, CTX])
        vrow = sb("vrow", [P, D])
        vblk = sb("vblk", [P, 4, D])
        qT = two(3072, [T])
        x4b = two(3584, [NT, D])
        s1 = one(0, [2, H, CTX])
        s2 = one(1024, [2, H, CTX])
        s3 = one(2048, [2, H, CTX])
        cmax = sb("cmax", [P, 2, H])
        pc = one(3072, [2, 4, P])
        pT = two(0, [4, T])

        glog = sb("glog", [P, NT, NE])
        gge = two(512, [NT, NE, NE])
        ggt = two(768, [NT, NE, NE])
        rank = sb("rank", [P, NT, NE])
        gtop = sb("gtop", [P, NT])
        gexp = sb("gexp", [P, NT, NE])
        gsum = sb("gsum", [P, NT])
        gates = sb("gates", [P, NT, NE])
        act_h = one(0, [2, FC, T])
        moe = two(0, [NT, D])

        bank = [ctx.enter_context(nc.psum_tensor(f"bank{i}", [P, 512], F32)) for i in range(8)]

        def tiles(t, n=P):
            return t.rearrange("p (a n) -> p a n", n=n)

        loaded = {n: sem("ld_" + n) for n in a if n != "xtok"}
        early = sem("early")
        pool_early = sem("pool_early")
        act_early = sem("act_early")
        pe_early = sem("pe_early")
        pool_passed = sem("pool_passed")
        dve_passed = sem("dve_passed")
        dve_link = sem("dve_link")
        act_link = sem("act_link")
        xz_ready = sem("xz_ready")
        xin_ready = sem("xin_ready")
        conv_done = sem("conv_done")
        z_act = sem("z_act")
        xc_ready = sem("xc_ready")
        bc_ready = sem("bc_ready")
        xcT_ready = sem("xcT_ready")
        b_ready = sem("b_ready")
        c_ready = sem("c_ready")
        ln_dt = sem("ln_dt")
        dt_ready = sem("dt_ready")
        dta_ready = sem("dta_ready")
        xdt_ready = sem("xdt_ready")
        gsuf_ready = sem("gsuf_ready")
        esuf_ready = sem("esuf_ready")
        bsuf_ready = sem("bsuf_ready")
        gdec_ready = sem("gdec_ready")
        dec_ready = sem("dec_ready")
        ct_ready = sem("ct_ready")
        bt_ready = sem("bt_ready")
        lev_ready = sem("lev_ready")
        masked = sem("masked")
        mix_ready = sem("mix_ready")
        hp_ready = sem("hp_ready")
        h_ready = sem("h_ready")
        y_ready = sem("y_ready")
        ya_ready = sem("ya_ready")
        yg_ready = sem("yg_ready")
        outA_ready = sem("outA_ready")
        var_ready = sem("var_ready")
        rstd_ready = sem("rstd_ready")
        x_ready = [sem(f"x{k}_ready") for k in range(1, 7)]
        xT_ps = [sem(f"x{k}T_ps") for k in range(1, 6)]
        xT_sb = [sem(f"x{k}T_sb") for k in range(1, 6)]
        comp_ps = sem("comp_ps")
        comp_sb = sem("comp_sb")
        back_ps = sem("back_ps")
        gsc_ready = sem("gsc_ready")
        gu_ps = sem("gu_ps")
        g_act = sem("g_act")
        hid_ready = sem("hid_ready")
        xq_ready = sem("xq_ready")
        hq_ready = sem("hq_ready")
        hq_magic = sem("hq_magic")
        hT_ps = sem("hT_ps")
        hT_sb = sem("hT_sb")
        down_ps = sem("down_ps")
        kq_ps = sem("kq_ps")
        v_ps = sem("v_ps")
        v_sb = sem("v_sb")
        part0 = sem("part0")
        rest0 = sem("rest0")
        part1 = sem("part1")
        part2 = sem("part2")
        stacked = sem("stacked")
        s_ps = sem("s_ps")
        s_max = sem("s_max")
        mp_ready = sem("mp_ready")
        mT_ps = sem("mT_ps")
        mT_sb = sem("mT_sb")
        st_ps = sem("st_ps")
        prob_ready = sem("prob_ready")
        pv_done = sem("pv_done")
        att_ready = sem("att_ready")
        proj_ps = sem("proj_ps")
        ctx_ready = sem("ctx_ready")
        ckv_ps = sem("ckv_ps")
        kcol_ready = sem("kcol_ready")
        kv_blk = sem("kv_blk")
        cq_ps = sem("cq_ps")
        cq_sb = sem("cq_sb")
        x4b_ready = sem("x4b_ready")
        cs_ps = sem("cs_ps")
        cs_kept = sem("cs_kept")
        cs_full = sem("cs_full")
        cs_max = sem("cs_max")
        cs_sub = sem("cs_sub")
        cp_ready = sem("cp_ready")
        cpT_ps = sem("cpT_ps")
        cpT_sb = sem("cpT_sb")
        co_ps = sem("co_ps")
        co_ready = sem("co_ready")
        cproj_ps = sem("cproj_ps")
        gate_ps = sem("gate_ps")
        gsub_ready = sem("gsub_ready")
        gexp_ready = sem("gexp_ready")
        h_ps = sem("h_ps")
        h_act = sem("h_act")
        e_ps = sem("e_ps")
        e_added = sem("e_added")
        tok_loaded = sem("tok_loaded")
        stored = sem("stored")

        block = ctx.enter_context(nc.Block())

        order = ["w_in", "xT", "conv_w", "chan", "w_bb", "w_cc", "w_bdt", "alog", "lev_a", "lev_b", "suf", "ident",
                 "lmask", "w_out", "ctxT", "ones", "cconv", "cols", "wg", "wu", "wd", "identb", "w_q", "w_k",
                 "w_v", "w_p", "tri_q", "tri_k", "pick", "c_q", "c_k", "c_v", "c_o", "rows", "hmask", "vmask", "mask",
                 "w1", "w2", "wgate", "before"]
        assert sorted(order + ["xtok"]) == sorted(a)

        def arrived(engine, *which):
            for n in which:
                engine.wait_ge(loaded[n], 16)

        @block.sync
        def _(sp):
            for n in order:
                sp.dma_start(names[n][:], a[n]).then_inc(loaded[n], 16)
            with sp.Fori(0, B) as b:
                sp.dma_start(xtok[:], a["xtok"][b]).then_inc(tok_loaded, 16)
                sp.wait_ge(part0, 2 * b + 2)
                sp.wait_ge(part1, 2 * b + 2)
                sp.wait_ge(part2, 2 * b + 2)
                for g, halves in enumerate(PRODUCTS):
                    for side in range(2):
                        for par in range(2):
                            base = 64 * par + HD * g
                            sp.dma_start(stack[side][base:base + HD, :, :],
                                                    part[side][halves[side]][64 * par:64 * par + 64, :]).then_inc(stacked, 16)
                sp.wait_ge(x_ready[5], NT * b + NT)
                sp.dma_start(out[b], xs[5][:]).then_inc(stored, 16)
            sp.wait_ge(stored, 16 * (B + 1))

        @block.gpsimd
        def _(pool):
            pool.memset(minus_half[:], -0.5).then_inc(pool_early, 1)
            pool.memset(xin[:, :, 0:TAPS - 1], 0.0).then_inc(pool_early, 1)
            pool.memset(vpad[:], 0.0).then_inc(pool_early, 1)
            pool.wait_ge(pool_early, 3)
            for h in range(H):
                lo = 64 + HD * (h % HG)
                pool.memset(vpad[:, :, h, lo:lo + HD], 1.0).then_inc(pool_early, 1)
            pool.memset(sparts[:], 0.0).then_inc(stored, 16)
            pool.wait_ge(stored, 16)

            def rstd_of(b, k):
                pool.wait_ge(var_ready, 6 * b + k)
                pool.tensor_tensor(rstd[:], var[:], minus_half[:], ALU.pow).then_inc(rstd_ready, 1)

            with pool.Fori(0, B) as b:
                pool.wait_ge(b_ready, b + 1)
                for t in range(NT):
                    pool.wait_ge(dec_ready, NT * b + (t + 1))
                    pool.tensor_tensor(
                        bt[:, t], dec[:, t], bs[:, None, t * P:(t + 1) * P].broadcast_to([P, 4, P]), ALU.mult).then_inc(bt_ready, 1)
                for c in range(NC):
                    pool.wait_ge(ya_ready, 2 * b + (c + 1))
                    pool.wait_ge(z_act, 2 * b + (c + 1))
                    pool.tensor_tensor(yg[:, c], ya[:, c], zs[:, c], ALU.mult).then_inc(yg_ready, 1)
                rstd_of(b, 1)
                rstd_of(b, 2)
                for t in range(NT):
                    pool.wait_ge(hq_magic, NT * b + (t + 1))
                    pool.sem_inc(pool_passed)
                    pool.tensor_scalar(hq[:, t], hqf[:, t], MAGIC, None, ALU.subtract).then_inc(hq_ready, 1)
                rstd_of(b, 3)
                for s in range(2):
                    pool.wait_ge(rest0, 2 * b + (s + 1))
                    pool.sem_inc(pool_passed)
                    pool.tensor_copy(part[s][1][:], rest[s][:]).then_inc(part1, 1)
                    pool.wait_ge(part1, 2 * b + (s + 1))
                    pool.tensor_tensor(part[s][2][:], rest[s][:], part[s][1][:], ALU.subtract).then_inc(part2, 1)
                rstd_of(b, 4)
                pool.wait_ge(x_ready[3], NT * b + NT)
                pool.tensor_tensor(x4b[:], xs[3][:], rows[:, None, 1].broadcast_to([P, NT, D]), ALU.add).then_inc(x4b_ready, 1)
                for t in range(NT):
                    pool.wait_ge(cs_kept, NT * b + (t + 1))
                    pool.tensor_tensor(s2[:, t % 2], s1[:, t % 2],
                                                  mfill[:, None, t].broadcast_to([P, H, CTX]), ALU.add).then_inc(cs_full, 1)
                    pool.wait_ge(cs_max, NT * b + (t + 1))
                    pool.tensor_tensor(s3[:, t % 2], s2[:, t % 2],
                                                 cmax[:, t % 2, :, None].broadcast_to([P, H, CTX]), ALU.subtract).then_inc(cs_sub, 1)
                rstd_of(b, 5)
                rstd_of(b, 6)

        @block.scalar
        def _(act):
            def do(out_, in_, func, **kw):
                return nc.scalar.activation(out_, in_, func, **kw)

            arrived(act, "alog")
            do(neg_a[:], alog[:], ACT.Exp).then_inc(act_early, 1)
            arrived(act, "chan", "cols", "ctxT")
            act.wait_ge(pool_early, 2)

            def turn(b, k, bk):
                act.wait_ge(xT_ps[k - 1], b + 1)
                do(turned[:, 0:T], bank[bk][:], ACT.Copy).then_inc(xT_sb[k - 1], 1)

            with act.Fori(0, B) as b:
                for c in range(NC):
                    act.wait_ge(xz_ready, 4 * b + (c + 1))
                    do(xin[:, c, TAPS - 1:], bank[c][:], ACT.Copy).then_inc(xin_ready, 1)
                for c in range(NC):
                    act.wait_ge(xz_ready, 4 * b + (NC + c + 1))
                    do(zs[:, c], bank[NC + c][:], ACT.Silu).then_inc(z_act, 1)
                for c in range(NC):
                    act.wait_ge(conv_done, 2 * b + (c + 1))
                    do(xc[:, c], cacc[:, c], ACT.Silu).then_inc(xc_ready, 1)
                act.wait_ge(bc_ready, 3 * b + 1)
                do(bs[:], bank[4][:], ACT.Copy).then_inc(b_ready, 1)
                act.wait_ge(bc_ready, 3 * b + 3)
                do(dts[:, 0], bank[6][:, 0:NT * (DS + 1)].rearrange("p (n c) -> p n c", c=DS + 1)[:, :, DS],
                               ACT.Abs).then_inc(act_link, 1)
                act.wait_ge(act_link, 3 * b + 1)
                do(dts[:, 1], dts[:, 0], ACT.Exp, scale=-1.0).then_inc(act_link, 1)
                act.wait_ge(act_link, 3 * b + 2)
                do(dts[:, 2], dts[:, 1], ACT.Ln, bias=1.0).then_inc(ln_dt, 1)
                act.wait_ge(dt_ready, b + 1)
                for t in range(NT):
                    act.wait_ge(xcT_ready, 2 * b + (t // 2 + 1))
                    do(xdt[:, t], bank[t // 2][:, (t % 2) * DI:(t % 2 + 1) * DI], ACT.Copy,
                                    scale=dts[:, 3, t:t + 1]).then_inc(xdt_ready, 1)
                act.wait_ge(gsuf_ready, b + 1)
                do(esuf[:], bank[7][:, 0:NT * DS].rearrange("p (n s) -> p n s", s=DS), ACT.Exp).then_inc(esuf_ready, 1)
                for t in range(NT):
                    act.wait_ge(gdec_ready, NT * b + (t + 1))
                    do(dec[:, t], tiles(bank[2 + t % 2]), ACT.Exp).then_inc(dec_ready, 1)
                turn(b, 1, 0)
                do(turned[:, T:], ctxT[:, b], ACT.Copy).then_inc(act_link, 1)
                act.wait_ge(comp_ps, b + 1)
                do(turned[:, KEEP:KEEP + COMP], bank[1][:, 0:COMP], ACT.Identity, bias=cols[:, 0:1]).then_inc(comp_sb, 1)
                do(ctx4[:], ctxT[:, b, None].broadcast_to([P, 4, CTX]), ACT.Copy).then_inc(ctx_ready, 1)
                act.wait_ge(ckv_ps, 2 * b + 1)
                do(kcol[:], bank[6][:, 0:CTX], ACT.Identity, bias=cols[:, 2:3]).then_inc(kcol_ready, 1)
                act.wait_ge(xT_ps[1], b + 1)
                do(xqT[:], bank[0][:].bitcast(BF16)[:, 0:T], ACT.Copy).then_inc(xT_sb[1], 1)
                for t in range(NT):
                    act.wait_ge(gu_ps, NT * b + (t + 1))
                    if t >= 2:
                        act.wait_ge(hid_ready, NT * b + (t - 1))
                    if t == 0:
                        act.wait_ge(gsc_ready, b + 1)
                    do(gact[:, t % 2], bank[2 + 2 * (t % 2)][:], ACT.Silu, scale=gsc[:, t, 0:1]).then_inc(g_act, 1)
                for t in range(NT):
                    act.wait_ge(hT_ps, NT * b + (t + 1))
                    do(hqT[:, t], bank[6 + t % 2][:].bitcast(BF16)[:, 0:FF].rearrange(
                        "p (c n) -> p c n", n=P), ACT.Copy).then_inc(hT_sb, 1)
                turn(b, 3, 0)
                for s in range(2):
                    act.wait_ge(kq_ps, 2 * b + (s + 1))
                    do(part[s][0][:], bank[1 + s][:], ACT.Copy).then_inc(part0, 1)
                for hg in range(2):
                    act.wait_ge(mT_ps, 2 * b + (hg + 1))
                    do(mT[:, hg], bank[3][0:3 * HG].bitcast(BF16)[:, 0:T], ACT.Copy).then_inc(mT_sb, 1)
                    for h in range(hg * HG, (hg + 1) * HG):
                        if h >= 2:
                            act.wait_ge(pv_done, H * b + (h - 1))
                        for j, n in enumerate((512, 512, 256)):
                            act.wait_ge(st_ps, 3 * H * b + (3 * h + j + 1))
                            do(prob[:, h % 2, j, 0:n], bank[4 + (3 * h + j) % 2][:, 0:n], ACT.Exp,
                                             scale=SCORE_SCALE).then_inc(prob_ready, 1)
                turn(b, 4, 0)
                act.wait_ge(cq_ps, b + 1)
                do(qT[:], bank[1][:], ACT.Identity, bias=cols[:, 1:2]).then_inc(cq_sb, 1)
                for t in range(NT):
                    act.wait_ge(cs_sub, NT * b + (t + 1))
                    if t >= 2:
                        act.wait_ge(cpT_ps, NT * b + (t - 1))
                    do(pc[:, t % 2], s3[:, t % 2].rearrange("p h k -> p (h k)").rearrange(
                        "p (c n) -> p c n", n=P), ACT.Exp).then_inc(cp_ready, 1)
                    act.wait_ge(cpT_ps, NT * b + (t + 1))
                    do(pT[:, :, t * P:(t + 1) * P], tiles(bank[4 + t % 2]), ACT.Copy).then_inc(cpT_sb, 1)
                turn(b, 5, 0)
                act.wait_ge(gsub_ready, b + 1)
                do(gexp[:], glog[:], ACT.Exp).then_inc(gexp_ready, 1)
                for e in range(SLICES):
                    for c in range(FC):
                        act.wait_ge(h_ps, SLICES * FC * b + (e * FC + c + 1))
                        if e >= 2:
                            act.wait_ge(e_ps, SLICES * b + (e - 1))
                        do(act_h[:, e % 2, c], bank[2 + c][:], ACT.Silu).then_inc(h_act, 1)

        @block.vector
        def _(dve):
            V = nc.vector
            step = [0]

            def link(instruction):
                instruction.then_inc(early, 1)
                step[0] += 1
                dve.wait_ge(early, step[0])

            arrived(dve, "wg", "wu", "wd")
            link(V.tensor_reduce(wabs[:, 0:1], wg[:], AX.X, ALU.add, apply_absolute_value=True))
            link(V.tensor_reduce(wabs[:, 1:2], wu[:], AX.X, ALU.add, apply_absolute_value=True))
            link(V.tensor_reduce(wabs[:, 2:3], wd[:].rearrange("p c n -> p (c n)"), AX.X, ALU.add,
                                 apply_absolute_value=True))
            summed = step[0]
            dve.wait_ge(pe_early, 1)
            link(V.tensor_scalar(wscale[:], bank[7][:, 0:3], 1.0 / (D * FF), 1e-5, ALU.mult, ALU.max))
            link(V.reciprocal(winv[:], wscale[:]))
            for i, (w, q) in enumerate(((wg, wgq), (wu, wuq), (wd, wdq))):
                if i == 2:
                    w, q = w[:].rearrange("p c n -> p (c n)"), q[:].rearrange("p c n -> p (c n)")
                else:
                    w, q = w[:], q[:]
                link(V.tensor_scalar(wtmp[:], w, winv[:, i:i + 1], MAGIC, ALU.mult, ALU.add))
                link(V.tensor_scalar(wtmp[:], wtmp[:], MAGIC, 1.0, ALU.subtract, ALU.min))
                link(V.tensor_scalar(q, wtmp[:], -1.0, None, ALU.max))
            arrived(dve, "mask")
            link(V.tensor_scalar(mkeep[:], mask[:], 0, CROSS_SCALE, ALU.not_equal, ALU.mult))
            link(V.tensor_scalar(mfill[:], mask[:], 0, -1e-9, ALU.is_equal, ALU.mult))
            arrived(dve, "conv_w", "chan", "lmask", "rows", "hmask", "vmask", "before")
            dve.wait_ge(act_early, 1)
            dve.wait_ge(pool_early, 3 + H)

            links = [0]

            with dve.Fori(0, B) as b:
                def chain(instruction):
                    instruction.then_inc(dve_link, 1)
                    links[0] += 1
                    dve.wait_ge(dve_link, 66 * b + links[0])

                def norm(k):
                    for t in range(NT):
                        last = V.bn_stats(stats[:, t], res[:, t])
                    chain(last)
                    dve.sem_inc(dve_passed)
                    for t in range(NT):
                        last = V.bn_aggr(mv[:, t], stats[:, t])
                    chain(last)
                    V.tensor_scalar(var[:], mv[:, :, 1], EPS, None, ALU.add).then_inc(var_ready, 1)
                    dve.wait_ge(rstd_ready, 6 * b + k)
                    if k == 6:
                        dve.wait_ge(stored, 16 * b + 16)
                    for t in range(NT):
                        V.tensor_scalar(xs[k - 1][:, t], res[:, t], mv[:, t, 0:1], rstd[:, t:t + 1],
                                                          ALU.subtract, ALU.mult).then_inc(x_ready[k - 1], 1)

                for c in range(NC):
                    dve.wait_ge(xin_ready, 2 * b + (c + 1))
                    chain(V.tensor_scalar(cacc[:, c], xin[:, c, 0:T], conv_w[:, c, 0:1], chan[:, c, 0:1],
                                          ALU.mult, ALU.add))
                    for k in range(1, TAPS):
                        tap = V.scalar_tensor_tensor(out=cacc[:, c], in0=xin[:, c, k:k + T], scalar=conv_w[:, c, k:k + 1],
                                                     in1=cacc[:, c], op0=ALU.mult, op1=ALU.add)
                        if k < TAPS - 1:
                            chain(tap)
                        else:
                            tap.then_inc(conv_done, 1)
                dve.wait_ge(bc_ready, 3 * b + 2)
                V.tensor_copy(cs[:], bank[5][:]).then_inc(c_ready, 1)
                dve.wait_ge(ln_dt, b + 1)
                V.scalar_tensor_tensor(
                    out=dts[:, 3], in0=bank[6][:, 0:NT * (DS + 1)].rearrange("p (n c) -> p n c", c=DS + 1)[:, :, DS],
                    scalar=0.0, in1=dts[:, 2], op0=ALU.max, op1=ALU.add).then_inc(dt_ready, 1)
                dve.wait_ge(dt_ready, b + 1)
                for t in range(NT):
                    V.tensor_scalar(dta[:, t], neg_a[:], dts[:, 3, t:t + 1], -1.0, ALU.mult, ALU.mult).then_inc(dta_ready, 1)
                dve.wait_ge(c_ready, b + 1)

                def decayed(t):
                    dve.wait_ge(dec_ready, NT * b + (t + 1))
                    V.tensor_tensor(ct[:, t], dec[:, t],
                                                cs[:, None, t * P:(t + 1) * P].broadcast_to([P, 4, P]), ALU.mult).then_inc(ct_ready, 1)

                def state(t):
                    dve.wait_ge(hp_ready, (NT - 1) * b + (t + 1))
                    if t == 0:
                        V.tensor_copy(hst[:, 0], bank[6][0:DS, 0:DI]).then_inc(h_ready, 1)
                    else:
                        dve.wait_ge(h_ready, (NT - 1) * b + t)
                        V.scalar_tensor_tensor(out=hst[:, t], in0=hst[:, t - 1],
                                                          scalar=dec[0:DS, t, 3, P - 1:P], in1=bank[6][0:DS, 0:DI],
                                                          op0=ALU.mult, op1=ALU.add).then_inc(h_ready, 1)

                def mixing(t):
                    dve.wait_ge(lev_ready, NT * b + (t + 1))
                    V.tensor_tensor(mm[:, t % 2, 0:4], tiles(bank[0]), lmask[:, 0:4], ALU.mult)
                    V.tensor_tensor(mm[:, t % 2, 4:8], tiles(bank[1]), lmask[:, 4:8], ALU.mult).then_inc(masked, 1)
                    dve.wait_ge(masked, NT * b + (t + 1))
                    V.tensor_reduce(mix[:, t], mm[:, t % 2].rearrange("p l n -> p n l"), AX.X, ALU.add).then_inc(mix_ready, 1)

                decayed(0)
                dve.wait_ge(esuf_ready, b + 1)
                V.tensor_tensor(
                    bsuf[:], esuf[:],
                    bank[6][:, 0:NT * (DS + 1)].rearrange("p (n c) -> p n c", c=DS + 1)[:, :, 0:DS], ALU.mult).then_inc(bsuf_ready, 1)
                decayed(1)
                mixing(0)
                state(0)
                decayed(2)
                mixing(1)
                state(1)
                decayed(3)
                mixing(2)
                state(2)
                mixing(3)
                dve.wait_ge(y_ready, b + 1)
                for c in range(NC):
                    V.scalar_tensor_tensor(out=ya[:, c], in0=xc[:, c], scalar=chan[:, c, 1:2],
                                                       in1=bank[4 + c][:], op0=ALU.mult, op1=ALU.add).then_inc(ya_ready, 1)
                dve.wait_ge(outA_ready, b + 1)
                dve.wait_ge(tok_loaded, 16 * b + 16)
                chain(V.tensor_tensor(res[:], tiles(bank[7]), xtok[:], ALU.add))
                norm(1)

                dve.wait_ge(back_ps, b + 1)
                chain(V.tensor_tensor(res[:], tiles(bank[2]), xs[0][:], ALU.add))
                norm(2)

                dve.wait_ge(x_ready[1], NT * b + NT)
                chain(V.tensor_reduce(amax[:], xs[1][:], AX.X, ALU.max, apply_absolute_value=True))
                chain(V.tensor_scalar(amax[:], amax[:], 1e-5, None, ALU.max))
                chain(V.reciprocal(ainv[:], amax[:]))
                chain(V.tensor_scalar(ainv[:], ainv[:], 127.0, None, ALU.mult))
                for t in range(NT):
                    last = V.tensor_scalar(xqf[:, t], xs[1][:, t], ainv[:, t:t + 1], MAGIC, ALU.mult, ALU.add)
                chain(last)
                V.tensor_scalar(xq[:], xqf[:], MAGIC, None, ALU.subtract).then_inc(xq_ready, 1)
                V.tensor_scalar(gsc[:, :, 0], amax[:], wscale[:, 0:1], 1.0 / 127.0, ALU.mult, ALU.mult)
                V.tensor_scalar(gsc[:, :, 1], amax[:], wscale[:, 1:2], 1.0 / 127.0, ALU.mult, ALU.mult).then_inc(gsc_ready, 1)
                dve.wait_ge(gsc_ready, b + 1)
                dve.wait_ge(kcol_ready, b + 1)
                V.tensor_tensor(kblk[:], kcol[:, None].broadcast_to([P, H, CTX]),
                                          hmask[:, :, None].broadcast_to([P, H, CTX]), ALU.mult).then_inc(kv_blk, 1)
                dve.wait_ge(ckv_ps, 2 * b + 2)
                chain(V.tensor_tensor(vrow[:], bank[7][:, 0:D], rows[:, 0], ALU.add))
                V.tensor_tensor(vblk[:], vrow[:, None].broadcast_to([P, 4, D]), vmask[:], ALU.mult).then_inc(kv_blk, 1)
                for t in range(NT):
                    dve.wait_ge(g_act, NT * b + (t + 1))
                    V.scalar_tensor_tensor(out=hid[:, t], in0=bank[3 + 2 * (t % 2)][:],
                                                        scalar=gsc[:, t, 1:2], in1=gact[:, t % 2],
                                                        op0=ALU.mult, op1=ALU.mult).then_inc(hid_ready, 1)
                    dve.wait_ge(hid_ready, NT * b + (t + 1))
                    chain(V.tensor_reduce(hmax[:, t:t + 1], hid[:, t], AX.X, ALU.max, apply_absolute_value=True))
                    chain(V.tensor_scalar(hmax[:, t:t + 1], hmax[:, t:t + 1], 1e-5, None, ALU.max))
                    chain(V.reciprocal(hinv[:, t:t + 1], hmax[:, t:t + 1]))
                    chain(V.tensor_scalar(hinv[:, t:t + 1], hinv[:, t:t + 1], 127.0, None, ALU.mult))
                    V.tensor_scalar(hqf[:, t], hid[:, t], hinv[:, t:t + 1], MAGIC, ALU.mult, ALU.add).then_inc(hq_magic, 1)
                chain(V.tensor_scalar(dsc[:], hmax[:], wscale[:, 2:3], 1.0 / 127.0, ALU.mult, ALU.mult))
                dve.wait_ge(down_ps, b + 1)
                for t in range(NT):
                    last = V.scalar_tensor_tensor(out=res[:, t], in0=bank[0][:, t * P:(t + 1) * P],
                                                  scalar=dsc[:, t:t + 1], in1=xs[1][:, t], op0=ALU.mult, op1=ALU.add)
                chain(last)
                norm(3)

                for s in range(2):
                    dve.wait_ge(part0, 2 * b + (s + 1))
                    V.tensor_tensor(rest[s][:], bank[1 + s][:], part[s][0][:], ALU.subtract).then_inc(rest0, 1)
                dve.wait_ge(v_ps, b + 1)
                for hg in range(2):
                    for t in range(NT):
                        last = V.tensor_copy(
                            diagonal(vpad, t, hg), bank[3][:, t * P + hg * 64:t * P + hg * 64 + 64]
                            .rearrange("p (h d) -> p h d", d=HD))
                last.then_inc(v_sb, 1)
                for hg in range(2):
                    for h in range(hg * HG, (hg + 1) * HG):
                        hl = h % HG
                        for j, (ta, tb) in enumerate(((3, None), (2, 0), (1, None))):
                            n = 3 * h + j
                            dve.wait_ge(s_ps, 3 * H * b + (n + 1))
                            src = bank[6 + n % 2]
                            last = V.tensor_reduce(smax[:, hg, ta, hl:hl + 1], src[:, 0:(ta + 1) * P], AX.X, ALU.max)
                            if tb is not None:
                                last = V.tensor_reduce(smax[:, hg, tb, hl:hl + 1], src[:, 384:512], AX.X, ALU.max)
                            last.then_inc(s_max, 1)
                    dve.wait_ge(s_max, 3 * H * b + (3 * HG * (hg + 1)))
                    chain(V.tensor_copy(sparts[:, hg, :, 0], smax[:, hg]))
                    chain(V.tensor_tensor(srest[:, hg], smax[:, hg], sparts[:, hg, :, 0], ALU.subtract))
                    chain(V.tensor_copy(sparts[:, hg, :, 1], srest[:, hg]))
                    V.tensor_tensor(sparts[:, hg, :, 2], srest[:, hg], sparts[:, hg, :, 1], ALU.subtract).then_inc(mp_ready, 1)
                for hg in range(2):
                    dve.wait_ge(pv_done, H * b + (HG * (hg + 1)))
                    if hg:
                        dve.wait_ge(att_ready, 2 * b + hg)
                    chain(V.reciprocal(rden[0:64], bank[1 + hg][64:128]))
                    V.tensor_tensor(att[64 * hg:64 * hg + 64], bank[1 + hg][0:64], rden[0:64], ALU.mult).then_inc(att_ready, 1)
                dve.wait_ge(proj_ps, b + 1)
                chain(V.scalar_tensor_tensor(out=res[:], in0=tiles(bank[0]), scalar=PROJ_SCALE, in1=xs[2][:],
                                             op0=ALU.mult, op1=ALU.add))
                norm(4)

                for t in range(NT):
                    dve.wait_ge(cs_ps, NT * b + (t + 1))
                    if t >= 2:
                        dve.wait_ge(cs_full, NT * b + (t - 1))
                    V.tensor_tensor(s1[:, t % 2], bank[2 + t % 2][:].rearrange("p (h k) -> p h k", k=CTX),
                                               mkeep[:, None, t].broadcast_to([P, H, CTX]), ALU.mult).then_inc(cs_kept, 1)
                    dve.wait_ge(cs_full, NT * b + (t + 1))
                    if t >= 2:
                        dve.wait_ge(cs_sub, NT * b + (t - 1))
                    V.tensor_reduce(cmax[:, t % 2], s2[:, t % 2], AX.X, ALU.max).then_inc(cs_max, 1)
                dve.wait_ge(co_ps, b + 1)
                chain(V.reciprocal(rden[:], bank[7][:]))
                V.tensor_tensor(att[:], bank[6][:], rden[:], ALU.mult).then_inc(co_ready, 1)
                dve.wait_ge(cproj_ps, b + 1)
                dve.wait_ge(x4b_ready, b + 1)
                chain(V.tensor_tensor(res[:], tiles(bank[0]), x4b[:], ALU.add))
                norm(5)

                dve.wait_ge(gate_ps, b + 1)
                logits = bank[1][:, 0:NT * NE].rearrange("p (n e) -> p n e", e=NE)
                chain(V.tensor_copy(glog[:], logits))
                for t in range(NT):
                    other = glog[:, t, None].broadcast_to([P, NE, NE])
                    own = glog[:, t, :, None].broadcast_to([P, NE, NE])
                    V.tensor_tensor(gge[:, t], other, own, ALU.is_ge)
                    last = V.tensor_tensor(ggt[:, t], other, own, ALU.is_gt)
                chain(last)
                chain(V.tensor_tensor(gge[:].rearrange("p n a c -> p n (a c)"), gge[:].rearrange("p n a c -> p n (a c)"),
                                      before[:, None].broadcast_to([P, NT, NE * NE]), ALU.mult))
                chain(V.tensor_tensor(ggt[:], ggt[:], gge[:], ALU.max))
                chain(V.tensor_reduce(rank[:], ggt[:], AX.X, ALU.add))
                chain(V.tensor_scalar(rank[:], rank[:], 2.0, None, ALU.is_lt))
                chain(V.tensor_reduce(gtop[:], glog[:], AX.X, ALU.max))
                V.tensor_tensor(glog[:], glog[:], gtop[:, :, None].broadcast_to([P, NT, NE]),
                                              ALU.subtract).then_inc(gsub_ready, 1)
                dve.wait_ge(gexp_ready, b + 1)
                chain(V.tensor_tensor(gates[:], gexp[:], rank[:], ALU.mult))
                chain(V.tensor_reduce(gsum[:], gates[:], AX.X, ALU.add))
                chain(V.reciprocal(gsum[:], gsum[:]))
                chain(V.tensor_tensor(gates[:], gates[:], gsum[:, :, None].broadcast_to([P, NT, NE]), ALU.mult))
                for e in range(SLICES):
                    dve.wait_ge(e_ps, SLICES * b + (e + 1))
                    src = bank[6 + e % 2]
                    if e == 0:
                        V.tensor_tensor(moe[:], tiles(src), xs[4][:], ALU.add).then_inc(e_added, 1)
                    else:
                        dve.wait_ge(e_added, SLICES * b + e)
                        dst = res if e == SLICES - 1 else moe
                        for t in range(NT):
                            last = V.scalar_tensor_tensor(out=dst[:, t], in0=src[:, t * P:(t + 1) * P],
                                                          scalar=gates[:, t, e - 1:e], in1=moe[:, t],
                                                          op0=ALU.mult, op1=ALU.add)
                        last.then_inc(e_added, 1)
                dve.wait_ge(e_added, SLICES * b + SLICES)
                norm(6)

        @block.tensor
        def _(pe):
            mmul = nc.tensor.matmul

            arrived(pe, "ones")
            pe.wait_ge(early, 3)
            mmul(bank[7][:, 0:3], ones[:], wabs[:], start=True, stop=True).then_inc(pe_early, 1)
            arrived(pe, "w_in", "xT", "w_bb", "w_cc", "w_bdt", "lev_a", "lev_b", "suf", "ident", "w_out", "cconv", "identb", "w_q", "w_k",
                    "w_v", "w_p", "tri_q", "tri_k", "pick", "c_q", "c_k", "c_v", "c_o", "vmask", "w1", "w2", "wgate")
            pe.wait_ge(pool_early, 3 + H)

            def turn(b, k, bk, src=None):
                for t in range(NT):
                    pe.wait_ge(x_ready[k - 1], NT * b + (t + 1))
                    last = nc.tensor.transpose(bank[bk][:, t * P:(t + 1) * P], xs[k - 1][:, t], ident[:])
                last.then_inc(xT_ps[k - 1], 1)
                pe.wait_ge(xT_sb[k - 1], b + 1)

            with pe.Fori(0, B) as b:
                for c in range(2 * NC):
                    mmul(bank[c][:], w_in[:, c * P:(c + 1) * P], xT[:, b], start=True, stop=True).then_inc(xz_ready, 1)
                pe.wait_ge(xc_ready, 2 * b + NC)
                for i, w in enumerate((w_bb, w_cc)):
                    for c in range(NC):
                        last = mmul(bank[4 + i][:], w[:, c], xc[:, c], start=c == 0, stop=c == NC - 1)
                    last.then_inc(bc_ready, 1)
                for t in range(NT):
                    for c in range(NC):
                        last = mmul(bank[6][:, t * (DS + 1):(t + 1) * (DS + 1)], xc[:, c, t * P:(t + 1) * P], w_bdt[:, c],
                                    start=c == 0, stop=c == NC - 1)
                last.then_inc(bc_ready, 1)
                for t in range(NT):
                    for c in range(NC):
                        last = nc.tensor.transpose(bank[t // 2][:, (t % 2) * DI + c * P:(t % 2) * DI + (c + 1) * P],
                                                   xc[:, c, t * P:(t + 1) * P], ident[:])
                    if t % 2:
                        last.then_inc(xcT_ready, 1)
                pe.wait_ge(z_act, 2 * b + NC)

                def decays(t):
                    pe.wait_ge(dta_ready, NT * b + (t + 1))
                    if t >= 2:
                        pe.wait_ge(dec_ready, NT * b + (t - 1))
                    mmul(bank[2 + t % 2][0:64], dta[:, t, 0:DS], lev_a[:].rearrange("p l n -> p (l n)"),
                         start=True, stop=True)
                    mmul(bank[2 + t % 2][64:128], dta[:, t, DS:2 * DS],
                                       lev_b[:].rearrange("p l n -> p (l n)"), start=True, stop=True).then_inc(gdec_ready, 1)

                def levels(t):
                    pe.wait_ge(ct_ready, NT * b + (t + 1))
                    pe.wait_ge(bt_ready, NT * b + (t + 1))
                    if t == 0:
                        pe.wait_ge(xdt_ready, NT * b + NT)
                    else:
                        pe.wait_ge(masked, NT * b + t)
                    for i in range(3):
                        mmul(bank[0][:, i * P:(i + 1) * P], bt[0:64, t, i], ct[0:64, t, i], start=True, stop=True)
                    mmul(bank[0][:, 3 * P:4 * P], bs[0:64, t * P:(t + 1) * P], cs[0:64, t * P:(t + 1) * P],
                         start=True, stop=True)
                    for i in range(4):
                        last = mmul(bank[1][:, i * P:(i + 1) * P], bt[64:128, t, i], ct[64:128, t, i],
                                    start=True, stop=True)
                    last.then_inc(lev_ready, 1)

                def carry(t):
                    if t == 0:
                        pe.wait_ge(bsuf_ready, b + 1)
                    else:
                        pe.wait_ge(h_ready, (NT - 1) * b + t)
                    mmul(bank[6][0:DS, 0:DI], bsuf[:, t], xdt[:, t], start=True, stop=True).then_inc(hp_ready, 1)

                def outputs(t):
                    pe.wait_ge(mix_ready, NT * b + (t + 1))
                    if t > 0:
                        pe.wait_ge(h_ready, (NT - 1) * b + t)
                    for c in range(NC):
                        dst = bank[4 + c][:, t * P:(t + 1) * P]
                        last = mmul(dst, xdt[:, t, c * P:(c + 1) * P], mix[:, t], start=True, stop=t == 0)
                        if t > 0:
                            last = mmul(dst, hst[:, t - 1, c * P:(c + 1) * P], ct[0:64, t, 3], start=False, stop=True)
                    return last

                decays(0)
                decays(1)
                for t in range(NT):
                    last = mmul(bank[7][:, t * DS:(t + 1) * DS], suf[:], dta[:, t, 0:DS], start=True, stop=True) \
                        if t < 2 else None
                for t in range(2, NT):
                    pe.wait_ge(dta_ready, NT * b + (t + 1))
                    last = mmul(bank[7][:, t * DS:(t + 1) * DS], suf[:], dta[:, t, 0:DS], start=True, stop=True)
                last.then_inc(gsuf_ready, 1)
                pe.wait_ge(b_ready, b + 1)
                pe.wait_ge(c_ready, b + 1)
                levels(0)
                decays(2)
                levels(1)
                carry(0)
                outputs(0)
                decays(3)
                levels(2)
                carry(1)
                outputs(1)
                levels(3)
                carry(2)
                outputs(2)
                outputs(3).then_inc(y_ready, 1)
                pe.wait_ge(yg_ready, 2 * b + NC)
                for t in range(NT):
                    for c in range(NC):
                        last = mmul(bank[7][:, t * P:(t + 1) * P], yg[:, c, t * P:(t + 1) * P], w_out[:, c],
                                    start=c == 0, stop=c == NC - 1)
                last.then_inc(outA_ready, 1)

                turn(b, 1, 0)
                for k in range(TAPS):
                    last = mmul(bank[1][:, 0:COMP], cconv[:, k], turned[:, KEEP + k:KEEP + CTX:TAPS],
                                start=k == 0, stop=k == TAPS - 1)
                last.then_inc(comp_ps, 1)
                pe.wait_ge(comp_sb, b + 1)
                for t, lo in enumerate((COMP, P + COMP, KEEP + CTX, KEEP + P + CTX)):
                    last = nc.tensor.transpose(bank[2][:, t * P:(t + 1) * P], turned[:, lo:lo + P], ident[:])
                last.then_inc(back_ps, 1)

                pe.wait_ge(ctx_ready, b + 1)
                mmul(bank[6][:, 0:CTX], c_k[:], ctx4[:, 0], start=True, stop=True).then_inc(ckv_ps, 1)
                mmul(bank[7][:, 0:D], ctx4[:].rearrange("p a k -> p (a k)"), c_v[:], start=True, stop=True).then_inc(ckv_ps, 1)

                pe.wait_ge(xq_ready, b + 1)
                for t in range(NT):
                    last = nc.tensor.transpose(bank[0][:].bitcast(BF16)[:, t * P:(t + 1) * P], xq[:, t], identb[:])
                last.then_inc(xT_ps[1], 1)
                pe.wait_ge(xT_sb[1], b + 1)
                for t in range(NT):
                    if t >= 2:
                        pe.wait_ge(hid_ready, NT * b + (t - 1))
                    mmul(bank[2 + 2 * (t % 2)][:], xqT[:, t * P:(t + 1) * P], wgq[:], start=True, stop=True)
                    mmul(bank[3 + 2 * (t % 2)][:], xqT[:, t * P:(t + 1) * P], wuq[:], start=True, stop=True).then_inc(gu_ps, 1)
                pe.wait_ge(kv_blk, 2 * b + 2)
                for t in range(NT):
                    pe.wait_ge(hq_ready, NT * b + (t + 1))
                    if t >= 2:
                        pe.wait_ge(hT_sb, NT * b + (t - 1))
                    for c in range(FC):
                        last = nc.tensor.transpose(bank[6 + t % 2][:].bitcast(BF16)[:, c * P:(c + 1) * P],
                                                   hq[:, t, c * P:(c + 1) * P], identb[:])
                    last.then_inc(hT_ps, 1)
                for t in range(NT):
                    pe.wait_ge(hT_sb, NT * b + (t + 1))
                    for c in range(FC):
                        last = mmul(bank[0][:, t * P:(t + 1) * P], hqT[:, t, c], wdq[:, c],
                                    start=c == 0, stop=c == FC - 1)
                last.then_inc(down_ps, 1)

                turn(b, 3, 0)
                mmul(bank[1][:], w_k[:], turned[:, 0:T], start=True, stop=True).then_inc(kq_ps, 1)
                mmul(bank[2][:], w_q[:], turned[:, 0:T], start=True, stop=True).then_inc(kq_ps, 1)
                for t in range(NT):
                    last = mmul(bank[3][:, t * P:(t + 1) * P], turned[:, t * P:(t + 1) * P], w_v[:],
                                start=True, stop=True)
                last.then_inc(v_ps, 1)
                pe.wait_ge(v_sb, b + 1)
                pe.wait_ge(stacked, 16 * 2 * 2 * PARTS * b + (16 * 2 * 2 * PARTS))

                def at(h):
                    return slice(64 * (h % 2), 64 * (h % 2) + PARTS * HD)

                def scores(h):
                    for j, tts in enumerate(((3,), (2, 0), (1,))):
                        n = 3 * h + j
                        if n >= 2:
                            pe.wait_ge(s_max, 3 * H * b + (n - 1))
                        for i, t in enumerate(tts):
                            lo, w = 384 * i, (t + 1) * P
                            dst = bank[6 + n % 2]
                            mmul(dst[:, lo:lo + w], stack[1][at(h), h // 2, t * P:(t + 1) * P],
                                 stack[0][at(h), h // 2, 0:w], start=True, stop=False)
                            last = mmul(dst[:, lo + w - P:lo + w], identb[:], tri_q[:], start=False, stop=True)
                        last.then_inc(s_ps, 1)

                def maxima(hg):
                    pe.wait_ge(mp_ready, 2 * b + (hg + 1))
                    for t in range(NT):
                        last = nc.tensor.transpose(bank[3][0:3 * HG].bitcast(BF16)[:, t * P:(t + 1) * P],
                                                   sparts[:, hg, t].rearrange("p a h -> p (a h)"), identb[:])
                    last.then_inc(mT_ps, 1)

                def turned_scores(h):
                    if h % HG == 0:
                        pe.wait_ge(mT_sb, 2 * b + (h // HG + 1))
                    for j, tts in enumerate(((0,), (1, 3), (2,))):
                        n = 3 * h + j
                        if n >= 2:
                            pe.wait_ge(prob_ready, 3 * H * b + (n - 1))
                        dst = bank[4 + n % 2]
                        for i, t in enumerate(tts):
                            lo, w = 384 * i, T - t * P
                            mmul(dst[:, lo:lo + w], stack[0][at(h), h // 2, t * P:(t + 1) * P],
                                 stack[1][at(h), h // 2, t * P:T], start=True, stop=False)
                            mmul(dst[:, lo:lo + w], pick[:, h % HG], mT[:, h // HG, t * P:T], start=False, stop=False)
                            last = mmul(dst[:, lo:lo + P], identb[:], tri_k[:], start=False, stop=True)
                        last.then_inc(st_ps, 1)

                def weigh(h):
                    dst = bank[1 + h // HG]
                    for j, tts in enumerate(((0,), (1, 3), (2,))):
                        pe.wait_ge(prob_ready, 3 * H * b + (3 * h + j + 1))
                        for i, t in enumerate(tts):
                            last = mmul(dst[:, t * P:T], vpad[:, t, h], prob[:, h % 2, j, 384 * i:384 * i + T - t * P],
                                        start=h % HG == 0 and t == 0, stop=h % HG == HG - 1 and t == 2)
                    last.then_inc(pv_done, 1)

                for h in range(HG):
                    scores(h)
                maxima(0)
                for h in range(H):
                    turned_scores(h)
                    if h < HG:
                        scores(HG + h)
                    if h > 0:
                        weigh(h - 1)
                    if h == HG - 1:
                        maxima(1)
                weigh(H - 1)
                pe.wait_ge(att_ready, 2 * b + 2)
                for t in range(NT):
                    last = mmul(bank[0][:, t * P:(t + 1) * P], att[:, t * P:(t + 1) * P], w_p[:], start=True, stop=True)
                last.then_inc(proj_ps, 1)

                turn(b, 4, 0)
                mmul(bank[1][:], c_q[:], turned[:, 0:T], start=True, stop=True).then_inc(cq_ps, 1)
                pe.wait_ge(cq_sb, b + 1)

                def cross_scores(t):
                    if t >= 2:
                        pe.wait_ge(cs_kept, NT * b + (t - 1))
                    mmul(bank[2 + t % 2][:], qT[:, t * P:(t + 1) * P], kblk[:].rearrange("p h k -> p (h k)"),
                                  start=True, stop=True).then_inc(cs_ps, 1)

                cross_scores(0)
                cross_scores(1)
                for t in range(NT):
                    pe.wait_ge(cp_ready, NT * b + (t + 1))
                    if t >= 2:
                        pe.wait_ge(cpT_sb, NT * b + (t - 1))
                    for c in range(4):
                        last = nc.tensor.transpose(bank[4 + t % 2][:, c * P:(c + 1) * P], pc[:, t % 2, c], ident[:])
                    last.then_inc(cpT_ps, 1)
                    if t + 2 < NT:
                        cross_scores(t + 2)
                pe.wait_ge(cpT_sb, NT * b + NT)
                for i, w in enumerate((vblk, vmask)):
                    for c in range(4):
                        last = mmul(bank[6 + i][:], w[:, c], pT[:, c], start=c == 0, stop=c == 3)
                last.then_inc(co_ps, 1)
                pe.wait_ge(co_ready, b + 1)
                for t in range(NT):
                    last = mmul(bank[0][:, t * P:(t + 1) * P], att[:, t * P:(t + 1) * P], c_o[:], start=True, stop=True)
                last.then_inc(cproj_ps, 1)

                turn(b, 5, 0)
                for t in range(NT):
                    last = mmul(bank[1][:, t * NE:(t + 1) * NE], turned[:, t * P:(t + 1) * P], wgate[:],
                                start=True, stop=True)
                last.then_inc(gate_ps, 1)

                def expand(e, c):
                    n = e * FC + c
                    if n >= FC:
                        pe.wait_ge(h_act, SLICES * FC * b + (n - FC + 1))
                    mmul(bank[2 + c][:], w1[:, e, c * P:(c + 1) * P], turned[:, 0:T], start=True, stop=True).then_inc(h_ps, 1)

                for c in range(FC):
                    expand(0, c)
                for e in range(SLICES):
                    pe.wait_ge(h_act, SLICES * FC * b + ((e + 1) * FC))
                    if e >= 2:
                        pe.wait_ge(e_added, SLICES * b + (e - 1))
                    for t in range(NT):
                        if e + 1 < SLICES:
                            expand(e + 1, t)
                        for c in range(FC):
                            last = mmul(bank[6 + e % 2][:, t * P:(t + 1) * P], act_h[:, e % 2, c, t * P:(t + 1) * P],
                                        w2[:, e, c], start=c == 0, stop=c == FC - 1)
                    last.then_inc(e_ps, 1)


def diagonal(vpad, t, hg):
    flat = vpad[:, t, hg * HG:(hg + 1) * HG].rearrange("p h c -> p (h c)")
    return bass.AP(tensor=flat.tensor, offset=flat.offset, ap=[list(flat.ap[0]), [P + HD, HG], [1, HD]])


def shape_constants():
    bf = np.dtype("bfloat16")
    f = np.float32
    j = np.arange(P)[:, None]
    t = np.arange(P)[None, :]

    def between(half):
        mid = t // (2 * half) * (2 * half) + half
        return np.where(t >= mid, (j >= mid) & (j <= t), (j > t) & (j < mid)).astype(f)

    def pairs(half):
        same = j // (2 * half) == t // (2 * half)
        return (same & (j % (2 * half) < half) & (t % (2 * half) >= half)).astype(f)

    eye = np.eye(P, dtype=f)
    head = np.arange(P) // HD
    pick = np.zeros((3 * HG, HG, P), f)
    for r in range(3 * HG):
        pick[r, r % HG] = -1.0
    vm = (4 * np.arange(4)[None, :, None] + (np.arange(P) // CTX)[:, None, None] == head[None, None, :]).astype(f)
    e = np.arange(NE)
    return {
        "lev_a": np.stack([between(h) for h in LEVELS_A] + [(j <= t).astype(f)], 1),
        "lev_b": np.stack([between(h) for h in LEVELS_B], 1),
        "suf": (j > t).astype(f),
        "lmask": np.stack([pairs(h) for h in LEVELS_A] + [eye] + [pairs(h) for h in LEVELS_B], 1).astype(bf),
        "ident": eye, "identb": eye.astype(bf), "ones": np.ones((P, P), f),
        "tri_q": np.where(t > j, NEG, 0.0).astype(bf), "tri_k": np.where(j > t, NEG, 0.0).astype(bf),
        "pick": pick.astype(bf),
        "hmask": (head[:, None] == np.arange(H)[None, :]).astype(f),
        "vmask": vm,
        "before": np.broadcast_to((e[None, :] < e[:, None]).astype(f).reshape(1, NE * NE), (P, NE * NE)),
    }


def kernel(**x):
    import concourse.bacc as bacc
    from concourse.bass_utils import run_bass_kernel_spmd

    x = {k: np.asarray(v) for k, v in x.items()}

    def chunks(w):
        return w.reshape(-1, P, w.shape[-1]).transpose(1, 0, 2)

    wx = x["L0_attn_W_x"].T
    wb, wc, wdt = wx[:, :DS], wx[:, DS:2 * DS], wx[:, 2 * DS:]
    perm = np.arange(D).reshape(NPAIR, 2, HD).transpose(1, 2, 0).reshape(-1)
    w1 = np.concatenate([x["L1_ffn_shared_w1"][None], x["L1_ffn_experts_w1"]])
    w2 = np.concatenate([x["L1_ffn_shared_w2"][None], x["L1_ffn_experts_w2"]])
    arrays = {
        "xT": x["x"].transpose(2, 0, 1),
        "xtok": x["x"].reshape(B, NT, P, D).transpose(0, 2, 1, 3),
        "ctxT": x["ctx_1024"].transpose(2, 0, 1),
        "w_in": x["L0_attn_W_in"].T,
        "conv_w": chunks(x["L0_attn_conv_w"].reshape(DI, TAPS)),
        "chan": chunks(np.stack([x["L0_attn_conv_b"], x["L0_attn_D"]], 1)),
        "w_bb": chunks(np.concatenate([wb, wb], 1)),
        "w_cc": chunks(np.concatenate([wc, wc], 1)),
        "w_bdt": chunks(np.concatenate([wb, wdt], 1)),
        "alog": np.broadcast_to(np.concatenate([x["L0_attn_A_log"]] * 2), (P, 2 * DS)),
        "w_out": chunks(x["L0_attn_W_out"].T),
        "cconv": x["L0_xattn_conv_w"].transpose(1, 0, 2),
        "cols": np.stack([x["L0_xattn_conv_b"], x["L1_xattn_bq"], x["L1_xattn_bk"]], 1),
        "wg": x["L0_ffn_w_gate"].T, "wu": x["L0_ffn_w_up"].T, "wd": chunks(x["L0_ffn_w_down"].T),
        "w_q": x["L1_attn_W_query"].T[:, perm], "w_k": x["L1_attn_W_key"].T[:, perm],
        "w_v": x["L1_attn_W_value"].T, "w_p": x["L1_attn_W_proj"].T,
        "c_q": x["L1_xattn_wq"].T, "c_k": x["L1_xattn_wk"].T, "c_v": x["L1_xattn_wv"].T, "c_o": x["L1_xattn_wo"].T,
        "rows": np.broadcast_to(np.stack([x["L1_xattn_bv"], x["L1_xattn_bo"]])[None], (P, 2, D)),
        "mask": x["mask_1x1xSxS2_if1"].reshape(NT, P, CTX).transpose(1, 0, 2),
        "w1": w1.transpose(2, 0, 1),
        "w2": w2.transpose(2, 0, 1).reshape(FC, P, SLICES, D).transpose(1, 2, 0, 3),
        "wgate": x["L1_ffn_gate_w"].T,
    }
    arrays.update(shape_constants())
    nc = bacc.Bacc("TRN2", target_bir_lowering=False, num_devices=1)
    given, aps = {}, {}
    for name, v in arrays.items():
        v = np.ascontiguousarray(v)
        given["in_" + name] = v
        aps[name] = nc.dram_tensor("in_" + name, v.shape, mybir.dt.from_np(v.dtype), kind="ExternalInput").ap()
    out = nc.dram_tensor("out_0", (B, P, NT, D), F32, kind="ExternalOutput").ap()
    decoder(nc, aps, out)
    r = run_bass_kernel_spmd(nc, [given], core_ids=[0])
    return r.results[0]["out_0"].transpose(0, 2, 1, 3).reshape(B, T, D)
```

```python
from contextlib import ExitStack

import numpy as np
import concourse.bass as bass
from concourse import mybir

ALU = mybir.AluOpType
ACT = mybir.ActivationFunctionType
AX = mybir.AxisListType
F32 = mybir.dt.float32
BF16 = mybir.dt.bfloat16
I32 = mybir.dt.int32

B, T, D = 4, 512, 128
P = 128
NT = T // P
DI = 2 * D
NC = DI // P
DS = 64
TAPS = 4
NLEV = 8
CTX = 32
COMP = 8
KEEP = 256
FF = 512
FC = FF // P
H, HD = 16, 8
NPAIR = H // 2
HG = 8
PARTS = 6
NE = 8
SLICES = NE + 1
EPS = 1e-5
MAGIC = 1.5 * 2.0 ** 23
NEG = -1e30
PRODUCTS = [(0, 0), (0, 1), (1, 0), (0, 2), (2, 0), (1, 1)]
LEVELS_A = [64, 16, 4]
LEVELS_B = [32, 8, 2, 1]
SCORE_SCALE = (1.0 / D) * HD ** -0.5
FRONT_LINKS = 42
BACK_LINKS = 27
E_SLOTS = 12
SLOTS = E_SLOTS + SLICES * FC
FRONT_AT = [0, 2, 4, 5, 6, 8, 9, 10, 11, 12, 14, 15, 17, 20, 22, 24, 29, 31, 33, 34, 36, 38, 40, 44, 46]
CROSS_SCALE = HD ** -0.5
PROJ_SCALE = 1.0 / D


def decoder(nc, a, out):
    with ExitStack() as ctx:
        def sb(name, shape, dt=F32):
            return ctx.enter_context(nc.sbuf_tensor(name, shape, dt))

        def sem(name):
            return ctx.enter_context(nc.semaphore(name))

        names = {}

        def resident(name, dt=F32):
            names[name] = sb("s_" + name, list(a[name].shape), dt)
            return names[name]

        def share(name, size):
            region = sb(name, [P, size])

            def view(at, shape, dt=F32):
                n = int(np.prod(shape)) // (1 if dt == F32 else 2)
                flat = region[:, at:at + n]
                if dt != F32:
                    flat = flat.bitcast(dt)
                dims = [f"d{i}" for i in range(len(shape))]
                if len(shape) == 1:
                    return flat
                return flat.rearrange(f"p ({' '.join(dims)}) -> p {' '.join(dims)}",
                                      **{d: v for d, v in zip(dims[1:], shape[1:])})

            return view

        one = share("region1", 5120)
        two = share("region2", 3072)
        three = share("region3", 4096)
        four = share("region4", 3584)

        xT = sb("xT", [P, T])
        xtok = sb("xtok", [P, NT, D])
        ctxT = resident("ctxT")
        w_in = resident("w_in")
        conv_w = resident("conv_w")
        chan = resident("chan")
        w_bb = resident("w_bb")
        w_cc = resident("w_cc")
        w_bdt = resident("w_bdt")
        alog = resident("alog")
        w_out = resident("w_out")
        lev_a = resident("lev_a")
        lev_b = resident("lev_b")
        suf = resident("suf")
        lmask = resident("lmask", BF16)
        ident = resident("ident")
        identb = resident("identb", BF16)
        ones = resident("ones")
        cconv = resident("cconv")
        cols = resident("cols")
        wg = names["wg"] = one(0, [FF])
        wu = names["wu"] = one(512, [FF])
        wd = names["wd"] = one(1024, [FC, D])
        w_q = resident("w_q")
        w_k = resident("w_k")
        w_v = resident("w_v")
        w_p = resident("w_p")
        tri_q = resident("tri_q", BF16)
        tri_k = resident("tri_k", BF16)
        pick = resident("pick", BF16)
        c_q = resident("c_q")
        c_k = resident("c_k")
        c_v = resident("c_v")
        c_o = resident("c_o")
        rows = resident("rows")
        hmask = resident("hmask")
        vmask = resident("vmask")
        mask = resident("mask", I32)
        experts = sb("experts", [P, 3, 2 * FF])
        wgate = resident("wgate")
        before = resident("before")

        neg_a = sb("neg_a", [P, 2 * DS])
        minus_half = sb("minus_half", [P, NT])
        wgq, wuq = sb("wgq", [P, FF], BF16), sb("wuq", [P, FF], BF16)
        wdq = sb("wdq", [P, FC, D], BF16)
        wabs = sb("wabs", [P, 3])
        wscale = sb("wscale", [P, 3])
        winv = sb("winv", [P, 3])
        wtmp = one(1536, [FF])
        mkeep = sb("mkeep", [P, NT, CTX])
        mfill = sb("mfill", [P, NT, CTX])
        vpad = sb("vpad", [P, NT, H, P])

        xin = sb("xin", [P, NC, TAPS - 1 + T])
        cacc = two(0, [NC, T])
        xc = sb("xc", [P, NC, T])
        zs = sb("zs", [P, NC, T])
        bs = sb("bs", [P, T])
        cs = sb("cs", [P, T])
        dts = sb("dts", [P, 4, NT])
        dta = sb("dta", [P, NT, P])
        xdt = two(0, [NT, DI])
        esuf = sb("esuf", [P, NT, DS])
        bsuf = sb("bsuf", [P, NT, DS])
        btok = sb("btok", [P, NT, DS + 1])
        dec = one(0, [NT, 4, P])
        last_dec = sb("last_dec", [DS, NT])
        bt = one(2048, [NT, 4, P])
        mm = one(4096, [NLEV, P])
        mix = two(1024, [NT, P])
        hst = sb("hst", [DS, NT - 1, DI])
        ya = two(1536, [NC, T])

        res = sb("res", [P, NT, D])
        res_b = sb("res_b", [P, NT, D])
        rows_a, rows_c = sb("rows_a", [P, NT, D]), sb("rows_c", [P, NT, D])
        xs = [rows_a, two(2560, [NT, D]), rows_a, rows_c, rows_c, rows_c]
        stats = [sb(f"stats{h}", [P, NT, 6]) for h in range(2)]
        mv = [sb(f"mv{h}", [P, NT, 2]) for h in range(2)]
        var = [sb(f"var{h}", [P, NT]) for h in range(2)]
        rstd = [sb(f"rstd{h}", [P, NT]) for h in range(2)]
        turned = sb("turned", [P, T + CTX])
        turned_b = sb("turned_b", [P, T])

        amax = sb("amax", [P, NT])
        ainv = sb("ainv", [P, NT])
        xqf = two(0, [NT, D])
        xq = sb("xq", [P, NT, D], BF16)
        xqT = sb("xqT", [P, T], BF16)
        gsc = sb("gsc", [P, NT, 2])
        hid = one(0, [NT, FF])
        gact = one(2048, [2, FF])
        hq = one(3072, [NT, FF], BF16)
        hqT = one(4096, [NT, FC, P], BF16)
        hmax = sb("hmax", [P, NT])
        hinv = sb("hinv", [P, NT])
        dsc = sb("dsc", [P, NT])

        part = [[two(256 * (3 * s + i), [T], BF16) for i in range(3)] for s in range(2)]
        rest = [two(1536 + 512 * s, [T]) for s in range(2)]
        stack = [sb(f"stack{s}", [P, NPAIR, T], BF16) for s in "kq"]
        smax = sb("smax", [P, 2, NT, HG])
        srest = sb("srest", [P, 2, NT, HG])
        sparts = sb("sparts", [P, 2, NT, 3, HG], BF16)
        mT = sb("mT", [3 * HG, 2, T], BF16)
        prob = three(0, [2, 3, T])
        rden = four(2048, [T])
        att = sb("att", [P, T])

        ctx4 = sb("ctx4", [P, 4, CTX])
        kcol = sb("kcol", [P, CTX])
        kblk = sb("kblk", [P, H, CTX])
        vrow = sb("vrow", [P, D])
        vblk = sb("vblk", [P, 4, D])
        qT = four(2560, [T])
        x4b = four(3072, [NT, D])
        s1 = three(0, [2, H, CTX])
        cmax = sb("cmax", [P, 2, H])
        pc = three(1024, [2, 4, P])
        pT = four(0, [4, T])

        glog = sb("glog", [P, NT, NE])
        gge = four(512, [NT, NE, NE])
        ggt = four(768, [NT, NE, NE])
        rank = sb("rank", [P, NT, NE])
        gtop = sb("gtop", [P, NT])
        gexp = sb("gexp", [P, NT, NE])
        gsum = sb("gsum", [P, NT])
        gates = sb("gates", [P, NT, NE])
        act_h = three(0, [2, FC, T])
        moe = four(0, [NT, D])

        bank = [ctx.enter_context(nc.psum_tensor(f"bank{i}", [P, 512], F32)) for i in range(8)]

        def tiles(t, n=P):
            return t.rearrange("p (a n) -> p a n", n=n)

        loaded = {n: sem("ld_" + n) for n in ("w_in", "conv_w", "chan", "w_bb", "w_cc", "w_bdt", "alog", "lev_a",
                                              "lev_b", "suf", "ident", "lmask", "w_out", "ctxT", "ones", "cconv",
                                              "cols", "wg", "wu", "wd", "identb")}
        loaded_late = sem("loaded_late")
        early = sem("early")
        pool_early = sem("pool_early")
        act_early = sem("act_early")
        pe_early = sem("pe_early")
        pool_passed = sem("pool_passed")
        dve_passed = sem("dve_passed")
        front_link = sem("front_link")
        back_link = sem("back_link")
        act_link = sem("act_link")
        xz_ready = sem("xz_ready")
        xin_ready = sem("xin_ready")
        conv_done = sem("conv_done")
        z_act = sem("z_act")
        xc_ready = sem("xc_ready")
        bc_ready = sem("bc_ready")
        btok_ready = sem("btok_ready")
        xcT_ready = sem("xcT_ready")
        b_ready = sem("b_ready")
        c_ready = sem("c_ready")
        ln_dt = sem("ln_dt")
        dt_ready = sem("dt_ready")
        dta_ready = sem("dta_ready")
        xdt_ready = sem("xdt_ready")
        gsuf_ready = sem("gsuf_ready")
        esuf_ready = sem("esuf_ready")
        bsuf_ready = sem("bsuf_ready")
        gdec_ready = sem("gdec_ready")
        dec_ready = sem("dec_ready")
        ct_ready = sem("ct_ready")
        bt_ready = sem("bt_ready")
        lev_ready = sem("lev_ready")
        masked = sem("masked")
        mix_ready = sem("mix_ready")
        hp_ready = sem("hp_ready")
        h_ready = sem("h_ready")
        y_ready = sem("y_ready")
        ya_ready = sem("ya_ready")
        yg_ready = sem("yg_ready")
        outA_ready = sem("outA_ready")
        var_ready = [sem(f"var{h}_ready") for h in range(2)]
        rstd_ready = [sem(f"rstd{h}_ready") for h in range(2)]
        x_ready = [sem(f"x{k}_ready") for k in range(1, 7)]
        xT_ps = [sem(f"x{k}T_ps") for k in range(1, 6)]
        xT_sb = [sem(f"x{k}T_sb") for k in range(1, 6)]
        comp_ps = sem("comp_ps")
        comp_sb = sem("comp_sb")
        back_ps = sem("back_ps")
        gsc_ready = sem("gsc_ready")
        gu_ps = sem("gu_ps")
        g_act = sem("g_act")
        hid_ready = sem("hid_ready")
        xq_ready = sem("xq_ready")
        hq_ready = sem("hq_ready")
        hq_magic = sem("hq_magic")
        hT_ps = sem("hT_ps")
        hT_sb = sem("hT_sb")
        down_ps = sem("down_ps")
        kq_ps = sem("kq_ps")
        v_ps = sem("v_ps")
        v_sb = sem("v_sb")
        part0 = sem("part0")
        rest0 = sem("rest0")
        part1 = sem("part1")
        part2 = sem("part2")
        stacked = sem("stacked")
        s_ps = sem("s_ps")
        s_max = sem("s_max")
        mp_ready = sem("mp_ready")
        mT_ps = sem("mT_ps")
        mT_sb = sem("mT_sb")
        st_ps = sem("st_ps")
        prob_ready = sem("prob_ready")
        pv_done = sem("pv_done")
        att_ready = sem("att_ready")
        proj_ps = sem("proj_ps")
        ctx_ready = sem("ctx_ready")
        ckv_ps = sem("ckv_ps")
        kcol_ready = sem("kcol_ready")
        kv_blk = sem("kv_blk")
        cq_ps = sem("cq_ps")
        cq_sb = sem("cq_sb")
        x4b_ready = sem("x4b_ready")
        cs_ps = sem("cs_ps")
        cs_kept = sem("cs_kept")
        cs_full = sem("cs_full")
        cs_max = sem("cs_max")
        cs_sub = sem("cs_sub")
        cp_ready = sem("cp_ready")
        cpT_ps = sem("cpT_ps")
        cpT_sb = sem("cpT_sb")
        co_ps = sem("co_ps")
        co_ready = sem("co_ready")
        cproj_ps = sem("cproj_ps")
        gate_ps = sem("gate_ps")
        glog_ready = sem("glog_ready")
        gsub_ready = sem("gsub_ready")
        gexp_ready = sem("gexp_ready")
        h_ps = sem("h_ps")
        h_act = sem("h_act")
        e_ps = sem("e_ps")
        e_added = sem("e_added")
        x_loaded = sem("x_loaded")
        tok_loaded = sem("tok_loaded")
        e_loaded = [sem(f"e_loaded{n}") for n in range(3)]
        stored = sem("stored")

        block = ctx.enter_context(nc.Block())

        order = ["w_in", "conv_w", "chan", "w_bb", "w_cc", "w_bdt", "alog", "lev_a", "lev_b", "suf", "ident",
                 "lmask", "w_out", "ctxT", "ones", "cconv", "cols", "wg", "wu", "wd", "identb", "w_q", "w_k",
                 "w_v", "w_p", "tri_q", "tri_k", "pick", "c_q", "c_k", "c_v", "c_o", "rows", "hmask", "vmask", "mask",
                 "wgate", "before"]
        late = order[order.index("w_q"):]
        assert sorted(order + ["xT", "xtok", "w12"]) == sorted(a)

        def arrived(engine, *which):
            for n in which:
                engine.wait_ge(loaded[n], 16)

        def halves(engine, attention, back, front):
            for n in range(len(FRONT_AT)):
                front(0, n)
            with engine.Fori(0, B - 1) as b:
                attention(b)
                for slot in range(SLOTS):
                    back(b, slot)
                    for n, at in enumerate(FRONT_AT):
                        if at == slot:
                            front(b + 1, n)
            attention(B - 1)
            for slot in range(SLOTS):
                back(B - 1, slot)

        @block.sync
        def _(sp):
            sp.dma_start(xT[:], a["xT"][0]).then_inc(x_loaded, 16)
            sp.dma_start(xtok[:], a["xtok"][0]).then_inc(tok_loaded, 16)
            for n in order:
                sp.dma_start(names[n][:], a[n]).then_inc(loaded_late if n in late else loaded[n], 16)
            for e in range(3):
                sp.dma_start(experts[:, e], a["w12"][e]).then_inc(e_loaded[e], 16)

            def attention(b):
                pass

            def front(i, n):
                if n == len(FRONT_AT) - 1:
                    sp.wait_ge(part0, 2 * i + 2)
                    sp.wait_ge(part1, 2 * i + 2)
                    sp.wait_ge(part2, 2 * i + 2)
                    for g, which in enumerate(PRODUCTS):
                        for par in range(2):
                            base = 64 * par + HD * g
                            sp.dma_start(stack[0][base:base + HD, :, :],
                                         part[0][which[0]][64 * par:64 * par + 64, :]).then_inc(stacked, 16)

            def back(b, slot):
                if slot == 0 and not isinstance(b, int):
                    sp.dma_start(xT[:], a["xT"][b + 1]).then_inc(x_loaded, 16)
                    sp.dma_start(xtok[:], a["xtok"][b + 1]).then_inc(tok_loaded, 16)
                e, sub = divmod(slot - E_SLOTS, FC)
                if slot >= E_SLOTS and sub == FC - 1:
                    last = isinstance(b, int)
                    if not last or e + 3 < SLICES:
                        sp.wait_ge(e_ps, SLICES * b + (e + 1))
                        sp.dma_start(experts[:, e % 3], a["w12"][(e + 3) % SLICES]).then_inc(e_loaded[e % 3], 16)
                if slot == SLOTS - 1:
                    sp.wait_ge(x_ready[5], NT * b + NT)
                    sp.dma_start(out[b], xs[5][:]).then_inc(stored, 16)

            halves(sp, attention, back, front)
            sp.wait_ge(stored, 16 * (B + 1))

        @block.gpsimd
        def _(pool):
            pool.memset(minus_half[:], -0.5).then_inc(pool_early, 1)
            pool.memset(xin[:, :, 0:TAPS - 1], 0.0).then_inc(pool_early, 1)
            pool.memset(vpad[:], 0.0).then_inc(pool_early, 1)
            pool.wait_ge(pool_early, 3)
            for h in range(H):
                lo = 64 + HD * (h % HG)
                pool.memset(vpad[:, :, h, lo:lo + HD], 1.0).then_inc(pool_early, 1)
            pool.memset(sparts[:], 0.0).then_inc(stored, 16)
            pool.wait_ge(stored, 16)

            def rstd_of(half, pass_, k):
                pool.wait_ge(var_ready[half], 3 * pass_ + k)
                pool.tensor_tensor(rstd[half][:], var[half][:], minus_half[:], ALU.pow).then_inc(rstd_ready[half], 1)

            def attention(b):
                rstd_of(1, b, 1)

            def front(i, n):
                if n in (4, 5):
                    if n == 4:
                        pool.wait_ge(b_ready, i + 1)
                    for t in (2 * (n - 4), 2 * (n - 4) + 1):
                        pool.wait_ge(dec_ready, NT * i + (t + 1))
                        pool.tensor_tensor(bt[:, t], dec[:, t],
                                           bs[:, None, t * P:(t + 1) * P].broadcast_to([P, 4, P]),
                                           ALU.mult).then_inc(bt_ready, 1)
                if n in (8, 9, 10, 11):
                    t = n - 8
                    if t == 0:
                        pool.wait_ge(z_act, 2 * i + 2)
                    pool.wait_ge(ya_ready, NT * i + (t + 1))
                    pool.tensor_tensor(ya[:, :, t * P:(t + 1) * P], ya[:, :, t * P:(t + 1) * P],
                                       zs[:, :, t * P:(t + 1) * P], ALU.mult).then_inc(yg_ready, 1)
                if n == 12:
                    rstd_of(0, i, 1)
                if n == 15:
                    rstd_of(0, i, 2)
                if 17 <= n < 20:
                    for t in ((0, 1), (2,), (3,))[n - 17]:
                        pool.wait_ge(hq_magic, NT * i + (t + 1))
                        pool.sem_inc(pool_passed)
                        pool.tensor_scalar(hq[:, t], hid[:, t], MAGIC, None, ALU.subtract).then_inc(hq_ready, 1)
                if n == 22:
                    rstd_of(0, i, 3)
                if n == 24:
                    for s in range(2):
                        pool.wait_ge(rest0, 2 * i + (s + 1))
                        pool.sem_inc(pool_passed)
                        pool.tensor_copy(part[s][1][:], rest[s][:]).then_inc(part1, 1)
                        pool.wait_ge(part1, 2 * i + (s + 1))
                        pool.tensor_tensor(part[s][2][:], rest[s][:], part[s][1][:], ALU.subtract).then_inc(part2, 1)

            def back(b, slot):
                if slot == 1:
                    pool.wait_ge(x_ready[3], NT * b + NT)
                    pool.tensor_tensor(x4b[:], xs[3][:], rows[:, None, 1].broadcast_to([P, NT, D]),
                                       ALU.add).then_inc(x4b_ready, 1)
                if 3 <= slot < 7:
                    t = slot - 3
                    pool.wait_ge(cs_kept, NT * b + (t + 1))
                    pool.tensor_tensor(s1[:, t % 2], s1[:, t % 2], mfill[:, None, t].broadcast_to([P, H, CTX]),
                                       ALU.add).then_inc(cs_full, 1)
                    pool.wait_ge(cs_max, NT * b + (t + 1))
                    pool.tensor_tensor(s1[:, t % 2], s1[:, t % 2], cmax[:, t % 2, :, None].broadcast_to([P, H, CTX]),
                                       ALU.subtract).then_inc(cs_sub, 1)
                if slot == 9:
                    rstd_of(1, b, 2)
                if slot == SLOTS - 1:
                    rstd_of(1, b, 3)

            halves(pool, attention, back, front)

        @block.scalar
        def _(act):
            def do(out_, in_, func, **kw):
                return nc.scalar.activation(out_, in_, func, **kw)

            arrived(act, "alog")
            do(neg_a[:], alog[:], ACT.Exp).then_inc(act_early, 1)
            arrived(act, "cols", "ctxT")
            act.wait_ge(pool_early, 2)

            def attention(b):
                for hg in range(2):
                    act.wait_ge(mT_ps, 2 * b + (hg + 1))
                    do(mT[:, hg], bank[3][0:3 * HG].bitcast(BF16)[:, 0:T], ACT.Copy).then_inc(mT_sb, 1)
                    for h in range(hg * HG, (hg + 1) * HG):
                        if h >= 2:
                            act.wait_ge(pv_done, H * b + (h - 1))
                        for j, n in enumerate((512, 512, 256)):
                            act.wait_ge(st_ps, 3 * H * b + (3 * h + j + 1))
                            do(prob[:, h % 2, j, 0:n], bank[4 + (3 * h + j) % 2][:, 0:n], ACT.Exp,
                               scale=SCORE_SCALE).then_inc(prob_ready, 1)

            def front(i, n):
                if n == 0:
                    for c in range(NC):
                        act.wait_ge(xz_ready, 4 * i + (c + 1))
                        do(xin[:, c, TAPS - 1:], bank[c][:], ACT.Copy).then_inc(xin_ready, 1)
                    for c in range(NC):
                        act.wait_ge(xz_ready, 4 * i + (NC + c + 1))
                        do(zs[:, c], bank[NC + c][:], ACT.Silu).then_inc(z_act, 1)
                    for c in range(NC):
                        act.wait_ge(conv_done, 2 * i + (c + 1))
                        do(xc[:, c], cacc[:, c], ACT.Silu).then_inc(xc_ready, 1)
                if n == 1:
                    act.wait_ge(bc_ready, 3 * i + 1)
                    do(bs[:], bank[0][:], ACT.Copy).then_inc(b_ready, 1)
                if n == 2:
                    act.wait_ge(btok_ready, i + 1)
                    do(dts[:, 0], btok[:, :, DS], ACT.Abs).then_inc(act_link, 1)
                    act.wait_ge(act_link, 3 * i + 1)
                    do(dts[:, 1], dts[:, 0], ACT.Exp, scale=-1.0).then_inc(act_link, 1)
                    act.wait_ge(act_link, 3 * i + 2)
                    do(dts[:, 2], dts[:, 1], ACT.Ln, bias=1.0).then_inc(ln_dt, 1)
                if n == 3:
                    act.wait_ge(dt_ready, i + 1)
                    for t in range(NT):
                        act.wait_ge(xcT_ready, 2 * i + (t // 2 + 1))
                        do(xdt[:, t], bank[3 if t < 2 else 0][:, (t % 2) * DI:(t % 2 + 1) * DI], ACT.Copy,
                           scale=dts[:, 3, t:t + 1]).then_inc(xdt_ready, 1)
                if n == 4:
                    for t in range(2):
                        act.wait_ge(gdec_ready, NT * i + (t + 1))
                        do(dec[:, t], tiles(bank[1 + t % 2]), ACT.Exp).then_inc(dec_ready, 1)
                    act.wait_ge(gsuf_ready, i + 1)
                    do(esuf[:], bank[3][:, 0:NT * DS].rearrange("p (n s) -> p n s", s=DS),
                       ACT.Exp).then_inc(esuf_ready, 1)
                if n == 5:
                    for t in range(2, NT):
                        act.wait_ge(gdec_ready, NT * i + (t + 1))
                        do(dec[:, t], tiles(bank[1 + t % 2]), ACT.Exp).then_inc(dec_ready, 1)
                if n == 13:
                    act.wait_ge(xT_ps[0], i + 1)
                    do(turned[:, 0:T], bank[0][:], ACT.Copy).then_inc(xT_sb[0], 1)
                    do(turned[:, T:], ctxT[:, i], ACT.Copy).then_inc(act_link, 1)
                if n == 14:
                    act.wait_ge(comp_ps, i + 1)
                    do(turned[:, KEEP:KEEP + COMP], bank[1][:, 0:COMP], ACT.Identity,
                       bias=cols[:, 0:1]).then_inc(comp_sb, 1)
                    do(ctx4[:], ctxT[:, i, None].broadcast_to([P, 4, CTX]), ACT.Copy).then_inc(ctx_ready, 1)
                if n == 15:
                    act.wait_ge(ckv_ps, 2 * i + 1)
                    do(kcol[:], bank[1][:, 0:CTX], ACT.Identity, bias=cols[:, 2:3]).then_inc(kcol_ready, 1)
                if n == 16:
                    act.wait_ge(xT_ps[1], i + 1)
                    do(xqT[:], bank[0][:].bitcast(BF16)[:, 0:T], ACT.Copy).then_inc(xT_sb[1], 1)
                    act.wait_ge(gsc_ready, i + 1)
                if 17 <= n < 20:
                    for t in ((0, 1), (2,), (3,))[n - 17]:
                        act.wait_ge(gu_ps, NT * i + (t + 1))
                        if t >= 2:
                            act.wait_ge(hid_ready, NT * i + (t - 1))
                        do(gact[:, t % 2], bank[1 if t % 2 == 0 else 3][:], ACT.Silu,
                           scale=gsc[:, t, 0:1]).then_inc(g_act, 1)
                if n in (20, 21):
                    for t in (2 * (n - 20), 2 * (n - 20) + 1):
                        act.wait_ge(hT_ps, NT * i + (t + 1))
                        do(hqT[:, t], bank[1 + t % 2][:].bitcast(BF16)[:, 0:FF].rearrange("p (c n) -> p c n", n=P),
                           ACT.Copy).then_inc(hT_sb, 1)
                if n == 23:
                    act.wait_ge(xT_ps[2], i + 1)
                    do(turned[:, 0:T], bank[0][:], ACT.Copy).then_inc(xT_sb[2], 1)
                if n == 24:
                    for s in range(2):
                        act.wait_ge(kq_ps, 2 * i + (s + 1))
                        do(part[s][0][:], bank[1 + s][:], ACT.Copy).then_inc(part0, 1)
                    act.wait_ge(part0, 2 * i + 2)
                    act.wait_ge(part1, 2 * i + 2)
                    act.wait_ge(part2, 2 * i + 2)
                    for g, which in enumerate(PRODUCTS):
                        for par in range(2):
                            base = 64 * par + HD * g
                            act.dma_start(stack[1][base:base + HD, :, :],
                                          part[1][which[1]][64 * par:64 * par + 64, :]).then_inc(stacked, 16)

            def back(b, slot):
                if slot == 1:
                    act.wait_ge(xT_ps[3], b + 1)
                    do(turned_b[:], bank[5][:], ACT.Copy).then_inc(xT_sb[3], 1)
                if slot == 2:
                    act.wait_ge(cq_ps, b + 1)
                    do(qT[:], bank[6][:], ACT.Identity, bias=cols[:, 1:2]).then_inc(cq_sb, 1)
                if 4 <= slot < 8:
                    t = slot - 4
                    act.wait_ge(cs_sub, NT * b + (t + 1))
                    if t >= 2:
                        act.wait_ge(cpT_ps, NT * b + (t - 1))
                    do(pc[:, t % 2], s1[:, t % 2].rearrange("p h k -> p (h k)").rearrange("p (c n) -> p c n", n=P),
                       ACT.Exp).then_inc(cp_ready, 1)
                    act.wait_ge(cpT_ps, NT * b + (t + 1))
                    do(pT[:, :, t * P:(t + 1) * P], tiles(bank[6 + t % 2]), ACT.Copy).then_inc(cpT_sb, 1)
                if slot == 10:
                    act.wait_ge(xT_ps[4], b + 1)
                    do(turned_b[:], bank[7][:], ACT.Copy).then_inc(xT_sb[4], 1)
                if slot == 11:
                    act.wait_ge(gsub_ready, b + 1)
                    do(gexp[:], glog[:], ACT.Exp).then_inc(gexp_ready, 1)
                    for c in range(2):
                        silu(b, 0, c)
                if slot >= E_SLOTS:
                    e, t = divmod(slot - E_SLOTS, FC)
                    if e == 0 and t == 0:
                        silu(b, 0, 2)
                        silu(b, 0, 3)
                    if e + 1 < SLICES:
                        silu(b, e + 1, t)

            def silu(b, e, c):
                act.wait_ge(h_ps, SLICES * FC * b + (e * FC + c + 1))
                if e >= 2:
                    act.wait_ge(e_ps, SLICES * b + (e - 1))
                do(act_h[:, e % 2, c], bank[4 + c % 2][:], ACT.Silu).then_inc(h_act, 1)

            halves(act, attention, back, front)

        @block.vector
        def _(dve):
            V = nc.vector
            step = [0]

            def link(instruction):
                instruction.then_inc(early, 1)
                step[0] += 1
                dve.wait_ge(early, step[0])

            arrived(dve, "wg", "wu", "wd")
            link(V.tensor_reduce(wabs[:, 0:1], wg[:], AX.X, ALU.add, apply_absolute_value=True))
            link(V.tensor_reduce(wabs[:, 1:2], wu[:], AX.X, ALU.add, apply_absolute_value=True))
            link(V.tensor_reduce(wabs[:, 2:3], wd[:].rearrange("p c n -> p (c n)"), AX.X, ALU.add,
                                 apply_absolute_value=True))
            dve.wait_ge(pe_early, 1)
            link(V.tensor_scalar(wscale[:], bank[7][:, 0:3], 1.0 / (D * FF), 1e-5, ALU.mult, ALU.max))
            link(V.reciprocal(winv[:], wscale[:]))
            for i, (w, q) in enumerate(((wg, wgq), (wu, wuq), (wd, wdq))):
                if i == 2:
                    w, q = w[:].rearrange("p c n -> p (c n)"), q[:].rearrange("p c n -> p (c n)")
                else:
                    w, q = w[:], q[:]
                link(V.tensor_scalar(wtmp[:], w, winv[:, i:i + 1], MAGIC, ALU.mult, ALU.add))
                link(V.tensor_scalar(wtmp[:], wtmp[:], MAGIC, 1.0, ALU.subtract, ALU.min))
                link(V.tensor_scalar(q, wtmp[:], -1.0, None, ALU.max))
            dve.wait_ge(loaded_late, 16 * len(late))
            link(V.tensor_scalar(mkeep[:], mask[:], 0, CROSS_SCALE, ALU.not_equal, ALU.mult))
            link(V.tensor_scalar(mfill[:], mask[:], 0, -1e-9, ALU.is_equal, ALU.mult))
            arrived(dve, "conv_w", "chan", "lmask")
            dve.wait_ge(act_early, 1)
            dve.wait_ge(pool_early, 3 + H)

            links = {"front": 0, "back": 0}

            def front_chain(i, instruction):
                instruction.then_inc(front_link, 1)
                links["front"] += 1
                dve.wait_ge(front_link, FRONT_LINKS * i + links["front"])

            def back_chain(b, instruction):
                instruction.then_inc(back_link, 1)
                links["back"] += 1
                dve.wait_ge(back_link, BACK_LINKS * b + links["back"])

            def norm(half, chain, pass_, k):
                rows_in = (res, res_b)[half]
                for t in range(NT):
                    last = V.bn_stats(stats[half][:, t], rows_in[:, t])
                chain(pass_, last)
                dve.sem_inc(dve_passed)
                for t in range(NT):
                    last = V.bn_aggr(mv[half][:, t], stats[half][:, t])
                chain(pass_, last)
                V.tensor_scalar(var[half][:], mv[half][:, :, 1], EPS, None, ALU.add).then_inc(var_ready[half], 1)
                dve.wait_ge(rstd_ready[half], 3 * pass_ + (k - 3 * half))
                if k == 4:
                    dve.wait_ge(stored, 16 * pass_ + 16)
                for t in range(NT):
                    V.tensor_scalar(xs[k - 1][:, t], rows_in[:, t], mv[half][:, t, 0:1], rstd[half][:, t:t + 1],
                                    ALU.subtract, ALU.mult).then_inc(x_ready[k - 1], 1)

            def attention(b):
                links["back"] = 0
                for hg in range(2):
                    for h in range(hg * HG, (hg + 1) * HG):
                        hl = h % HG
                        for j, (ta, tb) in enumerate(((3, None), (2, 0), (1, None))):
                            n = 3 * h + j
                            dve.wait_ge(s_ps, 3 * H * b + (n + 1))
                            src = bank[6 + n % 2]
                            last = V.tensor_reduce(smax[:, hg, ta, hl:hl + 1], src[:, 0:(ta + 1) * P], AX.X, ALU.max)
                            if tb is not None:
                                last = V.tensor_reduce(smax[:, hg, tb, hl:hl + 1], src[:, 384:512], AX.X, ALU.max)
                            last.then_inc(s_max, 1)
                    dve.wait_ge(s_max, 3 * H * b + 3 * HG * (hg + 1))
                    back_chain(b, V.tensor_copy(sparts[:, hg, :, 0], smax[:, hg]))
                    back_chain(b, V.tensor_tensor(srest[:, hg], smax[:, hg], sparts[:, hg, :, 0], ALU.subtract))
                    back_chain(b, V.tensor_copy(sparts[:, hg, :, 1], srest[:, hg]))
                    V.tensor_tensor(sparts[:, hg, :, 2], srest[:, hg], sparts[:, hg, :, 1],
                                    ALU.subtract).then_inc(mp_ready, 1)
                for hg in range(2):
                    dve.wait_ge(pv_done, H * b + HG * (hg + 1))
                    if hg:
                        dve.wait_ge(att_ready, 2 * b + hg)
                    back_chain(b, V.reciprocal(rden[0:64], bank[1 + hg][64:128]))
                    V.tensor_tensor(att[64 * hg:64 * hg + 64], bank[1 + hg][0:64], rden[0:64],
                                    ALU.mult).then_inc(att_ready, 1)
                dve.wait_ge(proj_ps, b + 1)
                back_chain(b, V.scalar_tensor_tensor(out=res_b[:], in0=tiles(bank[4]), scalar=PROJ_SCALE, in1=xs[2][:],
                                                     op0=ALU.mult, op1=ALU.add))
                norm(1, back_chain, b, 4)

            def decayed(i, t):
                dve.wait_ge(dec_ready, NT * i + (t + 1))
                front_chain(i, V.tensor_copy(last_dec[:, t:t + 1], dec[0:DS, t, 3, P - 1:P]))
                dve.wait_ge(bt_ready, NT * i + (t + 1))
                V.tensor_tensor(dec[:, t], dec[:, t], cs[:, None, t * P:(t + 1) * P].broadcast_to([P, 4, P]),
                                ALU.mult).then_inc(ct_ready, 1)

            def state(i, t):
                dve.wait_ge(hp_ready, 3 * i + (t + 1))
                if t == 0:
                    V.tensor_copy(hst[:, 0], bank[3][0:DS, 0:DI]).then_inc(h_ready, 1)
                else:
                    dve.wait_ge(h_ready, 3 * i + t)
                    V.scalar_tensor_tensor(out=hst[:, t], in0=hst[:, t - 1], scalar=last_dec[:, t:t + 1],
                                           in1=bank[3][0:DS, 0:DI], op0=ALU.mult, op1=ALU.add).then_inc(h_ready, 1)

            def mixing(i, t):
                dve.wait_ge(lev_ready, NT * i + (t + 1))
                if t > 0:
                    dve.wait_ge(mix_ready, NT * i + t)
                V.tensor_tensor(mm[:, 0:4], tiles(bank[0]), lmask[:, 0:4], ALU.mult)
                V.tensor_tensor(mm[:, 4:8], tiles(bank[1]), lmask[:, 4:8], ALU.mult).then_inc(masked, 1)
                dve.wait_ge(masked, NT * i + (t + 1))
                V.tensor_reduce(mix[:, t], mm[:].rearrange("p l n -> p n l"), AX.X, ALU.add).then_inc(mix_ready, 1)

            def skip(i, t):
                dve.wait_ge(y_ready, NT * i + (t + 1))
                for c in range(NC):
                    last = V.scalar_tensor_tensor(out=ya[:, c, t * P:(t + 1) * P], in0=xc[:, c, t * P:(t + 1) * P],
                                                  scalar=chan[:, c, 1:2], in1=bank[2][:, c * P:(c + 1) * P],
                                                  op0=ALU.mult, op1=ALU.add)
                last.then_inc(ya_ready, 1)

            def hidden(i, t):
                dve.wait_ge(g_act, NT * i + (t + 1))
                V.scalar_tensor_tensor(out=hid[:, t], in0=bank[2 if t % 2 == 0 else 0][:], scalar=gsc[:, t, 1:2],
                                       in1=gact[:, t % 2], op0=ALU.mult, op1=ALU.mult).then_inc(hid_ready, 1)
                dve.wait_ge(hid_ready, NT * i + (t + 1))
                front_chain(i, V.tensor_reduce(hmax[:, t:t + 1], hid[:, t], AX.X, ALU.max, apply_absolute_value=True))
                front_chain(i, V.tensor_scalar(hmax[:, t:t + 1], hmax[:, t:t + 1], 1e-5, None, ALU.max))
                front_chain(i, V.reciprocal(hinv[:, t:t + 1], hmax[:, t:t + 1]))
                front_chain(i, V.tensor_scalar(hinv[:, t:t + 1], hinv[:, t:t + 1], 127.0, None, ALU.mult))
                V.tensor_scalar(hid[:, t], hid[:, t], hinv[:, t:t + 1], MAGIC, ALU.mult, ALU.add).then_inc(hq_magic, 1)

            def front(i, n):
                if n == 0:
                    links["front"] = 0
                    for c in range(NC):
                        dve.wait_ge(xin_ready, 2 * i + (c + 1))
                        front_chain(i, V.tensor_scalar(cacc[:, c], xin[:, c, 0:T], conv_w[:, c, 0:1], chan[:, c, 0:1],
                                                       ALU.mult, ALU.add))
                        for k in range(1, TAPS):
                            tap = V.scalar_tensor_tensor(out=cacc[:, c], in0=xin[:, c, k:k + T],
                                                         scalar=conv_w[:, c, k:k + 1], in1=cacc[:, c],
                                                         op0=ALU.mult, op1=ALU.add)
                            if k < TAPS - 1:
                                front_chain(i, tap)
                            else:
                                tap.then_inc(conv_done, 1)
                if n == 1:
                    dve.wait_ge(bc_ready, 3 * i + 2)
                    V.tensor_copy(cs[:], bank[1][:]).then_inc(c_ready, 1)
                    dve.wait_ge(bc_ready, 3 * i + 3)
                    V.tensor_copy(btok[:], bank[2][:, 0:NT * (DS + 1)].rearrange(
                        "p (n c) -> p n c", c=DS + 1)).then_inc(btok_ready, 1)
                    dve.wait_ge(btok_ready, i + 1)
                    dve.wait_ge(c_ready, i + 1)
                if n == 2:
                    dve.wait_ge(ln_dt, i + 1)
                    V.scalar_tensor_tensor(out=dts[:, 3], in0=btok[:, :, DS], scalar=0.0, in1=dts[:, 2],
                                           op0=ALU.max, op1=ALU.add).then_inc(dt_ready, 1)
                    dve.wait_ge(dt_ready, i + 1)
                    for t in range(NT):
                        V.tensor_scalar(dta[:, t], neg_a[:], dts[:, 3, t:t + 1], -1.0, ALU.mult,
                                        ALU.mult).then_inc(dta_ready, 1)
                if n == 4:
                    decayed(i, 0)
                    decayed(i, 1)
                    dve.wait_ge(esuf_ready, i + 1)
                    V.tensor_tensor(bsuf[:], esuf[:], btok[:, :, 0:DS], ALU.mult).then_inc(bsuf_ready, 1)
                if n == 5:
                    decayed(i, 2)
                    decayed(i, 3)
                if n == 6:
                    mixing(i, 0)
                if n == 7:
                    state(i, 0)
                    mixing(i, 1)
                if n == 8:
                    skip(i, 0)
                    state(i, 1)
                if n == 9:
                    mixing(i, 2)
                    skip(i, 1)
                    state(i, 2)
                if n == 10:
                    mixing(i, 3)
                    skip(i, 2)
                if n == 11:
                    skip(i, 3)
                if n == 12:
                    dve.wait_ge(outA_ready, i + 1)
                    dve.wait_ge(tok_loaded, 16 * i + 16)
                    front_chain(i, V.tensor_tensor(res[:], tiles(bank[3]), xtok[:], ALU.add))
                    norm(0, front_chain, i, 1)
                if n == 15:
                    dve.wait_ge(back_ps, i + 1)
                    dve.wait_ge(x_ready[0], NT * i + NT)
                    front_chain(i, V.tensor_tensor(res[:], tiles(bank[2]), xs[0][:], ALU.add))
                    norm(0, front_chain, i, 2)
                    dve.wait_ge(x_ready[1], NT * i + NT)
                    front_chain(i, V.tensor_reduce(amax[:], xs[1][:], AX.X, ALU.max, apply_absolute_value=True))
                    front_chain(i, V.tensor_scalar(amax[:], amax[:], 1e-5, None, ALU.max))
                    front_chain(i, V.reciprocal(ainv[:], amax[:]))
                    front_chain(i, V.tensor_scalar(ainv[:], ainv[:], 127.0, None, ALU.mult))
                    for t in range(NT):
                        last = V.tensor_scalar(xqf[:, t], xs[1][:, t], ainv[:, t:t + 1], MAGIC, ALU.mult, ALU.add)
                    front_chain(i, last)
                    V.tensor_scalar(xq[:], xqf[:], MAGIC, None, ALU.subtract).then_inc(xq_ready, 1)
                    V.tensor_scalar(gsc[:, :, 0], amax[:], wscale[:, 0:1], 1.0 / 127.0, ALU.mult, ALU.mult)
                    V.tensor_scalar(gsc[:, :, 1], amax[:], wscale[:, 1:2], 1.0 / 127.0, ALU.mult,
                                    ALU.mult).then_inc(gsc_ready, 1)
                    dve.wait_ge(kcol_ready, i + 1)
                    V.tensor_tensor(kblk[:], kcol[:, None].broadcast_to([P, H, CTX]),
                                    hmask[:, :, None].broadcast_to([P, H, CTX]), ALU.mult).then_inc(kv_blk, 1)
                    dve.wait_ge(ckv_ps, 2 * i + 2)
                    front_chain(i, V.tensor_tensor(vrow[:], bank[3][:, 0:D], rows[:, 0], ALU.add))
                    V.tensor_tensor(vblk[:], vrow[:, None].broadcast_to([P, 4, D]), vmask[:], ALU.mult).then_inc(kv_blk, 1)
                    dve.wait_ge(gsc_ready, i + 1)
                if 17 <= n < 20:
                    for t in ((0, 1), (2,), (3,))[n - 17]:
                        hidden(i, t)
                if n == 22:
                    front_chain(i, V.tensor_scalar(dsc[:], hmax[:], wscale[:, 2:3], 1.0 / 127.0, ALU.mult, ALU.mult))
                    dve.wait_ge(down_ps, i + 1)
                    for t in range(NT):
                        last = V.scalar_tensor_tensor(out=res[:, t], in0=bank[3][:, t * P:(t + 1) * P],
                                                      scalar=dsc[:, t:t + 1], in1=xs[1][:, t],
                                                      op0=ALU.mult, op1=ALU.add)
                    front_chain(i, last)
                    norm(0, front_chain, i, 3)
                if n == 24:
                    for s in range(2):
                        dve.wait_ge(part0, 2 * i + (s + 1))
                        V.tensor_tensor(rest[s][:], bank[1 + s][:], part[s][0][:], ALU.subtract).then_inc(rest0, 1)
                    dve.wait_ge(v_ps, i + 1)
                    for hg in range(2):
                        for t in range(NT):
                            last = V.tensor_copy(diagonal(vpad, t, hg), bank[3][:, t * P + hg * 64:t * P + hg * 64 + 64]
                                                 .rearrange("p (h d) -> p h d", d=HD))
                    last.then_inc(v_sb, 1)
                    assert links["front"] == FRONT_LINKS, links["front"]

            def back(b, slot):
                if 3 <= slot < 7:
                    t = slot - 3
                    dve.wait_ge(cs_ps, NT * b + (t + 1))
                    if t >= 2:
                        dve.wait_ge(cp_ready, NT * b + (t - 1))
                    V.tensor_tensor(s1[:, t % 2], bank[4 + t % 2][:].rearrange("p (h k) -> p h k", k=CTX),
                                    mkeep[:, None, t].broadcast_to([P, H, CTX]), ALU.mult).then_inc(cs_kept, 1)
                    dve.wait_ge(cs_full, NT * b + (t + 1))
                    V.tensor_reduce(cmax[:, t % 2], s1[:, t % 2], AX.X, ALU.max).then_inc(cs_max, 1)
                if slot == 8:
                    dve.wait_ge(co_ps, b + 1)
                    back_chain(b, V.reciprocal(rden[:], bank[5][:]))
                    V.tensor_tensor(att[:], bank[4][:], rden[:], ALU.mult).then_inc(co_ready, 1)
                if slot == 9:
                    dve.wait_ge(cproj_ps, b + 1)
                    dve.wait_ge(x4b_ready, b + 1)
                    back_chain(b, V.tensor_tensor(res_b[:], tiles(bank[6]), x4b[:], ALU.add))
                    norm(1, back_chain, b, 5)
                if slot == 11:
                    dve.wait_ge(gate_ps, b + 1)
                    V.tensor_copy(glog[:], bank[6][:, 0:NT * NE].rearrange("p (n e) -> p n e", e=NE)).then_inc(glog_ready, 1)
                    dve.wait_ge(glog_ready, b + 1)
                    for t in range(NT):
                        other = glog[:, t, None].broadcast_to([P, NE, NE])
                        own = glog[:, t, :, None].broadcast_to([P, NE, NE])
                        V.tensor_tensor(gge[:, t], other, own, ALU.is_ge)
                        last = V.tensor_tensor(ggt[:, t], other, own, ALU.is_gt)
                    back_chain(b, last)
                    back_chain(b, V.tensor_tensor(gge[:].rearrange("p n a c -> p n (a c)"),
                                                  gge[:].rearrange("p n a c -> p n (a c)"),
                                                  before[:, None].broadcast_to([P, NT, NE * NE]), ALU.mult))
                    back_chain(b, V.tensor_tensor(ggt[:], ggt[:], gge[:], ALU.max))
                    back_chain(b, V.tensor_reduce(rank[:], ggt[:], AX.X, ALU.add))
                    back_chain(b, V.tensor_scalar(rank[:], rank[:], 2.0, None, ALU.is_lt))
                    back_chain(b, V.tensor_reduce(gtop[:], glog[:], AX.X, ALU.max))
                    V.tensor_tensor(glog[:], glog[:], gtop[:, :, None].broadcast_to([P, NT, NE]),
                                    ALU.subtract).then_inc(gsub_ready, 1)
                    dve.wait_ge(gexp_ready, b + 1)
                    back_chain(b, V.tensor_tensor(gates[:], gexp[:], rank[:], ALU.mult))
                    back_chain(b, V.tensor_reduce(gsum[:], gates[:], AX.X, ALU.add))
                    back_chain(b, V.reciprocal(gsum[:], gsum[:]))
                    back_chain(b, V.tensor_tensor(gates[:], gates[:], gsum[:, :, None].broadcast_to([P, NT, NE]),
                                                  ALU.mult))
                e, sub = divmod(slot - E_SLOTS, FC)
                if slot >= E_SLOTS and sub == FC - 1:
                    dve.wait_ge(e_ps, SLICES * b + (e + 1))
                    src = bank[6 + e % 2]
                    if e == 0:
                        V.tensor_tensor(moe[:], tiles(src), xs[4][:], ALU.add).then_inc(e_added, 1)
                    else:
                        dve.wait_ge(e_added, SLICES * b + e)
                        dst = res_b if e == SLICES - 1 else moe
                        for t in range(NT):
                            last = V.scalar_tensor_tensor(out=dst[:, t], in0=src[:, t * P:(t + 1) * P],
                                                          scalar=gates[:, t, e - 1:e], in1=moe[:, t],
                                                          op0=ALU.mult, op1=ALU.add)
                        last.then_inc(e_added, 1)
                    if e == SLICES - 1:
                        dve.wait_ge(e_added, SLICES * b + SLICES)
                        norm(1, back_chain, b, 6)
                        assert links["back"] == BACK_LINKS, links["back"]

            halves(dve, attention, back, front)

        @block.tensor
        def _(pe):
            mmul = nc.tensor.matmul

            arrived(pe, "ones")
            pe.wait_ge(early, 3)
            mmul(bank[7][:, 0:3], ones[:], wabs[:], start=True, stop=True).then_inc(pe_early, 1)
            arrived(pe, "w_in", "w_bb", "w_cc", "w_bdt", "lev_a", "lev_b", "suf", "ident", "w_out", "cconv", "identb")
            pe.wait_ge(loaded_late, 16 * len(late))
            pe.wait_ge(pool_early, 3 + H)

            def turn(pass_, k, bk):
                for t in range(NT):
                    pe.wait_ge(x_ready[k - 1], NT * pass_ + (t + 1))
                    last = nc.tensor.transpose(bank[bk][:, t * P:(t + 1) * P], xs[k - 1][:, t], ident[:])
                last.then_inc(xT_ps[k - 1], 1)

            def at(h):
                return slice(64 * (h % 2), 64 * (h % 2) + PARTS * HD)

            def scores(b, h):
                for j, tts in enumerate(((3,), (2, 0), (1,))):
                    n = 3 * h + j
                    if n >= 2:
                        pe.wait_ge(s_max, 3 * H * b + (n - 1))
                    for i, t in enumerate(tts):
                        lo, w = 384 * i, (t + 1) * P
                        dst = bank[6 + n % 2]
                        mmul(dst[:, lo:lo + w], stack[1][at(h), h // 2, t * P:(t + 1) * P],
                             stack[0][at(h), h // 2, 0:w], start=True, stop=False)
                        last = mmul(dst[:, lo + w - P:lo + w], identb[:], tri_q[:], start=False, stop=True)
                    last.then_inc(s_ps, 1)

            def maxima(b, hg):
                pe.wait_ge(mp_ready, 2 * b + (hg + 1))
                for t in range(NT):
                    last = nc.tensor.transpose(bank[3][0:3 * HG].bitcast(BF16)[:, t * P:(t + 1) * P],
                                               sparts[:, hg, t].rearrange("p a h -> p (a h)"), identb[:])
                last.then_inc(mT_ps, 1)

            def turned_scores(b, h):
                if h % HG == 0:
                    pe.wait_ge(mT_sb, 2 * b + (h // HG + 1))
                for j, tts in enumerate(((0,), (1, 3), (2,))):
                    n = 3 * h + j
                    if n >= 2:
                        pe.wait_ge(prob_ready, 3 * H * b + (n - 1))
                    dst = bank[4 + n % 2]
                    for i, t in enumerate(tts):
                        lo, w = 384 * i, T - t * P
                        mmul(dst[:, lo:lo + w], stack[0][at(h), h // 2, t * P:(t + 1) * P],
                             stack[1][at(h), h // 2, t * P:T], start=True, stop=False)
                        mmul(dst[:, lo:lo + w], pick[:, h % HG], mT[:, h // HG, t * P:T], start=False, stop=False)
                        last = mmul(dst[:, lo:lo + P], identb[:], tri_k[:], start=False, stop=True)
                    last.then_inc(st_ps, 1)

            def weigh(b, h):
                dst = bank[1 + h // HG]
                for j, tts in enumerate(((0,), (1, 3), (2,))):
                    pe.wait_ge(prob_ready, 3 * H * b + (3 * h + j + 1))
                    for i, t in enumerate(tts):
                        last = mmul(dst[:, t * P:T], vpad[:, t, h], prob[:, h % 2, j, 384 * i:384 * i + T - t * P],
                                    start=h % HG == 0 and t == 0, stop=h % HG == HG - 1 and t == 2)
                last.then_inc(pv_done, 1)

            def attention(b):
                pe.wait_ge(v_sb, b + 1)
                pe.wait_ge(stacked, 16 * 2 * 2 * PARTS * b + 16 * 2 * 2 * PARTS)
                for h in range(HG):
                    scores(b, h)
                maxima(b, 0)
                for h in range(H):
                    turned_scores(b, h)
                    if h < HG:
                        scores(b, HG + h)
                    if h > 0:
                        weigh(b, h - 1)
                    if h == HG - 1:
                        maxima(b, 1)
                weigh(b, H - 1)
                pe.wait_ge(att_ready, 2 * b + 2)
                for t in range(NT):
                    last = mmul(bank[4][:, t * P:(t + 1) * P], att[:, t * P:(t + 1) * P], w_p[:], start=True, stop=True)
                last.then_inc(proj_ps, 1)

            def decays(i, t):
                pe.wait_ge(dta_ready, NT * i + (t + 1))
                if t >= 2:
                    pe.wait_ge(dec_ready, NT * i + (t - 1))
                mmul(bank[1 + t % 2][0:64], dta[:, t, 0:DS], lev_a[:].rearrange("p l n -> p (l n)"),
                     start=True, stop=True)
                mmul(bank[1 + t % 2][64:128], dta[:, t, DS:2 * DS], lev_b[:].rearrange("p l n -> p (l n)"),
                     start=True, stop=True).then_inc(gdec_ready, 1)

            def levels(i, t):
                pe.wait_ge(ct_ready, NT * i + (t + 1))
                if t == 0:
                    pe.wait_ge(xdt_ready, NT * i + NT)
                    pe.wait_ge(dec_ready, NT * i + NT)
                else:
                    pe.wait_ge(masked, NT * i + t)
                for l in range(3):
                    mmul(bank[0][:, l * P:(l + 1) * P], bt[0:64, t, l], dec[0:64, t, l], start=True, stop=True)
                mmul(bank[0][:, 3 * P:4 * P], bs[0:64, t * P:(t + 1) * P], cs[0:64, t * P:(t + 1) * P],
                     start=True, stop=True)
                for l in range(4):
                    last = mmul(bank[1][:, l * P:(l + 1) * P], bt[64:128, t, l], dec[64:128, t, l],
                                start=True, stop=True)
                last.then_inc(lev_ready, 1)

            def carry(i, t):
                if t == 0:
                    pe.wait_ge(bsuf_ready, i + 1)
                else:
                    pe.wait_ge(h_ready, 3 * i + t)
                mmul(bank[3][0:DS, 0:DI], bsuf[:, t], xdt[:, t], start=True, stop=True).then_inc(hp_ready, 1)

            def outputs(i, t):
                pe.wait_ge(mix_ready, NT * i + (t + 1))
                if t > 0:
                    pe.wait_ge(h_ready, 3 * i + t)
                    pe.wait_ge(ya_ready, NT * i + t)
                for c in range(NC):
                    dst = bank[2][:, c * P:(c + 1) * P]
                    last = mmul(dst, xdt[:, t, c * P:(c + 1) * P], mix[:, t], start=True, stop=t == 0)
                    if t > 0:
                        last = mmul(dst, hst[:, t - 1, c * P:(c + 1) * P], dec[0:64, t, 3], start=False, stop=True)
                last.then_inc(y_ready, 1)

            def front(i, n):
                if n == 0:
                    pe.wait_ge(x_loaded, 16 * i + 16)
                    for c in range(2 * NC):
                        mmul(bank[c][:], w_in[:, c * P:(c + 1) * P], xT[:], start=True, stop=True).then_inc(xz_ready, 1)
                if n == 1:
                    pe.wait_ge(xc_ready, 2 * i + 2)
                    for k, w in enumerate((w_bb, w_cc)):
                        for c in range(NC):
                            last = mmul(bank[k][:], w[:, c], xc[:, c], start=c == 0, stop=c == NC - 1)
                        last.then_inc(bc_ready, 1)
                    for t in range(NT):
                        for c in range(NC):
                            last = mmul(bank[2][:, t * (DS + 1):(t + 1) * (DS + 1)], xc[:, c, t * P:(t + 1) * P],
                                        w_bdt[:, c], start=c == 0, stop=c == NC - 1)
                    last.then_inc(bc_ready, 1)
                if n in (1, 2):
                    if n == 2:
                        pe.wait_ge(b_ready, i + 1)
                    for t in (2 * (n - 1), 2 * (n - 1) + 1):
                        for c in range(NC):
                            lo = (t % 2) * DI + c * P
                            last = nc.tensor.transpose(bank[3 if n == 1 else 0][:, lo:lo + P],
                                                       xc[:, c, t * P:(t + 1) * P], ident[:])
                    last.then_inc(xcT_ready, 1)
                if n == 3:
                    pe.wait_ge(c_ready, i + 1)
                    decays(i, 0)
                    pe.wait_ge(btok_ready, i + 1)
                    decays(i, 1)
                if n == 4:
                    pe.wait_ge(xdt_ready, NT * i + 2)
                    for t in range(NT):
                        pe.wait_ge(dta_ready, NT * i + (t + 1))
                        last = mmul(bank[3][:, t * DS:(t + 1) * DS], suf[:], dta[:, t, 0:DS], start=True, stop=True)
                    last.then_inc(gsuf_ready, 1)
                if n == 5:
                    decays(i, 2)
                    decays(i, 3)
                if n == 6:
                    levels(i, 0)
                if n == 7:
                    carry(i, 0)
                    levels(i, 1)
                if n == 8:
                    outputs(i, 0)
                    carry(i, 1)
                if n == 9:
                    levels(i, 2)
                    outputs(i, 1)
                    carry(i, 2)
                if n == 10:
                    levels(i, 3)
                    outputs(i, 2)
                if n == 11:
                    outputs(i, 3)
                if n == 12:
                    for t in range(NT):
                        pe.wait_ge(yg_ready, NT * i + (t + 1))
                        for c in range(NC):
                            last = mmul(bank[3][:, t * P:(t + 1) * P], ya[:, c, t * P:(t + 1) * P], w_out[:, c],
                                        start=c == 0, stop=c == NC - 1)
                    last.then_inc(outA_ready, 1)
                if n == 13:
                    turn(i, 1, 0)
                if n == 14:
                    pe.wait_ge(xT_sb[0], i + 1)
                    for k in range(TAPS):
                        last = mmul(bank[1][:, 0:COMP], cconv[:, k], turned[:, KEEP + k:KEEP + CTX:TAPS],
                                    start=k == 0, stop=k == TAPS - 1)
                    last.then_inc(comp_ps, 1)
                if n == 15:
                    pe.wait_ge(comp_sb, i + 1)
                    for t, lo in enumerate((COMP, P + COMP, KEEP + CTX, KEEP + P + CTX)):
                        last = nc.tensor.transpose(bank[2][:, t * P:(t + 1) * P], turned[:, lo:lo + P], ident[:])
                    last.then_inc(back_ps, 1)
                    pe.wait_ge(ctx_ready, i + 1)
                    mmul(bank[1][:, 0:CTX], c_k[:], ctx4[:, 0], start=True, stop=True).then_inc(ckv_ps, 1)
                    mmul(bank[3][:, 0:D], ctx4[:].rearrange("p a k -> p (a k)"), c_v[:],
                         start=True, stop=True).then_inc(ckv_ps, 1)
                if n == 16:
                    pe.wait_ge(xq_ready, i + 1)
                    for t in range(NT):
                        last = nc.tensor.transpose(bank[0][:].bitcast(BF16)[:, t * P:(t + 1) * P], xq[:, t], identb[:])
                    last.then_inc(xT_ps[1], 1)
                if 17 <= n < 20:
                    for t in ((0, 1), (2,), (3,))[n - 17]:
                        if t == 0:
                            pe.wait_ge(xT_sb[1], i + 1)
                            pe.wait_ge(kv_blk, 2 * i + 2)
                        if t >= 2:
                            pe.wait_ge(hid_ready, NT * i + (t - 1))
                        mmul(bank[1 if t % 2 == 0 else 3][:], xqT[:, t * P:(t + 1) * P], wgq[:], start=True, stop=True)
                        mmul(bank[2 if t % 2 == 0 else 0][:], xqT[:, t * P:(t + 1) * P], wuq[:],
                             start=True, stop=True).then_inc(gu_ps, 1)
                if n in (20, 21):
                    if n == 20:
                        pe.wait_ge(hid_ready, NT * i + 3)
                    for t in (2 * (n - 20), 2 * (n - 20) + 1):
                        pe.wait_ge(hq_ready, NT * i + (t + 1))
                        if t >= 2:
                            pe.wait_ge(hT_sb, NT * i + (t - 1))
                        for c in range(FC):
                            last = nc.tensor.transpose(bank[1 + t % 2][:].bitcast(BF16)[:, c * P:(c + 1) * P],
                                                       hq[:, t, c * P:(c + 1) * P], identb[:])
                        last.then_inc(hT_ps, 1)
                if n == 22:
                    for t in range(NT):
                        pe.wait_ge(hT_sb, NT * i + (t + 1))
                        for c in range(FC):
                            last = mmul(bank[3][:, t * P:(t + 1) * P], hqT[:, t, c], wdq[:, c],
                                        start=c == 0, stop=c == FC - 1)
                    last.then_inc(down_ps, 1)
                if n == 23:
                    turn(i, 3, 0)
                if n == 24:
                    pe.wait_ge(xT_sb[2], i + 1)
                    mmul(bank[1][:], w_k[:], turned[:, 0:T], start=True, stop=True).then_inc(kq_ps, 1)
                    mmul(bank[2][:], w_q[:], turned[:, 0:T], start=True, stop=True).then_inc(kq_ps, 1)
                    for t in range(NT):
                        last = mmul(bank[3][:, t * P:(t + 1) * P], turned[:, t * P:(t + 1) * P], w_v[:],
                                    start=True, stop=True)
                    last.then_inc(v_ps, 1)

            def cross_scores(b, t):
                if t >= 2:
                    pe.wait_ge(cs_kept, NT * b + (t - 1))
                mmul(bank[4 + t % 2][:], qT[:, t * P:(t + 1) * P], kblk[:].rearrange("p h k -> p (h k)"),
                     start=True, stop=True).then_inc(cs_ps, 1)

            def expand(b, e, c):
                n = e * FC + c
                if c == 0:
                    pe.wait_ge(e_loaded[e % 3], 16 * 3 * b + 16 * (e // 3 + 1))
                if n >= 2:
                    pe.wait_ge(h_act, SLICES * FC * b + (n - 1))
                mmul(bank[4 + n % 2][:], experts[:, e % 3, c * P:(c + 1) * P], turned_b[:],
                     start=True, stop=True).then_inc(h_ps, 1)

            def back(b, slot):
                if slot == 1:
                    turn(b, 4, 5)
                if slot == 2:
                    pe.wait_ge(xT_sb[3], b + 1)
                    mmul(bank[6][:], c_q[:], turned_b[:], start=True, stop=True).then_inc(cq_ps, 1)
                if slot == 3:
                    pe.wait_ge(cq_sb, b + 1)
                    pe.wait_ge(kv_blk, 2 * b + 2)
                    cross_scores(b, 0)
                    cross_scores(b, 1)
                if 4 <= slot < 8:
                    t = slot - 4
                    pe.wait_ge(cp_ready, NT * b + (t + 1))
                    if t >= 2:
                        pe.wait_ge(cpT_sb, NT * b + (t - 1))
                    for c in range(4):
                        last = nc.tensor.transpose(bank[6 + t % 2][:, c * P:(c + 1) * P], pc[:, t % 2, c], ident[:])
                    last.then_inc(cpT_ps, 1)
                    if t + 2 < NT:
                        cross_scores(b, t + 2)
                if slot == 8:
                    pe.wait_ge(cpT_sb, NT * b + NT)
                    for k, w in enumerate((vblk, vmask)):
                        for c in range(4):
                            last = mmul(bank[4 + k][:], w[:, c], pT[:, c], start=c == 0, stop=c == 3)
                    last.then_inc(co_ps, 1)
                if slot == 9:
                    pe.wait_ge(co_ready, b + 1)
                    for t in range(NT):
                        last = mmul(bank[6][:, t * P:(t + 1) * P], att[:, t * P:(t + 1) * P], c_o[:],
                                    start=True, stop=True)
                    last.then_inc(cproj_ps, 1)
                if slot == 10:
                    turn(b, 5, 7)
                if slot == 11:
                    pe.wait_ge(xT_sb[4], b + 1)
                    for t in range(NT):
                        last = mmul(bank[6][:, t * NE:(t + 1) * NE], turned_b[:, t * P:(t + 1) * P], wgate[:],
                                    start=True, stop=True)
                    last.then_inc(gate_ps, 1)
                    expand(b, 0, 0)
                    expand(b, 0, 1)
                if slot >= E_SLOTS:
                    e, t = divmod(slot - E_SLOTS, FC)
                    if e == 0 and t == 0:
                        expand(b, 0, 2)
                        expand(b, 0, 3)
                        pe.wait_ge(glog_ready, b + 1)
                    if e + 1 < SLICES:
                        expand(b, e + 1, t)
                    if e >= 2 and t == 0:
                        pe.wait_ge(e_added, SLICES * b + (e - 1))
                    for c in range(FC):
                        if t == 0:
                            pe.wait_ge(h_act, SLICES * FC * b + (e * FC + c + 1))
                        last = mmul(bank[6 + e % 2][:, t * P:(t + 1) * P], act_h[:, e % 2, c, t * P:(t + 1) * P],
                                    experts[:, e % 3, FF + c * P:FF + (c + 1) * P], start=c == 0, stop=c == FC - 1)
                    if t == FC - 1:
                        last.then_inc(e_ps, 1)
                    if slot == SLOTS - 1:
                        pe.wait_ge(e_added, SLICES * b + SLICES)

            halves(pe, attention, back, front)


def diagonal(vpad, t, hg):
    flat = vpad[:, t, hg * HG:(hg + 1) * HG].rearrange("p h c -> p (h c)")
    return bass.AP(tensor=flat.tensor, offset=flat.offset, ap=[list(flat.ap[0]), [P + HD, HG], [1, HD]])


def shape_constants():
    bf = np.dtype("bfloat16")
    f = np.float32
    j = np.arange(P)[:, None]
    t = np.arange(P)[None, :]

    def between(half):
        mid = t // (2 * half) * (2 * half) + half
        return np.where(t >= mid, (j >= mid) & (j <= t), (j > t) & (j < mid)).astype(f)

    def pairs(half):
        same = j // (2 * half) == t // (2 * half)
        return (same & (j % (2 * half) < half) & (t % (2 * half) >= half)).astype(f)

    eye = np.eye(P, dtype=f)
    head = np.arange(P) // HD
    pick = np.zeros((3 * HG, HG, P), f)
    for r in range(3 * HG):
        pick[r, r % HG] = -1.0
    vm = (4 * np.arange(4)[None, :, None] + (np.arange(P) // CTX)[:, None, None] == head[None, None, :]).astype(f)
    e = np.arange(NE)
    return {
        "lev_a": np.stack([between(h) for h in LEVELS_A] + [(j <= t).astype(f)], 1),
        "lev_b": np.stack([between(h) for h in LEVELS_B], 1),
        "suf": (j > t).astype(f),
        "lmask": np.stack([pairs(h) for h in LEVELS_A] + [eye] + [pairs(h) for h in LEVELS_B], 1).astype(bf),
        "ident": eye, "identb": eye.astype(bf), "ones": np.ones((P, P), f),
        "tri_q": np.where(t > j, NEG, 0.0).astype(bf), "tri_k": np.where(j > t, NEG, 0.0).astype(bf),
        "pick": pick.astype(bf),
        "hmask": (head[:, None] == np.arange(H)[None, :]).astype(f),
        "vmask": vm,
        "before": np.broadcast_to((e[None, :] < e[:, None]).astype(f).reshape(1, NE * NE), (P, NE * NE)),
    }


def kernel(**x):
    import concourse.bacc as bacc
    from concourse.bass_utils import run_bass_kernel_spmd

    x = {k: np.asarray(v) for k, v in x.items()}

    def chunks(w):
        return w.reshape(-1, P, w.shape[-1]).transpose(1, 0, 2)

    wx = x["L0_attn_W_x"].T
    wb, wc, wdt = wx[:, :DS], wx[:, DS:2 * DS], wx[:, 2 * DS:]
    perm = np.arange(D).reshape(NPAIR, 2, HD).transpose(1, 2, 0).reshape(-1)
    w1 = np.concatenate([x["L1_ffn_shared_w1"][None], x["L1_ffn_experts_w1"]])
    w2 = np.concatenate([x["L1_ffn_shared_w2"][None], x["L1_ffn_experts_w2"]])
    arrays = {
        "xT": x["x"].transpose(0, 2, 1),
        "xtok": x["x"].reshape(B, NT, P, D).transpose(0, 2, 1, 3),
        "ctxT": x["ctx_1024"].transpose(2, 0, 1),
        "w_in": x["L0_attn_W_in"].T,
        "conv_w": chunks(x["L0_attn_conv_w"].reshape(DI, TAPS)),
        "chan": chunks(np.stack([x["L0_attn_conv_b"], x["L0_attn_D"]], 1)),
        "w_bb": chunks(np.concatenate([wb, wb], 1)),
        "w_cc": chunks(np.concatenate([wc, wc], 1)),
        "w_bdt": chunks(np.concatenate([wb, wdt], 1)),
        "alog": np.broadcast_to(np.concatenate([x["L0_attn_A_log"]] * 2), (P, 2 * DS)),
        "w_out": chunks(x["L0_attn_W_out"].T),
        "cconv": x["L0_xattn_conv_w"].transpose(1, 0, 2),
        "cols": np.stack([x["L0_xattn_conv_b"], x["L1_xattn_bq"], x["L1_xattn_bk"]], 1),
        "wg": x["L0_ffn_w_gate"].T, "wu": x["L0_ffn_w_up"].T, "wd": chunks(x["L0_ffn_w_down"].T),
        "w_q": x["L1_attn_W_query"].T[:, perm], "w_k": x["L1_attn_W_key"].T[:, perm],
        "w_v": x["L1_attn_W_value"].T, "w_p": x["L1_attn_W_proj"].T,
        "c_q": x["L1_xattn_wq"].T, "c_k": x["L1_xattn_wk"].T, "c_v": x["L1_xattn_wv"].T, "c_o": x["L1_xattn_wo"].T,
        "rows": np.broadcast_to(np.stack([x["L1_xattn_bv"], x["L1_xattn_bo"]])[None], (P, 2, D)),
        "mask": x["mask_1x1xSxS2_if1"].reshape(NT, P, CTX).transpose(1, 0, 2),
        "w12": np.concatenate([w1.transpose(0, 2, 1), w2.transpose(0, 2, 1).reshape(SLICES, FC, P, D)
                               .transpose(0, 2, 1, 3).reshape(SLICES, P, FF)], 2),
        "wgate": x["L1_ffn_gate_w"].T,
    }
    arrays.update(shape_constants())
    nc = bacc.Bacc("TRN2", target_bir_lowering=False, num_devices=1)
    given, aps = {}, {}
    for name, v in arrays.items():
        v = np.ascontiguousarray(v)
        given["in_" + name] = v
        aps[name] = nc.dram_tensor("in_" + name, v.shape, mybir.dt.from_np(v.dtype), kind="ExternalInput").ap()
    out = nc.dram_tensor("out_0", (B, P, NT, D), F32, kind="ExternalOutput").ap()
    decoder(nc, aps, out)
    r = run_bass_kernel_spmd(nc, [given], core_ids=[0])
    return r.results[0]["out_0"].transpose(0, 2, 1, 3).reshape(B, T, D)
```

```python
from contextlib import ExitStack

import numpy as np
import concourse.bass as bass
from concourse import mybir

ALU = mybir.AluOpType
ACT = mybir.ActivationFunctionType
AX = mybir.AxisListType
F32 = mybir.dt.float32
BF16 = mybir.dt.bfloat16
I32 = mybir.dt.int32

B, T, D = 4, 512, 128
P = 128
NT = T // P
DI = 2 * D
NC = DI // P
DS = 64
TAPS = 4
NLEV = 8
CTX = 32
COMP = 8
KEEP = 256
FF = 512
FC = FF // P
H, HD = 16, 8
NPAIR = H // 2
HG = 8
PARTS = 6
NE = 8
SLICES = NE + 1
EPS = 1e-5
MAGIC = 1.5 * 2.0 ** 23
NEG = -1e30
PRODUCTS = [(0, 0), (0, 1), (1, 0), (0, 2), (2, 0), (1, 1)]
LEVELS_A = [64, 16, 4]
LEVELS_B = [32, 8, 2, 1]
SCORE_SCALE = (1.0 / D) * HD ** -0.5
FRONT_LINKS = 45
BACK_LINKS = 27
E_SLOTS = 11
SLOTS = E_SLOTS + SLICES * FC
ATT_UNITS = H + 2
RAMP = 10
SCORE_BANKS = (0, 1, 3)
KEY_TILES = ((0,), (1, 3), (2,))
IN_ATTENTION = [7, 9, 10, 11, 12, 13, 14, 15, 16, 17]
IN_SLOTS = [0, 3, 4, 5, 7, 8, 9, 13, 14, 15, 17, 18, 19, 21, 23, 24,
            34, 35, 36, 37, 38, 39, 40, 40, 42, 43, 41]
FRONT_AT = IN_ATTENTION + [ATT_UNITS + slot for slot in IN_SLOTS]
assert len(FRONT_AT) == 26 + RAMP + 1
CROSS_SCALE = HD ** -0.5
PROJ_SCALE = 1.0 / D


def decoder(nc, a, out):
    with ExitStack() as ctx:
        def sb(name, shape, dt=F32):
            return ctx.enter_context(nc.sbuf_tensor(name, shape, dt))

        def sem(name):
            return ctx.enter_context(nc.semaphore(name))

        names = {}

        def resident(name, dt=F32):
            names[name] = sb("s_" + name, list(a[name].shape), dt)
            return names[name]

        def share(name, size):
            region = sb(name, [P, size])

            def view(at, shape, dt=F32):
                n = int(np.prod(shape)) // (1 if dt == F32 else 2)
                flat = region[:, at:at + n]
                if dt != F32:
                    flat = flat.bitcast(dt)
                dims = [f"d{i}" for i in range(len(shape))]
                if len(shape) == 1:
                    return flat
                return flat.rearrange(f"p ({' '.join(dims)}) -> p {' '.join(dims)}",
                                      **{d: v for d, v in zip(dims[1:], shape[1:])})

            return view

        one = share("region1", 5120)
        two = share("region2", 3072)
        three = share("region3", 4096)
        four = share("region4", 3584)

        xT = sb("xT", [P, T])
        xtok = sb("xtok", [P, NT, D])
        ctxT = resident("ctxT")
        w_in = resident("w_in")
        conv_w = resident("conv_w")
        chan = resident("chan")
        w_bb = resident("w_bb")
        w_cc = resident("w_cc")
        w_bdt = resident("w_bdt")
        alog = resident("alog")
        w_out = resident("w_out")
        lev_a = resident("lev_a")
        lev_b = resident("lev_b")
        suf = resident("suf")
        lmask = resident("lmask", BF16)
        ident = resident("ident")
        identb = resident("identb", BF16)
        ones = resident("ones")
        cconv = resident("cconv")
        cols = resident("cols")
        wg = names["wg"] = one(0, [FF])
        wu = names["wu"] = one(512, [FF])
        wd = names["wd"] = one(1024, [FC, D])
        w_q = resident("w_q")
        w_k = resident("w_k")
        w_v = resident("w_v")
        w_p = resident("w_p")
        tri_q = resident("tri_q", BF16)
        tri_k = resident("tri_k", BF16)
        c_q = resident("c_q")
        c_k = resident("c_k")
        c_v = resident("c_v")
        c_o = resident("c_o")
        rows = resident("rows")
        hmask = resident("hmask")
        vmask = resident("vmask")
        mask = resident("mask", I32)
        experts = sb("experts", [P, 3, 2 * FF])
        wgate = resident("wgate")
        before = resident("before")

        neg_a = sb("neg_a", [P, 2 * DS])
        minus_half = sb("minus_half", [P, NT])
        wgq, wuq = sb("wgq", [P, FF], BF16), sb("wuq", [P, FF], BF16)
        wdq = sb("wdq", [P, FC, D], BF16)
        wabs = sb("wabs", [P, 3])
        wscale = sb("wscale", [P, 3])
        winv = sb("winv", [P, 3])
        wtmp = one(1536, [FF])
        mkeep = sb("mkeep", [P, NT, CTX])
        mfill = sb("mfill", [P, NT, CTX])
        vpad = sb("vpad", [P, NT, H, P])

        xin = sb("xin", [P, NC, TAPS - 1 + T])
        cacc = two(0, [NC, T])
        xc = sb("xc", [P, NC, T])
        zs = sb("zs", [P, NC, T])
        bs = sb("bs", [P, T])
        cs = sb("cs", [P, T])
        dts = sb("dts", [P, 4, NT])
        dta = sb("dta", [P, NT, P])
        xdt = two(0, [NT, DI])
        esuf = sb("esuf", [P, NT, DS])
        bsuf = sb("bsuf", [P, NT, DS])
        btok = sb("btok", [P, NT, DS + 1])
        dec = one(0, [NT, 4, P])
        last_dec = sb("last_dec", [DS, NT])
        bt = one(2048, [NT, 4, P])
        mm = one(4096, [NLEV, P])
        mix = two(1024, [NT, P])
        hst = sb("hst", [DS, NT - 1, DI])
        ya = two(1536, [NC, T])

        res = sb("res", [P, NT, D])
        res_b = sb("res_b", [P, NT, D])
        rows_a, rows_c = sb("rows_a", [P, NT, D]), sb("rows_c", [P, NT, D])
        xs = [rows_a, two(2560, [NT, D]), rows_a, rows_c, rows_c, rows_c]
        stats = [sb(f"stats{h}", [P, NT, 6]) for h in range(2)]
        mv = [sb(f"mv{h}", [P, NT, 2]) for h in range(2)]
        var = [sb(f"var{h}", [P, NT]) for h in range(2)]
        rstd = [sb(f"rstd{h}", [P, NT]) for h in range(2)]
        turned = sb("turned", [P, T + CTX])
        turned_b = sb("turned_b", [P, T])

        amax = sb("amax", [P, NT])
        ainv = sb("ainv", [P, NT])
        xqf = two(0, [NT, D])
        xq = sb("xq", [P, NT, D], BF16)
        xqT = sb("xqT", [P, T], BF16)
        gsc = sb("gsc", [P, NT, 2])
        hid = one(0, [NT, FF])
        gact = one(2048, [2, FF])
        hq = one(3072, [NT, FF], BF16)
        hqT = one(4096, [NT, FC, P], BF16)
        hmax = sb("hmax", [P, NT])
        hinv = sb("hinv", [P, NT])
        dsc = sb("dsc", [P, NT])

        part = [[two(256 * (3 * s + i), [T], BF16) for i in range(3)] for s in range(2)]
        rest = [two(1536 + 512 * s, [T]) for s in range(2)]
        stack = [sb(f"stack{s}", [P, NPAIR, T], BF16) for s in "kq"]
        smax = sb("smax", [P, 2, NT, HG])
        srest = sb("srest", [P, 2, NT, HG])
        sparts = sb("sparts", [P, 2, NT, 2, 3, HG // 2], BF16)
        mT = sb("mT", [3 * HG, 2, T], BF16)
        prob = three(0, [2, 3, T])
        rden = four(2048, [T])
        att = sb("att", [P, T])

        ctx4 = sb("ctx4", [P, 4, CTX])
        kcol = sb("kcol", [P, CTX])
        kblk = sb("kblk", [P, H, CTX])
        vrow = sb("vrow", [P, D])
        vblk = sb("vblk", [P, 4, D])
        qT = four(2560, [T])
        x4b = four(3072, [NT, D])
        cmax = sb("cmax", [P, NT, H])
        csum = sb("csum", [P, NT, H])
        pc = three(0, [NT, H, CTX])
        pc_flat = three(0, [NT, H * CTX])
        pT = four(0, [4, T])

        glog = sb("glog", [P, NT, NE])
        gge = four(512, [NT, NE, NE])
        ggt = four(768, [NT, NE, NE])
        rank = sb("rank", [P, NT, NE])
        gtop = sb("gtop", [P, NT])
        gexp = sb("gexp", [P, NT, NE])
        gsum = sb("gsum", [P, NT])
        gates = sb("gates", [P, NT, NE])
        act_h = three(0, [2, FC, T])
        moe = four(0, [NT, D])

        bank = [ctx.enter_context(nc.psum_tensor(f"bank{i}", [P, 512], F32)) for i in range(8)]

        def tiles(t, n=P):
            return t.rearrange("p (a n) -> p a n", n=n)

        loaded = {n: sem("ld_" + n) for n in ("w_in", "conv_w", "chan", "w_bb", "w_cc", "w_bdt", "alog", "lev_a",
                                              "lev_b", "suf", "ident", "lmask", "w_out", "ctxT", "ones", "cconv",
                                              "cols", "wg", "wu", "wd", "identb")}
        loaded_late = sem("loaded_late")
        early = sem("early")
        pool_early = sem("pool_early")
        act_early = sem("act_early")
        pe_early = sem("pe_early")
        pool_passed = sem("pool_passed")
        dve_passed = sem("dve_passed")
        front_link = sem("front_link")
        back_link = sem("back_link")
        act_link = sem("act_link")
        xz_ready = sem("xz_ready")
        xin_ready = sem("xin_ready")
        conv_done = sem("conv_done")
        z_act = sem("z_act")
        xc_ready = sem("xc_ready")
        bc_ready = sem("bc_ready")
        btok_ready = sem("btok_ready")
        xcT_ready = sem("xcT_ready")
        b_ready = sem("b_ready")
        c_ready = sem("c_ready")
        ln_dt = sem("ln_dt")
        dt_ready = sem("dt_ready")
        dta_ready = sem("dta_ready")
        xdt_ready = sem("xdt_ready")
        gsuf_ready = sem("gsuf_ready")
        esuf_ready = sem("esuf_ready")
        bsuf_ready = sem("bsuf_ready")
        gdec_ready = sem("gdec_ready")
        dec_ready = sem("dec_ready")
        ct_ready = sem("ct_ready")
        bt_ready = sem("bt_ready")
        lev_ready = sem("lev_ready")
        masked = sem("masked")
        mix_ready = sem("mix_ready")
        hp_ready = sem("hp_ready")
        h_ready = sem("h_ready")
        y_ready = sem("y_ready")
        ya_ready = sem("ya_ready")
        yg_ready = sem("yg_ready")
        outA_ready = sem("outA_ready")
        var_ready = [sem(f"var{h}_ready") for h in range(2)]
        rstd_ready = [sem(f"rstd{h}_ready") for h in range(2)]
        x_ready = [sem(f"x{k}_ready") for k in range(1, 7)]
        xT_ps = [sem(f"x{k}T_ps") for k in range(1, 6)]
        xT_sb = [sem(f"x{k}T_sb") for k in range(1, 6)]
        comp_ps = sem("comp_ps")
        comp_sb = sem("comp_sb")
        back_ps = sem("back_ps")
        gsc_ready = sem("gsc_ready")
        gu_ps = sem("gu_ps")
        g_act = sem("g_act")
        hid_ready = sem("hid_ready")
        xq_ready = sem("xq_ready")
        hq_ready = sem("hq_ready")
        hq_magic = sem("hq_magic")
        hT_ps = sem("hT_ps")
        hT_sb = sem("hT_sb")
        down_ps = sem("down_ps")
        kq_ps = sem("kq_ps")
        v_ps = sem("v_ps")
        v_sb = sem("v_sb")
        part0 = sem("part0")
        rest0 = sem("rest0")
        part1 = sem("part1")
        part2 = sem("part2")
        stacked = sem("stacked")
        s_ps = sem("s_ps")
        s_max = sem("s_max")
        mp_ready = sem("mp_ready")
        mT_ps = sem("mT_ps")
        mT_sb = sem("mT_sb")
        st_ps = sem("st_ps")
        prob_ready = sem("prob_ready")
        pv_done = sem("pv_done")
        att_ready = sem("att_ready")
        proj_ps = sem("proj_ps")
        ctx_ready = sem("ctx_ready")
        ckv_ps = sem("ckv_ps")
        kcol_ready = sem("kcol_ready")
        kv_blk = sem("kv_blk")
        cq_ps = sem("cq_ps")
        cq_sb = sem("cq_sb")
        x4b_ready = sem("x4b_ready")
        cs_ps = sem("cs_ps")
        cs_kept = sem("cs_kept")
        cs_full = sem("cs_full")
        cs_max = sem("cs_max")
        cs_sub = sem("cs_sub")
        cp_ready = sem("cp_ready")
        cpT_ps = sem("cpT_ps")
        cpT_sb = sem("cpT_sb")
        co_ps = sem("co_ps")
        co_ready = sem("co_ready")
        cproj_ps = sem("cproj_ps")
        gate_ps = sem("gate_ps")
        glog_ready = sem("glog_ready")
        gsub_ready = sem("gsub_ready")
        gexp_ready = sem("gexp_ready")
        h_ps = sem("h_ps")
        h_act = sem("h_act")
        e_ps = sem("e_ps")
        e_added = sem("e_added")
        appended = sem("appended")
        minus_ones = sem("minus_ones")
        cp_scaled = sem("cp_scaled")
        x_loaded = sem("x_loaded")
        tok_loaded = sem("tok_loaded")
        e_loaded = [sem(f"e_loaded{n}") for n in range(3)]
        stored = sem("stored")

        block = ctx.enter_context(nc.Block())

        order = ["w_in", "conv_w", "chan", "w_bb", "w_cc", "w_bdt", "alog", "lev_a", "lev_b", "suf", "ident",
                 "lmask", "w_out", "ctxT", "ones", "cconv", "cols", "wg", "wu", "wd", "identb", "w_q", "w_k",
                 "w_v", "w_p", "tri_q", "tri_k", "c_q", "c_k", "c_v", "c_o", "rows", "hmask", "vmask", "mask",
                 "wgate", "before"]
        late = order[order.index("w_q"):]
        assert sorted(order + ["xT", "xtok", "w12"]) == sorted(a)

        def arrived(engine, *which):
            for n in which:
                engine.wait_ge(loaded[n], 16)

        def spread(engine, s, k):
            for g, which in enumerate(PRODUCTS):
                if which[s] == k:
                    for par in range(2):
                        base = 64 * par + HD * g
                        engine.dma_start(stack[s][base:base + HD, :, :],
                                         part[s][k][64 * par:64 * par + 64, :]).then_inc(stacked, 16)

        def halves(engine, attention, back, front):
            for n in range(len(FRONT_AT)):
                front(0, n)
            with engine.Fori(0, B - 1) as b:
                for unit in range(ATT_UNITS + SLOTS):
                    if unit < ATT_UNITS:
                        attention(b, unit)
                    else:
                        back(b, unit - ATT_UNITS)
                    for n, at in enumerate(FRONT_AT):
                        if at == unit:
                            front(b + 1, n)
            for unit in range(ATT_UNITS):
                attention(B - 1, unit)
            for slot in range(SLOTS):
                back(B - 1, slot)

        @block.sync
        def _(sp):
            sp.dma_start(xT[:], a["xT"][0]).then_inc(x_loaded, 16)
            sp.dma_start(xtok[:], a["xtok"][0]).then_inc(tok_loaded, 16)
            for n in order:
                sp.dma_start(names[n][:], a[n]).then_inc(loaded_late if n in late else loaded[n], 16)
            for e in range(3):
                sp.dma_start(experts[:, e], a["w12"][e]).then_inc(e_loaded[e], 16)

            def append_maxima(b, hg):
                sp.wait_ge(mT_sb, 2 * b + (hg + 1))
                for par in range(2):
                    base = 64 * par + PARTS * HD
                    sp.dma_start(stack[1][base:base + 3, hg * HG // 2:(hg + 1) * HG // 2, :],
                                 mT[12 * par:12 * par + 12, hg, :]).then_inc(appended, 16)

            def attention(b, unit):
                if unit == HG - 1:
                    append_maxima(b, 1)
                if unit == 0 and not isinstance(b, int):
                    sp.dma_start(xT[:], a["xT"][b + 1]).then_inc(x_loaded, 16)
                    sp.dma_start(xtok[:], a["xtok"][b + 1]).then_inc(tok_loaded, 16)

            def front(i, n):
                if n == 25:
                    sp.wait_ge(minus_ones, 1)
                    for k, ready in enumerate((part0, part1, part2)):
                        for s in range(2):
                            sp.wait_ge(ready, 2 * i + (s + 1))
                            spread(sp, s, k)
                if n == 26 + RAMP:
                    append_maxima(i, 0)

            def back(b, slot):
                if slot == SLOTS - 1:
                    sp.wait_ge(x_ready[5], NT * b + NT)
                    sp.dma_start(out[b], xs[5][:]).then_inc(stored, 16)

            halves(sp, attention, back, front)
            sp.wait_ge(stored, 16 * (B + 1))

        @block.gpsimd
        def _(pool):
            pool.memset(minus_half[:], -0.5).then_inc(pool_early, 1)
            pool.memset(xin[:, :, 0:TAPS - 1], 0.0).then_inc(pool_early, 1)
            pool.memset(vpad[:], 0.0).then_inc(pool_early, 1)
            pool.wait_ge(pool_early, 3)
            for h in range(H):
                lo = 64 + HD * (h % HG)
                pool.memset(vpad[:, :, h, lo:lo + HD], 1.0).then_inc(pool_early, 1)
            pool.memset(stack[0][:], -1.0).then_inc(minus_ones, 1)
            pool.memset(sparts[:], 0.0).then_inc(stored, 16)
            pool.wait_ge(stored, 16)

            def rstd_of(half, pass_, k):
                pool.wait_ge(var_ready[half], 3 * pass_ + k)
                pool.tensor_tensor(rstd[half][:], var[half][:], minus_half[:], ALU.pow).then_inc(rstd_ready[half], 1)

            def attention(b, unit):
                if unit == H + 1:
                    rstd_of(1, b, 1)

            def front(i, n):
                if n in (5, 6):
                    if n == 5:
                        pool.wait_ge(b_ready, i + 1)
                    for t in (2 * (n - 5), 2 * (n - 5) + 1):
                        pool.wait_ge(dec_ready, NT * i + (t + 1))
                        pool.tensor_tensor(bt[:, t], dec[:, t],
                                           bs[:, None, t * P:(t + 1) * P].broadcast_to([P, 4, P]),
                                           ALU.mult).then_inc(bt_ready, 1)
                if n in (9, 10, 11, 12):
                    t = n - 9
                    if t == 0:
                        pool.wait_ge(z_act, 2 * i + 2)
                    pool.wait_ge(ya_ready, NT * i + (t + 1))
                    pool.tensor_tensor(ya[:, :, t * P:(t + 1) * P], ya[:, :, t * P:(t + 1) * P],
                                       zs[:, :, t * P:(t + 1) * P], ALU.mult).then_inc(yg_ready, 1)
                if n == 13:
                    rstd_of(0, i, 1)
                if n == 16:
                    rstd_of(0, i, 2)
                if 18 <= n < 21:
                    for t in ((0, 1), (2,), (3,))[n - 18]:
                        pool.wait_ge(hq_magic, NT * i + (t + 1))
                        pool.sem_inc(pool_passed)
                        pool.tensor_scalar(hq[:, t], hid[:, t], MAGIC, None, ALU.subtract).then_inc(hq_ready, 1)
                if n == 23:
                    rstd_of(0, i, 3)
                if n == 25:
                    for s in range(2):
                        pool.wait_ge(rest0, 2 * i + (s + 1))
                        pool.sem_inc(pool_passed)
                        pool.tensor_copy(part[s][1][:], rest[s][:]).then_inc(part1, 1)
                        pool.wait_ge(part1, 2 * i + (s + 1))
                        pool.tensor_tensor(part[s][2][:], rest[s][:], part[s][1][:], ALU.subtract).then_inc(part2, 1)

            def back(b, slot):
                if slot == 1:
                    pool.wait_ge(x_ready[3], NT * b + NT)
                    pool.tensor_tensor(x4b[:], xs[3][:], rows[:, None, 1].broadcast_to([P, NT, D]),
                                       ALU.add).then_inc(x4b_ready, 1)
                if slot == 3:
                    for t in range(NT):
                        pool.wait_ge(cs_kept, NT * b + (t + 1))
                        pool.tensor_tensor(pc[:, t], pc[:, t], mfill[:, None, t].broadcast_to([P, H, CTX]),
                                           ALU.add).then_inc(cs_full, 1)
                if slot == 4:
                    for t in range(NT):
                        pool.wait_ge(cs_max, NT * b + (t + 1))
                        pool.tensor_tensor(pc[:, t], pc[:, t], cmax[:, t, :, None].broadcast_to([P, H, CTX]),
                                           ALU.subtract).then_inc(cs_sub, 1)
                if slot == 8:
                    rstd_of(1, b, 2)
                if slot == SLOTS - 1:
                    rstd_of(1, b, 3)

            halves(pool, attention, back, front)

        @block.scalar
        def _(act):
            def do(out_, in_, func, **kw):
                return nc.scalar.activation(out_, in_, func, **kw)

            act.wait_ge(pool_early, 2)

            def turn_maxima(b, hg):
                act.wait_ge(mT_ps, 2 * b + (hg + 1))
                do(mT[:, hg], bank[2][0:3 * HG].bitcast(BF16)[:, 0:T], ACT.Copy).then_inc(mT_sb, 1)

            def attention(b, h):
                if h < H:
                    if h >= 2:
                        act.wait_ge(pv_done, H * b + (h - 1))
                    for j, n in enumerate((512, 512, 256)):
                        act.wait_ge(st_ps, 3 * H * b + (3 * h + j + 1))
                        do(prob[:, h % 2, j, 0:n], bank[4 + (3 * h + j) % 2][:, 0:n], ACT.Exp,
                           scale=SCORE_SCALE).then_inc(prob_ready, 1)
                if h == HG - 1:
                    turn_maxima(b, 1)

            def front(i, n):
                if n == 2 and isinstance(i, int):
                    arrived(act, "alog")
                    do(neg_a[:], alog[:], ACT.Exp).then_inc(act_early, 1)
                if n == 14 and isinstance(i, int):
                    arrived(act, "cols", "ctxT")
                if n == 0:
                    for c in range(NC):
                        act.wait_ge(xz_ready, 4 * i + (c + 1))
                        do(xin[:, c, TAPS - 1:], bank[c][:], ACT.Copy).then_inc(xin_ready, 1)
                    for c in range(NC):
                        act.wait_ge(xz_ready, 4 * i + (NC + c + 1))
                        do(zs[:, c], bank[NC + c][:], ACT.Silu).then_inc(z_act, 1)
                if n == 1:
                    for c in range(NC):
                        act.wait_ge(conv_done, 2 * i + (c + 1))
                        do(xc[:, c], cacc[:, c], ACT.Silu).then_inc(xc_ready, 1)
                if n == 3:
                    act.wait_ge(bc_ready, 3 * i + 1)
                    do(bs[:], bank[0][:], ACT.Copy).then_inc(b_ready, 1)
                    act.wait_ge(btok_ready, i + 1)
                    do(dts[:, 0], btok[:, :, DS], ACT.Abs).then_inc(act_link, 1)
                    act.wait_ge(act_link, 3 * i + 1)
                    do(dts[:, 1], dts[:, 0], ACT.Exp, scale=-1.0).then_inc(act_link, 1)
                    act.wait_ge(act_link, 3 * i + 2)
                    do(dts[:, 2], dts[:, 1], ACT.Ln, bias=1.0).then_inc(ln_dt, 1)
                if n == 4:
                    act.wait_ge(dt_ready, i + 1)
                    for t in range(NT):
                        act.wait_ge(xcT_ready, 2 * i + (t // 2 + 1))
                        do(xdt[:, t], bank[3 if t < 2 else 0][:, (t % 2) * DI:(t % 2 + 1) * DI], ACT.Copy,
                           scale=dts[:, 3, t:t + 1]).then_inc(xdt_ready, 1)
                if n == 5:
                    for t in range(2):
                        act.wait_ge(gdec_ready, NT * i + (t + 1))
                        do(dec[:, t], tiles(bank[1 + t % 2]), ACT.Exp).then_inc(dec_ready, 1)
                    act.wait_ge(gsuf_ready, i + 1)
                    do(esuf[:], bank[3][:, 0:NT * DS].rearrange("p (n s) -> p n s", s=DS),
                       ACT.Exp).then_inc(esuf_ready, 1)
                if n == 6:
                    for t in range(2, NT):
                        act.wait_ge(gdec_ready, NT * i + (t + 1))
                        do(dec[:, t], tiles(bank[1 + t % 2]), ACT.Exp).then_inc(dec_ready, 1)
                if n == 14:
                    act.wait_ge(xT_ps[0], i + 1)
                    do(turned[:, 0:T], bank[0][:], ACT.Copy).then_inc(xT_sb[0], 1)
                    do(turned[:, T:], ctxT[:, i], ACT.Copy).then_inc(act_link, 1)
                if n == 15:
                    act.wait_ge(comp_ps, i + 1)
                    do(turned[:, KEEP:KEEP + COMP], bank[1][:, 0:COMP], ACT.Identity,
                       bias=cols[:, 0:1]).then_inc(comp_sb, 1)
                    do(ctx4[:], ctxT[:, i, None].broadcast_to([P, 4, CTX]), ACT.Copy).then_inc(ctx_ready, 1)
                if n == 16:
                    act.wait_ge(ckv_ps, 2 * i + 1)
                    do(kcol[:], bank[1][:, 0:CTX], ACT.Identity, bias=cols[:, 2:3]).then_inc(kcol_ready, 1)
                if n == 17:
                    act.wait_ge(xT_ps[1], i + 1)
                    do(xqT[:], bank[0][:].bitcast(BF16)[:, 0:T], ACT.Copy).then_inc(xT_sb[1], 1)
                if 18 <= n < 21:
                    if n == 18:
                        act.wait_ge(gsc_ready, i + 1)
                    for t in ((0, 1), (2,), (3,))[n - 18]:
                        act.wait_ge(gu_ps, NT * i + (t + 1))
                        if t >= 2:
                            act.wait_ge(hid_ready, NT * i + (t - 1))
                        do(gact[:, t % 2], bank[1 if t % 2 == 0 else 3][:], ACT.Silu,
                           scale=gsc[:, t, 0:1]).then_inc(g_act, 1)
                if n in (21, 22):
                    for t in (2 * (n - 21), 2 * (n - 21) + 1):
                        act.wait_ge(hT_ps, NT * i + (t + 1))
                        do(hqT[:, t], bank[1 + t % 2][:].bitcast(BF16)[:, 0:FF].rearrange("p (c n) -> p c n", n=P),
                           ACT.Copy).then_inc(hT_sb, 1)
                if n == 24:
                    act.wait_ge(xT_ps[2], i + 1)
                    do(turned[:, 0:T], bank[0][:], ACT.Copy).then_inc(xT_sb[2], 1)
                if n == 25:
                    for s in range(2):
                        act.wait_ge(kq_ps, 2 * i + (s + 1))
                        do(part[s][0][:], bank[1 + s][:], ACT.Copy).then_inc(part0, 1)
                if n == 26 + RAMP:
                    turn_maxima(i, 0)

            def back(b, slot):
                if slot == 1:
                    act.wait_ge(xT_ps[3], b + 1)
                    do(turned_b[:], bank[5][:], ACT.Copy).then_inc(xT_sb[3], 1)
                if slot == 2:
                    act.wait_ge(cq_ps, b + 1)
                    do(qT[:], bank[6][:], ACT.Identity, bias=cols[:, 1:2]).then_inc(cq_sb, 1)
                if slot == 4:
                    for t in range(NT):
                        act.wait_ge(cs_sub, NT * b + (t + 1))
                        do(pc[:, t], pc[:, t], ACT.Exp).then_inc(cp_ready, 1)
                if slot == 6:
                    for t in range(NT):
                        act.wait_ge(cpT_ps, NT * b + (t + 1))
                        do(pT[:, :, t * P:(t + 1) * P], tiles(bank[4 + t]), ACT.Copy).then_inc(cpT_sb, 1)
                if slot == 9:
                    act.wait_ge(xT_ps[4], b + 1)
                    do(turned_b[:], bank[7][:], ACT.Copy).then_inc(xT_sb[4], 1)
                if slot == 7:
                    act.wait_ge(co_ps, b + 1)
                    do(att[:], bank[4][:], ACT.Copy).then_inc(co_ready, 1)
                if slot == 10:
                    silu(b, 0, 0)
                    silu(b, 0, 1)
                if slot == E_SLOTS + 3:
                    act.wait_ge(gsub_ready, b + 1)
                    do(gexp[:], glog[:], ACT.Exp).then_inc(gexp_ready, 1)
                if slot >= E_SLOTS:
                    e, t = divmod(slot - E_SLOTS, FC)
                    if e == 0 and t == 0:
                        silu(b, 0, 2)
                        silu(b, 0, 3)
                    if e + 1 < SLICES:
                        silu(b, e + 1, t)
                    if t == 1 and e > 0:
                        next_slice(b, e - 1)
                if slot == SLOTS - 1:
                    next_slice(b, SLICES - 1)

            def next_slice(b, e):
                if not isinstance(b, int) or e + 3 < SLICES:
                    act.wait_ge(e_ps, SLICES * b + (e + 1))
                    act.dma_start(experts[:, e % 3], a["w12"][(e + 3) % SLICES]).then_inc(e_loaded[e % 3], 16)

            def silu(b, e, c):
                act.wait_ge(h_ps, SLICES * FC * b + (e * FC + c + 1))
                if e >= 2:
                    act.wait_ge(e_ps, SLICES * b + (e - 1))
                do(act_h[:, e % 2, c], bank[4 + c % 2][:], ACT.Silu).then_inc(h_act, 1)

            halves(act, attention, back, front)

        @block.vector
        def _(dve):
            V = nc.vector
            step = [0]

            def link(instruction):
                instruction.then_inc(early, 1)
                step[0] += 1
                dve.wait_ge(early, step[0])

            links = {"front": 0, "back": 0}

            def front_chain(i, instruction):
                instruction.then_inc(front_link, 1)
                links["front"] += 1
                dve.wait_ge(front_link, FRONT_LINKS * i + links["front"])

            def back_chain(b, instruction):
                instruction.then_inc(back_link, 1)
                links["back"] += 1
                dve.wait_ge(back_link, BACK_LINKS * b + links["back"])

            def norm(half, chain, pass_, k):
                rows_in = (res, res_b)[half]
                for t in range(NT):
                    last = V.bn_stats(stats[half][:, t], rows_in[:, t])
                chain(pass_, last)
                dve.sem_inc(dve_passed)
                for t in range(NT):
                    last = V.bn_aggr(mv[half][:, t], stats[half][:, t])
                chain(pass_, last)
                V.tensor_scalar(var[half][:], mv[half][:, :, 1], EPS, None, ALU.add).then_inc(var_ready[half], 1)
                dve.wait_ge(rstd_ready[half], 3 * pass_ + (k - 3 * half))
                if k == 4:
                    dve.wait_ge(stored, 16 * pass_ + 16)
                for t in range(NT):
                    V.tensor_scalar(xs[k - 1][:, t], rows_in[:, t], mv[half][:, t, 0:1], rstd[half][:, t:t + 1],
                                    ALU.subtract, ALU.mult).then_inc(x_ready[k - 1], 1)

            def row_maxima(b, h):
                hg, hl = divmod(h, HG)
                at = hl % 2 * (HG // 2) + hl // 2
                for j, (ta, tb) in enumerate(((3, None), (2, 0), (1, None))):
                    n = 3 * h + j
                    dve.wait_ge(s_ps, 3 * H * b + (n + 1))
                    src = bank[SCORE_BANKS[n % 3]]
                    last = V.tensor_reduce(smax[:, hg, ta, at:at + 1], src[:, 0:(ta + 1) * P], AX.X, ALU.max)
                    if tb is not None:
                        last = V.tensor_reduce(smax[:, hg, tb, at:at + 1], src[:, 384:512], AX.X, ALU.max)
                    last.then_inc(s_max, 1)

            def split_maxima(chain, b, hg):
                dve.wait_ge(s_max, 3 * H * b + 3 * HG * (hg + 1))
                whole, rest_of = (r[:, hg].rearrange("p t (r a) -> p t r a", r=2) for r in (smax, srest))
                chain(b, V.tensor_copy(sparts[:, hg, :, :, 0], whole))
                chain(b, V.tensor_tensor(rest_of, whole, sparts[:, hg, :, :, 0], ALU.subtract))
                chain(b, V.tensor_copy(sparts[:, hg, :, :, 1], rest_of))
                V.tensor_tensor(sparts[:, hg, :, :, 2], rest_of, sparts[:, hg, :, :, 1],
                                ALU.subtract).then_inc(mp_ready, 1)

            def attended(b, hg):
                dve.wait_ge(pv_done, H * b + HG * (hg + 1))
                if hg:
                    dve.wait_ge(att_ready, 4 * b + 2)
                for k in range(2):
                    half = slice(k * T // 2, (k + 1) * T // 2)
                    back_chain(b, V.reciprocal(rden[0:64, half], bank[6 + hg][64:128, half]))
                    V.tensor_tensor(att[64 * hg:64 * hg + 64, half], bank[6 + hg][0:64, half], rden[0:64, half],
                                    ALU.mult).then_inc(att_ready, 1)

            def attention(b, h):
                if h == 0:
                    links["back"] = 0
                if RAMP - HG <= h < HG:
                    row_maxima(b, HG + h)
                if h == HG - 1:
                    split_maxima(back_chain, b, 1)
                if h == HG + 1:
                    attended(b, 0)
                if h == H:
                    attended(b, 1)
                if h == H + 1:
                    dve.wait_ge(proj_ps, b + 1)
                    back_chain(b, V.scalar_tensor_tensor(out=res_b[:], in0=tiles(bank[4]), scalar=PROJ_SCALE,
                                                         in1=xs[2][:], op0=ALU.mult, op1=ALU.add))
                    norm(1, back_chain, b, 4)

            def decayed(i, t):
                dve.wait_ge(dec_ready, NT * i + (t + 1))
                front_chain(i, V.tensor_copy(last_dec[:, t:t + 1], dec[0:DS, t, 3, P - 1:P]))
                dve.wait_ge(bt_ready, NT * i + (t + 1))
                V.tensor_tensor(dec[:, t], dec[:, t], cs[:, None, t * P:(t + 1) * P].broadcast_to([P, 4, P]),
                                ALU.mult).then_inc(ct_ready, 1)

            def state(i, t):
                dve.wait_ge(hp_ready, 3 * i + (t + 1))
                if t == 0:
                    V.tensor_copy(hst[:, 0], bank[3][0:DS, 0:DI]).then_inc(h_ready, 1)
                else:
                    dve.wait_ge(h_ready, 3 * i + t)
                    V.scalar_tensor_tensor(out=hst[:, t], in0=hst[:, t - 1], scalar=last_dec[:, t:t + 1],
                                           in1=bank[3][0:DS, 0:DI], op0=ALU.mult, op1=ALU.add).then_inc(h_ready, 1)

            def mixing(i, t):
                dve.wait_ge(lev_ready, NT * i + (t + 1))
                if t > 0:
                    dve.wait_ge(mix_ready, NT * i + t)
                V.tensor_tensor(mm[:, 0:4], tiles(bank[0]), lmask[:, 0:4], ALU.mult)
                V.tensor_tensor(mm[:, 4:8], tiles(bank[1]), lmask[:, 4:8], ALU.mult).then_inc(masked, 1)
                dve.wait_ge(masked, NT * i + (t + 1))
                V.tensor_reduce(mix[:, t], mm[:].rearrange("p l n -> p n l"), AX.X, ALU.add).then_inc(mix_ready, 1)

            def skip(i, t):
                dve.wait_ge(y_ready, NT * i + (t + 1))
                for c in range(NC):
                    last = V.scalar_tensor_tensor(out=ya[:, c, t * P:(t + 1) * P], in0=xc[:, c, t * P:(t + 1) * P],
                                                  scalar=chan[:, c, 1:2], in1=bank[2][:, c * P:(c + 1) * P],
                                                  op0=ALU.mult, op1=ALU.add)
                last.then_inc(ya_ready, 1)

            def hidden(i, t):
                dve.wait_ge(g_act, NT * i + (t + 1))
                V.scalar_tensor_tensor(out=hid[:, t], in0=bank[2 if t % 2 == 0 else 0][:], scalar=gsc[:, t, 1:2],
                                       in1=gact[:, t % 2], op0=ALU.mult, op1=ALU.mult).then_inc(hid_ready, 1)
                dve.wait_ge(hid_ready, NT * i + (t + 1))
                front_chain(i, V.tensor_reduce(hmax[:, t:t + 1], hid[:, t], AX.X, ALU.max, apply_absolute_value=True))
                front_chain(i, V.tensor_scalar(hmax[:, t:t + 1], hmax[:, t:t + 1], 1e-5, None, ALU.max))
                front_chain(i, V.reciprocal(hinv[:, t:t + 1], hmax[:, t:t + 1]))
                front_chain(i, V.tensor_scalar(hinv[:, t:t + 1], hinv[:, t:t + 1], 127.0, None, ALU.mult))
                V.tensor_scalar(hid[:, t], hid[:, t], hinv[:, t:t + 1], MAGIC, ALU.mult, ALU.add).then_inc(hq_magic, 1)

            def quantise():
                arrived(dve, "wg", "wu", "wd")
                link(V.tensor_reduce(wabs[:, 0:1], wg[:], AX.X, ALU.add, apply_absolute_value=True))
                link(V.tensor_reduce(wabs[:, 1:2], wu[:], AX.X, ALU.add, apply_absolute_value=True))
                link(V.tensor_reduce(wabs[:, 2:3], wd[:].rearrange("p c n -> p (c n)"), AX.X, ALU.add,
                                     apply_absolute_value=True))
                dve.wait_ge(pe_early, 1)
                link(V.tensor_scalar(wscale[:], bank[7][:, 0:3], 1.0 / (D * FF), 1e-5, ALU.mult, ALU.max))
                link(V.reciprocal(winv[:], wscale[:]))
                for i, (w, q) in enumerate(((wg, wgq), (wu, wuq), (wd, wdq))):
                    if i == 2:
                        w, q = w[:].rearrange("p c n -> p (c n)"), q[:].rearrange("p c n -> p (c n)")
                    else:
                        w, q = w[:], q[:]
                    link(V.tensor_scalar(wtmp[:], w, winv[:, i:i + 1], MAGIC, ALU.mult, ALU.add))
                    link(V.tensor_scalar(wtmp[:], wtmp[:], MAGIC, 1.0, ALU.subtract, ALU.min))
                    link(V.tensor_scalar(q, wtmp[:], -1.0, None, ALU.max))

            def read_mask():
                dve.wait_ge(loaded_late, 16 * len(late))
                link(V.tensor_scalar(mkeep[:], mask[:], 0, CROSS_SCALE, ALU.not_equal, ALU.mult))
                link(V.tensor_scalar(mfill[:], mask[:], 0, -1e-9, ALU.is_equal, ALU.mult))

            def front(i, n):
                if isinstance(i, int):
                    if n == 0:
                        arrived(dve, "conv_w", "chan")
                    if n == 1:
                        quantise()
                    if n == 3:
                        dve.wait_ge(act_early, 1)
                        arrived(dve, "lmask")
                    if n == 16:
                        read_mask()
                    if n == 25:
                        dve.wait_ge(pool_early, 3 + H)
                if n == 0:
                    links["front"] = 0
                    for c in range(NC):
                        dve.wait_ge(xin_ready, 2 * i + (c + 1))
                        front_chain(i, V.tensor_scalar(cacc[:, c], xin[:, c, 0:T], conv_w[:, c, 0:1], chan[:, c, 0:1],
                                                       ALU.mult, ALU.add))
                        for k in range(1, TAPS):
                            tap = V.scalar_tensor_tensor(out=cacc[:, c], in0=xin[:, c, k:k + T],
                                                         scalar=conv_w[:, c, k:k + 1], in1=cacc[:, c],
                                                         op0=ALU.mult, op1=ALU.add)
                            if k < TAPS - 1:
                                front_chain(i, tap)
                            else:
                                tap.then_inc(conv_done, 1)
                if n == 2:
                    dve.wait_ge(bc_ready, 3 * i + 2)
                    V.tensor_copy(cs[:], bank[1][:]).then_inc(c_ready, 1)
                    dve.wait_ge(bc_ready, 3 * i + 3)
                    V.tensor_copy(btok[:], bank[2][:, 0:NT * (DS + 1)].rearrange(
                        "p (n c) -> p n c", c=DS + 1)).then_inc(btok_ready, 1)
                    dve.wait_ge(btok_ready, i + 1)
                    dve.wait_ge(c_ready, i + 1)
                if n == 3:
                    dve.wait_ge(ln_dt, i + 1)
                    V.scalar_tensor_tensor(out=dts[:, 3], in0=btok[:, :, DS], scalar=0.0, in1=dts[:, 2],
                                           op0=ALU.max, op1=ALU.add).then_inc(dt_ready, 1)
                    dve.wait_ge(dt_ready, i + 1)
                    for t in range(NT):
                        V.tensor_scalar(dta[:, t], neg_a[:], dts[:, 3, t:t + 1], -1.0, ALU.mult,
                                        ALU.mult).then_inc(dta_ready, 1)
                if n == 5:
                    decayed(i, 0)
                    decayed(i, 1)
                    dve.wait_ge(esuf_ready, i + 1)
                    V.tensor_tensor(bsuf[:], esuf[:], btok[:, :, 0:DS], ALU.mult).then_inc(bsuf_ready, 1)
                if n == 6:
                    decayed(i, 2)
                    decayed(i, 3)
                if n == 7:
                    mixing(i, 0)
                if n == 8:
                    state(i, 0)
                    mixing(i, 1)
                if n == 9:
                    skip(i, 0)
                    state(i, 1)
                if n == 10:
                    mixing(i, 2)
                    skip(i, 1)
                    state(i, 2)
                if n == 11:
                    mixing(i, 3)
                    skip(i, 2)
                if n == 12:
                    skip(i, 3)
                if n == 13:
                    dve.wait_ge(outA_ready, i + 1)
                    dve.wait_ge(tok_loaded, 16 * i + 16)
                    front_chain(i, V.tensor_tensor(res[:], tiles(bank[3]), xtok[:], ALU.add))
                    norm(0, front_chain, i, 1)
                if n == 16:
                    dve.wait_ge(back_ps, i + 1)
                    dve.wait_ge(x_ready[0], NT * i + NT)
                    front_chain(i, V.tensor_tensor(res[:], tiles(bank[2]), xs[0][:], ALU.add))
                    norm(0, front_chain, i, 2)
                    dve.wait_ge(x_ready[1], NT * i + NT)
                    front_chain(i, V.tensor_reduce(amax[:], xs[1][:], AX.X, ALU.max, apply_absolute_value=True))
                    front_chain(i, V.tensor_scalar(amax[:], amax[:], 1e-5, None, ALU.max))
                    front_chain(i, V.reciprocal(ainv[:], amax[:]))
                    front_chain(i, V.tensor_scalar(ainv[:], ainv[:], 127.0, None, ALU.mult))
                    for t in range(NT):
                        last = V.tensor_scalar(xqf[:, t], xs[1][:, t], ainv[:, t:t + 1], MAGIC, ALU.mult, ALU.add)
                    front_chain(i, last)
                    V.tensor_scalar(xq[:], xqf[:], MAGIC, None, ALU.subtract).then_inc(xq_ready, 1)
                    V.tensor_scalar(gsc[:, :, 0], amax[:], wscale[:, 0:1], 1.0 / 127.0, ALU.mult, ALU.mult)
                    V.tensor_scalar(gsc[:, :, 1], amax[:], wscale[:, 1:2], 1.0 / 127.0, ALU.mult,
                                    ALU.mult).then_inc(gsc_ready, 1)
                    dve.wait_ge(kcol_ready, i + 1)
                    V.tensor_tensor(kblk[:], kcol[:, None].broadcast_to([P, H, CTX]),
                                    hmask[:, :, None].broadcast_to([P, H, CTX]), ALU.mult).then_inc(kv_blk, 1)
                    dve.wait_ge(ckv_ps, 2 * i + 2)
                    front_chain(i, V.tensor_tensor(vrow[:], bank[3][:, 0:D], rows[:, 0], ALU.add))
                    V.tensor_tensor(vblk[:], vrow[:, None].broadcast_to([P, 4, D]), vmask[:], ALU.mult).then_inc(kv_blk, 1)
                    dve.wait_ge(gsc_ready, i + 1)
                if 18 <= n < 21:
                    for t in ((0, 1), (2,), (3,))[n - 18]:
                        hidden(i, t)
                if n == 23:
                    front_chain(i, V.tensor_scalar(dsc[:], hmax[:], wscale[:, 2:3], 1.0 / 127.0, ALU.mult, ALU.mult))
                    dve.wait_ge(down_ps, i + 1)
                    for t in range(NT):
                        last = V.scalar_tensor_tensor(out=res[:, t], in0=bank[3][:, t * P:(t + 1) * P],
                                                      scalar=dsc[:, t:t + 1], in1=xs[1][:, t],
                                                      op0=ALU.mult, op1=ALU.add)
                    front_chain(i, last)
                    norm(0, front_chain, i, 3)
                if n == 25:
                    for s in range(2):
                        dve.wait_ge(part0, 2 * i + (s + 1))
                        V.tensor_tensor(rest[s][:], bank[1 + s][:], part[s][0][:], ALU.subtract).then_inc(rest0, 1)
                    dve.wait_ge(v_ps, i + 1)
                    for hg in range(2):
                        for t in range(NT):
                            last = V.tensor_copy(diagonal(vpad, t, hg), bank[3][:, t * P + hg * 64:t * P + hg * 64 + 64]
                                                 .rearrange("p (h d) -> p h d", d=HD))
                    last.then_inc(v_sb, 1)
                if 26 <= n < 26 + RAMP:
                    row_maxima(i, n - 26)
                if n == 26 + RAMP:
                    split_maxima(front_chain, i, 0)
                    assert links["front"] == FRONT_LINKS, links["front"]

            def back(b, slot):
                if slot == 3:
                    for t in range(NT):
                        dve.wait_ge(cs_ps, NT * b + (t + 1))
                        V.tensor_tensor(pc[:, t], bank[4 + t][:].rearrange("p (h k) -> p h k", k=CTX),
                                        mkeep[:, None, t].broadcast_to([P, H, CTX]), ALU.mult).then_inc(cs_kept, 1)
                if slot == 4:
                    for t in range(NT):
                        dve.wait_ge(cs_full, NT * b + (t + 1))
                        V.tensor_reduce(cmax[:, t], pc[:, t], AX.X, ALU.max).then_inc(cs_max, 1)
                if slot == 5:
                    for t in range(NT):
                        dve.wait_ge(cp_ready, NT * b + (t + 1))
                        last = V.tensor_reduce(csum[:, t], pc[:, t], AX.X, ALU.add)
                    back_chain(b, last)
                    back_chain(b, V.reciprocal(csum[:], csum[:]))
                    for t in range(NT):
                        V.tensor_tensor(pc[:, t], pc[:, t], csum[:, t, :, None].broadcast_to([P, H, CTX]),
                                        ALU.mult).then_inc(cp_scaled, 1)
                if slot == 8:
                    dve.wait_ge(cproj_ps, b + 1)
                    dve.wait_ge(x4b_ready, b + 1)
                    back_chain(b, V.tensor_tensor(res_b[:], tiles(bank[6]), x4b[:], ALU.add))
                    norm(1, back_chain, b, 5)
                if slot == 10:
                    dve.wait_ge(gate_ps, b + 1)
                    V.tensor_copy(glog[:], bank[6][:, 0:NT * NE].rearrange("p (n e) -> p n e", e=NE)).then_inc(glog_ready, 1)
                if slot == E_SLOTS + 2:
                    dve.wait_ge(glog_ready, b + 1)
                    for t in range(NT):
                        other = glog[:, t, None].broadcast_to([P, NE, NE])
                        own = glog[:, t, :, None].broadcast_to([P, NE, NE])
                        V.tensor_tensor(gge[:, t], other, own, ALU.is_ge)
                        last = V.tensor_tensor(ggt[:, t], other, own, ALU.is_gt)
                    back_chain(b, last)
                    back_chain(b, V.tensor_tensor(gge[:].rearrange("p n a c -> p n (a c)"),
                                                  gge[:].rearrange("p n a c -> p n (a c)"),
                                                  before[:, None].broadcast_to([P, NT, NE * NE]), ALU.mult))
                    back_chain(b, V.tensor_tensor(ggt[:], ggt[:], gge[:], ALU.max))
                    back_chain(b, V.tensor_reduce(rank[:], ggt[:], AX.X, ALU.add))
                    back_chain(b, V.tensor_scalar(rank[:], rank[:], 2.0, None, ALU.is_lt))
                    back_chain(b, V.tensor_reduce(gtop[:], glog[:], AX.X, ALU.max))
                    V.tensor_tensor(glog[:], glog[:], gtop[:, :, None].broadcast_to([P, NT, NE]),
                                    ALU.subtract).then_inc(gsub_ready, 1)
                if slot == E_SLOTS + 4:
                    dve.wait_ge(gexp_ready, b + 1)
                    back_chain(b, V.tensor_tensor(gates[:], gexp[:], rank[:], ALU.mult))
                    back_chain(b, V.tensor_reduce(gsum[:], gates[:], AX.X, ALU.add))
                    back_chain(b, V.reciprocal(gsum[:], gsum[:]))
                    back_chain(b, V.tensor_tensor(gates[:], gates[:], gsum[:, :, None].broadcast_to([P, NT, NE]),
                                                  ALU.mult))
                e, sub = divmod(slot - E_SLOTS, FC)
                if slot >= E_SLOTS and sub == FC - 1:
                    dve.wait_ge(e_ps, SLICES * b + (e + 1))
                    src = bank[6 + e % 2]
                    if e == 0:
                        V.tensor_tensor(moe[:], tiles(src), xs[4][:], ALU.add).then_inc(e_added, 1)
                    else:
                        dve.wait_ge(e_added, SLICES * b + e)
                        dst = res_b if e == SLICES - 1 else moe
                        for t in range(NT):
                            last = V.scalar_tensor_tensor(out=dst[:, t], in0=src[:, t * P:(t + 1) * P],
                                                          scalar=gates[:, t, e - 1:e], in1=moe[:, t],
                                                          op0=ALU.mult, op1=ALU.add)
                        last.then_inc(e_added, 1)
                    if e == SLICES - 1:
                        dve.wait_ge(e_added, SLICES * b + SLICES)
                        norm(1, back_chain, b, 6)
                        assert links["back"] == BACK_LINKS, links["back"]

            halves(dve, attention, back, front)

        @block.tensor
        def _(pe):
            mmul = nc.tensor.matmul

            def turn(pass_, k, bk):
                for t in range(NT):
                    pe.wait_ge(x_ready[k - 1], NT * pass_ + (t + 1))
                    last = nc.tensor.transpose(bank[bk][:, t * P:(t + 1) * P], xs[k - 1][:, t], ident[:])
                last.then_inc(xT_ps[k - 1], 1)

            def at(h, extra=0):
                return slice(64 * (h % 2), 64 * (h % 2) + PARTS * HD + extra)

            def scores(b, h, j):
                n = 3 * h + j
                if n >= 3:
                    pe.wait_ge(s_max, 3 * H * b + (n - 2))
                for i, t in enumerate(((3,), (2, 0), (1,))[j]):
                    lo, w = 384 * i, (t + 1) * P
                    dst = bank[SCORE_BANKS[n % 3]]
                    mmul(dst[:, lo:lo + w], stack[1][at(h), h // 2, t * P:(t + 1) * P],
                         stack[0][at(h), h // 2, 0:w], start=True, stop=False)
                    last = mmul(dst[:, lo + w - P:lo + w], identb[:], tri_q[:], start=False, stop=True)
                last.then_inc(s_ps, 1)

            def maxima(b, hg):
                pe.wait_ge(mp_ready, 2 * b + (hg + 1))
                for t in range(NT):
                    last = nc.tensor.transpose(bank[2][0:3 * HG].bitcast(BF16)[:, t * P:(t + 1) * P],
                                               sparts[:, hg, t].rearrange("p r s a -> p (r s a)"), identb[:])
                last.then_inc(mT_ps, 1)

            def turned_scores(b, h, j):
                if h % HG == 0 and j == 0:
                    pe.wait_ge(appended, 16 * 2 * 2 * b + 16 * 2 * (h // HG + 1))
                n = 3 * h + j
                if n >= 2:
                    pe.wait_ge(prob_ready, 3 * H * b + (n - 1))
                dst = bank[4 + n % 2]
                for i, t in enumerate(KEY_TILES[j]):
                    lo, w = 384 * i, T - t * P
                    mmul(dst[:, lo:lo + w], stack[0][at(h, 3), h // 2, t * P:(t + 1) * P],
                         stack[1][at(h, 3), h // 2, t * P:T], start=True, stop=False)
                    last = mmul(dst[:, lo:lo + P], identb[:], tri_k[:], start=False, stop=True)
                last.then_inc(st_ps, 1)

            def weigh(b, h, j):
                dst = bank[6 + h // HG]
                pe.wait_ge(prob_ready, 3 * H * b + (3 * h + j + 1))
                for i, t in enumerate(KEY_TILES[j]):
                    last = mmul(dst[:, t * P:T], vpad[:, t, h], prob[:, h % 2, j, 384 * i:384 * i + T - t * P],
                                start=h % HG == 0 and t == 0, stop=h % HG == HG - 1 and t == 2)
                if j == 2:
                    last.then_inc(pv_done, 1)

            def attention(b, h):
                if h == 0:
                    pe.wait_ge(v_sb, b + 1)
                for j in range(3):
                    if h < H:
                        turned_scores(b, h, j)
                    if RAMP - HG <= h < HG:
                        scores(b, HG + h, j)
                    if 0 < h <= H:
                        weigh(b, h - 1, j)
                if h == HG - 1:
                    maxima(b, 1)
                if h == H + 1:
                    for t in range(NT):
                        pe.wait_ge(att_ready, 4 * b + (3 + t // 2))
                        last = mmul(bank[4][:, t * P:(t + 1) * P], att[:, t * P:(t + 1) * P], w_p[:],
                                    start=True, stop=True)
                    last.then_inc(proj_ps, 1)

            def decays(i, t):
                pe.wait_ge(dta_ready, NT * i + (t + 1))
                if t >= 2:
                    pe.wait_ge(dec_ready, NT * i + (t - 1))
                mmul(bank[1 + t % 2][0:64], dta[:, t, 0:DS], lev_a[:].rearrange("p l n -> p (l n)"),
                     start=True, stop=True)
                mmul(bank[1 + t % 2][64:128], dta[:, t, DS:2 * DS], lev_b[:].rearrange("p l n -> p (l n)"),
                     start=True, stop=True).then_inc(gdec_ready, 1)

            def levels(i, t):
                pe.wait_ge(ct_ready, NT * i + (t + 1))
                if t == 0:
                    pe.wait_ge(xdt_ready, NT * i + NT)
                    pe.wait_ge(dec_ready, NT * i + NT)
                else:
                    pe.wait_ge(masked, NT * i + t)
                for l in range(3):
                    mmul(bank[0][:, l * P:(l + 1) * P], bt[0:64, t, l], dec[0:64, t, l], start=True, stop=True)
                mmul(bank[0][:, 3 * P:4 * P], bs[0:64, t * P:(t + 1) * P], cs[0:64, t * P:(t + 1) * P],
                     start=True, stop=True)
                for l in range(4):
                    last = mmul(bank[1][:, l * P:(l + 1) * P], bt[64:128, t, l], dec[64:128, t, l],
                                start=True, stop=True)
                last.then_inc(lev_ready, 1)

            def carry(i, t):
                if t == 0:
                    pe.wait_ge(bsuf_ready, i + 1)
                else:
                    pe.wait_ge(h_ready, 3 * i + t)
                mmul(bank[3][0:DS, 0:DI], bsuf[:, t], xdt[:, t], start=True, stop=True).then_inc(hp_ready, 1)

            def outputs(i, t):
                pe.wait_ge(mix_ready, NT * i + (t + 1))
                if t > 0:
                    pe.wait_ge(h_ready, 3 * i + t)
                    pe.wait_ge(ya_ready, NT * i + t)
                for c in range(NC):
                    dst = bank[2][:, c * P:(c + 1) * P]
                    last = mmul(dst, xdt[:, t, c * P:(c + 1) * P], mix[:, t], start=True, stop=t == 0)
                    if t > 0:
                        last = mmul(dst, hst[:, t - 1, c * P:(c + 1) * P], dec[0:64, t, 3], start=False, stop=True)
                last.then_inc(y_ready, 1)

            def front(i, n):
                if isinstance(i, int):
                    if n == 0:
                        arrived(pe, "w_in")
                    if n == 1:
                        arrived(pe, "ones")
                        pe.wait_ge(early, 3)
                        mmul(bank[7][:, 0:3], ones[:], wabs[:], start=True, stop=True).then_inc(pe_early, 1)
                        arrived(pe, "w_bb", "w_cc", "w_bdt", "lev_a", "lev_b", "suf", "ident", "w_out", "cconv",
                                "identb")
                    if n == 15:
                        pe.wait_ge(loaded_late, 16 * len(late))
                    if n == 25:
                        pe.wait_ge(pool_early, 3 + H)
                if n == 0:
                    pe.wait_ge(x_loaded, 16 * i + 16)
                    for c in range(2 * NC):
                        if c == 2 and not isinstance(i, int):
                            pe.wait_ge(mT_sb, 2 * i)
                        mmul(bank[c][:], w_in[:, c * P:(c + 1) * P], xT[:], start=True, stop=True).then_inc(xz_ready, 1)
                if n == 2:
                    pe.wait_ge(xc_ready, 2 * i + 2)
                    for k, w in enumerate((w_bb, w_cc)):
                        for c in range(NC):
                            last = mmul(bank[k][:], w[:, c], xc[:, c], start=c == 0, stop=c == NC - 1)
                        last.then_inc(bc_ready, 1)
                    for t in range(NT):
                        for c in range(NC):
                            last = mmul(bank[2][:, t * (DS + 1):(t + 1) * (DS + 1)], xc[:, c, t * P:(t + 1) * P],
                                        w_bdt[:, c], start=c == 0, stop=c == NC - 1)
                    last.then_inc(bc_ready, 1)
                if n in (2, 3):
                    if n == 3:
                        pe.wait_ge(b_ready, i + 1)
                    for t in (2 * (n - 2), 2 * (n - 2) + 1):
                        for c in range(NC):
                            lo = (t % 2) * DI + c * P
                            last = nc.tensor.transpose(bank[3 if n == 2 else 0][:, lo:lo + P],
                                                       xc[:, c, t * P:(t + 1) * P], ident[:])
                    last.then_inc(xcT_ready, 1)
                if n == 4:
                    pe.wait_ge(c_ready, i + 1)
                    decays(i, 0)
                    pe.wait_ge(btok_ready, i + 1)
                    decays(i, 1)
                if n == 5:
                    pe.wait_ge(xdt_ready, NT * i + 2)
                    for t in range(NT):
                        pe.wait_ge(dta_ready, NT * i + (t + 1))
                        last = mmul(bank[3][:, t * DS:(t + 1) * DS], suf[:], dta[:, t, 0:DS], start=True, stop=True)
                    last.then_inc(gsuf_ready, 1)
                if n == 6:
                    decays(i, 2)
                    decays(i, 3)
                if n == 7:
                    levels(i, 0)
                if n == 8:
                    carry(i, 0)
                    levels(i, 1)
                if n == 9:
                    outputs(i, 0)
                    carry(i, 1)
                if n == 10:
                    levels(i, 2)
                    outputs(i, 1)
                    carry(i, 2)
                if n == 11:
                    levels(i, 3)
                    outputs(i, 2)
                if n == 12:
                    outputs(i, 3)
                if n == 13:
                    for t in range(NT):
                        pe.wait_ge(yg_ready, NT * i + (t + 1))
                        for c in range(NC):
                            last = mmul(bank[3][:, t * P:(t + 1) * P], ya[:, c, t * P:(t + 1) * P], w_out[:, c],
                                        start=c == 0, stop=c == NC - 1)
                    last.then_inc(outA_ready, 1)
                if n == 14:
                    turn(i, 1, 0)
                if n == 15:
                    pe.wait_ge(xT_sb[0], i + 1)
                    for k in range(TAPS):
                        last = mmul(bank[1][:, 0:COMP], cconv[:, k], turned[:, KEEP + k:KEEP + CTX:TAPS],
                                    start=k == 0, stop=k == TAPS - 1)
                    last.then_inc(comp_ps, 1)
                if n == 16:
                    pe.wait_ge(comp_sb, i + 1)
                    for t, lo in enumerate((COMP, P + COMP, KEEP + CTX, KEEP + P + CTX)):
                        last = nc.tensor.transpose(bank[2][:, t * P:(t + 1) * P], turned[:, lo:lo + P], ident[:])
                    last.then_inc(back_ps, 1)
                    pe.wait_ge(ctx_ready, i + 1)
                    mmul(bank[1][:, 0:CTX], c_k[:], ctx4[:, 0], start=True, stop=True).then_inc(ckv_ps, 1)
                    mmul(bank[3][:, 0:D], ctx4[:].rearrange("p a k -> p (a k)"), c_v[:],
                         start=True, stop=True).then_inc(ckv_ps, 1)
                if n == 17:
                    pe.wait_ge(xq_ready, i + 1)
                    for t in range(NT):
                        last = nc.tensor.transpose(bank[0][:].bitcast(BF16)[:, t * P:(t + 1) * P], xq[:, t], identb[:])
                    last.then_inc(xT_ps[1], 1)
                if 18 <= n < 21:
                    for t in ((0, 1), (2,), (3,))[n - 18]:
                        if t == 0:
                            pe.wait_ge(xT_sb[1], i + 1)
                            pe.wait_ge(kv_blk, 2 * i + 2)
                        if t >= 2:
                            pe.wait_ge(hid_ready, NT * i + (t - 1))
                        mmul(bank[1 if t % 2 == 0 else 3][:], xqT[:, t * P:(t + 1) * P], wgq[:], start=True, stop=True)
                        mmul(bank[2 if t % 2 == 0 else 0][:], xqT[:, t * P:(t + 1) * P], wuq[:],
                             start=True, stop=True).then_inc(gu_ps, 1)
                if n in (21, 22):
                    if n == 21:
                        pe.wait_ge(hid_ready, NT * i + 3)
                    for t in (2 * (n - 21), 2 * (n - 21) + 1):
                        pe.wait_ge(hq_ready, NT * i + (t + 1))
                        if t >= 2:
                            pe.wait_ge(hT_sb, NT * i + (t - 1))
                        for c in range(FC):
                            last = nc.tensor.transpose(bank[1 + t % 2][:].bitcast(BF16)[:, c * P:(c + 1) * P],
                                                       hq[:, t, c * P:(c + 1) * P], identb[:])
                        last.then_inc(hT_ps, 1)
                if n == 23:
                    for t in range(NT):
                        pe.wait_ge(hT_sb, NT * i + (t + 1))
                        for c in range(FC):
                            last = mmul(bank[3][:, t * P:(t + 1) * P], hqT[:, t, c], wdq[:, c],
                                        start=c == 0, stop=c == FC - 1)
                    last.then_inc(down_ps, 1)
                if n == 24:
                    turn(i, 3, 0)
                if n == 25:
                    pe.wait_ge(xT_sb[2], i + 1)
                    mmul(bank[1][:], w_k[:], turned[:, 0:T], start=True, stop=True).then_inc(kq_ps, 1)
                    mmul(bank[2][:], w_q[:], turned[:, 0:T], start=True, stop=True).then_inc(kq_ps, 1)
                    for t in range(NT):
                        last = mmul(bank[3][:, t * P:(t + 1) * P], turned[:, t * P:(t + 1) * P], w_v[:],
                                    start=True, stop=True)
                    last.then_inc(v_ps, 1)
                if 26 <= n < 26 + RAMP:
                    if n == 26:
                        pe.wait_ge(v_sb, i + 1)
                        pe.wait_ge(stacked, 16 * 2 * 2 * PARTS * i + 16 * 2 * 2 * PARTS)
                    for j in range(3):
                        scores(i, n - 26, j)
                if n == 26 + RAMP:
                    maxima(i, 0)

            def expand(b, e, c):
                n = e * FC + c
                if c == 0:
                    pe.wait_ge(e_loaded[e % 3], 16 * 3 * b + 16 * (e // 3 + 1))
                if n >= 2:
                    pe.wait_ge(h_act, SLICES * FC * b + (n - 1))
                mmul(bank[4 + n % 2][:], experts[:, e % 3, c * P:(c + 1) * P], turned_b[:],
                     start=True, stop=True).then_inc(h_ps, 1)

            def back(b, slot):
                if slot == 1:
                    turn(b, 4, 5)
                if slot == 2:
                    pe.wait_ge(xT_sb[3], b + 1)
                    mmul(bank[6][:], c_q[:], turned_b[:], start=True, stop=True).then_inc(cq_ps, 1)
                if slot == 3:
                    pe.wait_ge(cq_sb, b + 1)
                    pe.wait_ge(kv_blk, 2 * b + 2)
                    for t in range(NT):
                        mmul(bank[4 + t][:], qT[:, t * P:(t + 1) * P], kblk[:].rearrange("p h k -> p (h k)"),
                             start=True, stop=True).then_inc(cs_ps, 1)
                if slot == 6:
                    for t in range(NT):
                        pe.wait_ge(cp_scaled, NT * b + (t + 1))
                        for c in range(4):
                            last = nc.tensor.transpose(bank[4 + t][:, c * P:(c + 1) * P],
                                                       pc_flat[:, t, c * P:(c + 1) * P], ident[:])
                        last.then_inc(cpT_ps, 1)
                if slot == 7:
                    pe.wait_ge(cpT_sb, NT * b + NT)
                    for c in range(4):
                        last = mmul(bank[4][:], vblk[:, c], pT[:, c], start=c == 0, stop=c == 3)
                    last.then_inc(co_ps, 1)
                if slot == 8:
                    pe.wait_ge(co_ready, b + 1)
                    for t in range(NT):
                        last = mmul(bank[6][:, t * P:(t + 1) * P], att[:, t * P:(t + 1) * P], c_o[:],
                                    start=True, stop=True)
                    last.then_inc(cproj_ps, 1)
                if slot == 9:
                    turn(b, 5, 7)
                if slot == 10:
                    pe.wait_ge(xT_sb[4], b + 1)
                    for t in range(NT):
                        last = mmul(bank[6][:, t * NE:(t + 1) * NE], turned_b[:, t * P:(t + 1) * P], wgate[:],
                                    start=True, stop=True)
                    last.then_inc(gate_ps, 1)
                    expand(b, 0, 0)
                    expand(b, 0, 1)
                if slot >= E_SLOTS:
                    e, t = divmod(slot - E_SLOTS, FC)
                    if e == 0 and t == 0:
                        expand(b, 0, 2)
                        expand(b, 0, 3)
                        pe.wait_ge(glog_ready, b + 1)
                    if e + 1 < SLICES:
                        expand(b, e + 1, t)
                    if e >= 2 and t == 0:
                        pe.wait_ge(e_added, SLICES * b + (e - 1))
                    for c in range(FC):
                        if t == 0:
                            pe.wait_ge(h_act, SLICES * FC * b + (e * FC + c + 1))
                        last = mmul(bank[6 + e % 2][:, t * P:(t + 1) * P], act_h[:, e % 2, c, t * P:(t + 1) * P],
                                    experts[:, e % 3, FF + c * P:FF + (c + 1) * P], start=c == 0, stop=c == FC - 1)
                    if t == FC - 1:
                        last.then_inc(e_ps, 1)
                    if slot == SLOTS - 1:
                        pe.wait_ge(e_added, SLICES * b + SLICES)

            halves(pe, attention, back, front)


def diagonal(vpad, t, hg):
    flat = vpad[:, t, hg * HG:(hg + 1) * HG].rearrange("p h c -> p (h c)")
    return bass.AP(tensor=flat.tensor, offset=flat.offset, ap=[list(flat.ap[0]), [P + HD, HG], [1, HD]])


def shape_constants():
    bf = np.dtype("bfloat16")
    f = np.float32
    j = np.arange(P)[:, None]
    t = np.arange(P)[None, :]

    def between(half):
        mid = t // (2 * half) * (2 * half) + half
        return np.where(t >= mid, (j >= mid) & (j <= t), (j > t) & (j < mid)).astype(f)

    def pairs(half):
        same = j // (2 * half) == t // (2 * half)
        return (same & (j % (2 * half) < half) & (t % (2 * half) >= half)).astype(f)

    eye = np.eye(P, dtype=f)
    head = np.arange(P) // HD
    vm = (4 * np.arange(4)[None, :, None] + (np.arange(P) // CTX)[:, None, None] == head[None, None, :]).astype(f)
    e = np.arange(NE)
    return {
        "lev_a": np.stack([between(h) for h in LEVELS_A] + [(j <= t).astype(f)], 1),
        "lev_b": np.stack([between(h) for h in LEVELS_B], 1),
        "suf": (j > t).astype(f),
        "lmask": np.stack([pairs(h) for h in LEVELS_A] + [eye] + [pairs(h) for h in LEVELS_B], 1).astype(bf),
        "ident": eye, "identb": eye.astype(bf), "ones": np.ones((P, P), f),
        "tri_q": np.where(t > j, NEG, 0.0).astype(bf), "tri_k": np.where(j > t, NEG, 0.0).astype(bf),
        "hmask": (head[:, None] == np.arange(H)[None, :]).astype(f),
        "vmask": vm,
        "before": np.broadcast_to((e[None, :] < e[:, None]).astype(f).reshape(1, NE * NE), (P, NE * NE)),
    }


def kernel(**x):
    import concourse.bacc as bacc
    from concourse.bass_utils import run_bass_kernel_spmd

    x = {k: np.asarray(v) for k, v in x.items()}

    def chunks(w):
        return w.reshape(-1, P, w.shape[-1]).transpose(1, 0, 2)

    wx = x["L0_attn_W_x"].T
    wb, wc, wdt = wx[:, :DS], wx[:, DS:2 * DS], wx[:, 2 * DS:]
    perm = np.arange(D).reshape(NPAIR, 2, HD).transpose(1, 2, 0).reshape(-1)
    w1 = np.concatenate([x["L1_ffn_shared_w1"][None], x["L1_ffn_experts_w1"]])
    w2 = np.concatenate([x["L1_ffn_shared_w2"][None], x["L1_ffn_experts_w2"]])
    arrays = {
        "xT": x["x"].transpose(0, 2, 1),
        "xtok": x["x"].reshape(B, NT, P, D).transpose(0, 2, 1, 3),
        "ctxT": x["ctx_1024"].transpose(2, 0, 1),
        "w_in": x["L0_attn_W_in"].T,
        "conv_w": chunks(x["L0_attn_conv_w"].reshape(DI, TAPS)),
        "chan": chunks(np.stack([x["L0_attn_conv_b"], x["L0_attn_D"]], 1)),
        "w_bb": chunks(np.concatenate([wb, wb], 1)),
        "w_cc": chunks(np.concatenate([wc, wc], 1)),
        "w_bdt": chunks(np.concatenate([wb, wdt], 1)),
        "alog": np.broadcast_to(np.concatenate([x["L0_attn_A_log"]] * 2), (P, 2 * DS)),
        "w_out": chunks(x["L0_attn_W_out"].T),
        "cconv": x["L0_xattn_conv_w"].transpose(1, 0, 2),
        "cols": np.stack([x["L0_xattn_conv_b"], x["L1_xattn_bq"], x["L1_xattn_bk"]], 1),
        "wg": x["L0_ffn_w_gate"].T, "wu": x["L0_ffn_w_up"].T, "wd": chunks(x["L0_ffn_w_down"].T),
        "w_q": x["L1_attn_W_query"].T[:, perm], "w_k": x["L1_attn_W_key"].T[:, perm],
        "w_v": x["L1_attn_W_value"].T, "w_p": x["L1_attn_W_proj"].T,
        "c_q": x["L1_xattn_wq"].T, "c_k": x["L1_xattn_wk"].T, "c_v": x["L1_xattn_wv"].T, "c_o": x["L1_xattn_wo"].T,
        "rows": np.broadcast_to(np.stack([x["L1_xattn_bv"], x["L1_xattn_bo"]])[None], (P, 2, D)),
        "mask": x["mask_1x1xSxS2_if1"].reshape(NT, P, CTX).transpose(1, 0, 2),
        "w12": np.concatenate([w1.transpose(0, 2, 1), w2.transpose(0, 2, 1).reshape(SLICES, FC, P, D)
                               .transpose(0, 2, 1, 3).reshape(SLICES, P, FF)], 2),
        "wgate": x["L1_ffn_gate_w"].T,
    }
    arrays.update(shape_constants())
    nc = bacc.Bacc("TRN2", target_bir_lowering=False, num_devices=1)
    given, aps = {}, {}
    for name, v in arrays.items():
        v = np.ascontiguousarray(v)
        given["in_" + name] = v
        aps[name] = nc.dram_tensor("in_" + name, v.shape, mybir.dt.from_np(v.dtype), kind="ExternalInput").ap()
    out = nc.dram_tensor("out_0", (B, P, NT, D), F32, kind="ExternalOutput").ap()
    decoder(nc, aps, out)
    r = run_bass_kernel_spmd(nc, [given], core_ids=[0])
    return r.results[0]["out_0"].transpose(0, 2, 1, 3).reshape(B, T, D)
```
